# Optimizing a Trainium2 kernel written in Bass

```python
import numpy as np
import jax
import jax.numpy as jnp

def _softmax(x, axis=-1):
    return jax.nn.softmax(x, axis=axis)

def _gelu(x):
    return jax.nn.gelu(x, approximate=True)

def _silu(x):
    return jax.nn.silu(x)

def _sigmoid(x):
    return jax.nn.sigmoid(x)

def _layernorm(x, axis=-1, eps=1e-05):
    m = jnp.mean(x, axis=axis, keepdims=True)
    v = jnp.var(x, axis=axis, keepdims=True)
    return (x - m) / jnp.sqrt(v + eps)

def _scatter_add(tgt, idx, src, axis=0):
    return tgt.at[idx].add(src)

def _segment_sum(src, seg, n):
    return jax.ops.segment_sum(src, seg, n)
kernel_name = 'mk_adaln_d2_jaxref_r4_1f09a2'

def setup_inputs(seed: int=0):
    np.random.seed(seed)
    _w = jnp.asarray

    def _L0_attn_setup():
        import jax, jax.numpy as jnp
        import numpy as np
        H = 256
        F = 1024
        B, S = (4, 1024)
        EPS = 1e-05

        def _layernorm(x, scale, bias):
            mu = jnp.mean(x, axis=-1, keepdims=True)
            var = jnp.var(x, axis=-1, keepdims=True)
            return (x - mu) * jax.lax.rsqrt(var + EPS) * scale + bias
        key = jax.random.key(seed)
        ks = jax.random.split(key, 4)
        x = jax.random.normal(ks[0], (B, S, H), dtype=jnp.float32)
        W_ret = jax.random.normal(ks[1], (H, H), dtype=jnp.float32) * 0.02
        b_ret = jnp.zeros((H,), dtype=jnp.float32)
        ln1_scale = jnp.ones((H,), dtype=jnp.float32)
        ln1_bias = jnp.zeros((H,), dtype=jnp.float32)
        W1 = jax.random.normal(ks[2], (H, F), dtype=jnp.float32) * 0.02
        b1 = jnp.zeros((F,), dtype=jnp.float32)
        W2 = jax.random.normal(ks[3], (F, H), dtype=jnp.float32) * 0.02
        b2 = jnp.zeros((H,), dtype=jnp.float32)
        ln2_scale = jnp.ones((H,), dtype=jnp.float32)
        ln2_bias = jnp.zeros((H,), dtype=jnp.float32)
        return {'x': x, 'W_ret': W_ret, 'b_ret': b_ret, 'ln1_scale': ln1_scale, 'ln1_bias': ln1_bias, 'W1': W1, 'b1': b1, 'W2': W2, 'b2': b2, 'ln2_scale': ln2_scale, 'ln2_bias': ln2_bias}
    _L0_attn_in = _L0_attn_setup()

    def _L0_ffn_setup():
        import jax, jax.numpy as jnp
        import numpy as np
        NUM_EXPERTS = 8
        TOP_K = 2
        D_MODEL = 256
        EXPERT_CAP = 128
        B, S = (4, 512)
        key = jax.random.key(seed)
        ks = jax.random.split(key, 4)
        scale = 1.0 / np.sqrt(D_MODEL)
        x = jax.random.normal(ks[0], (B, S, D_MODEL), dtype=jnp.float32)
        gate_w = jax.random.normal(ks[1], (D_MODEL, NUM_EXPERTS), dtype=jnp.float32) * scale
        w1 = jax.random.normal(ks[2], (NUM_EXPERTS, D_MODEL, EXPERT_CAP), dtype=jnp.float32) * scale
        b1 = jnp.zeros((NUM_EXPERTS, EXPERT_CAP), dtype=jnp.float32)
        w2 = jax.random.normal(ks[3], (NUM_EXPERTS, EXPERT_CAP, D_MODEL), dtype=jnp.float32) * (1.0 / np.sqrt(EXPERT_CAP))
        b2 = jnp.zeros((NUM_EXPERTS, D_MODEL), dtype=jnp.float32)
        return {'x': x, 'gate_w': gate_w, 'w1': w1, 'b1': b1, 'w2': w2, 'b2': b2}
    _L0_ffn_in = _L0_ffn_setup()
    _L0_c = _w((lambda *s: np.random.randn(*s).astype(np.float32) * 0.05)(8, 256))
    _L0_wmod = _w((lambda *s: np.random.randn(*s).astype(np.float32) * 0.05)(256, 6 * 256) * 256 ** (-0.5))

    def _L1_attn_setup():
        import jax, jax.numpy as jnp
        import numpy as np
        D = 256
        H = 16
        HD = D // H
        ROPE_BASE = 10000.0
        EPS_RMS = 1e-08
        EPS_RENORM = 1e-08

        def rms_norm(x, scale):
            norm = jnp.mean(x * x, axis=-1, keepdims=True)
            return scale * (x * jax.lax.rsqrt(norm + EPS_RMS))

        def rope_tables(seq_len):
            inv_freq = 1.0 / ROPE_BASE ** (jnp.arange(0, HD, 2, dtype=jnp.float32) / HD)
            t = jnp.arange(seq_len, dtype=jnp.float32)
            freqs = t[:, None] * inv_freq[None, :]
            emb = jnp.concatenate([freqs, freqs], axis=-1)
            return (jnp.cos(emb), jnp.sin(emb))

        def apply_rotary(x, cos, sin):
            x1 = x[..., ::2]
            x2 = x[..., 1::2]
            x_rot = jnp.stack([-x2, x1], axis=-1).reshape(x.shape)
            return x * cos + x_rot * sin
        key = jax.random.key(seed)
        ks = jax.random.split(key, 11)
        B, L = (2, 512)
        s = 1.0 / np.sqrt(D)
        inp = {'x': jax.random.normal(ks[0], (B, L, D), dtype=jnp.float32), 'q_w': jax.random.uniform(ks[1], (D, D), jnp.float32, -s, s), 'q_b': jax.random.uniform(ks[2], (D,), jnp.float32, -s, s), 'k_w': jax.random.uniform(ks[3], (D, D), jnp.float32, -s, s), 'k_b': jax.random.uniform(ks[4], (D,), jnp.float32, -s, s), 'v_w': jax.random.uniform(ks[5], (D, D), jnp.float32, -s, s), 'v_b': jax.random.uniform(ks[6], (D,), jnp.float32, -s, s), 'o_w': jax.random.uniform(ks[7], (D, D), jnp.float32, -s, s), 'o_b': jax.random.uniform(ks[8], (D,), jnp.float32, -s, s), 'qn_scale': jnp.ones((D,), dtype=jnp.float32), 'kn_scale': jnp.ones((D,), dtype=jnp.float32)}
        return inp
    _L1_attn_in = _L1_attn_setup()

    def _L1_ffn_setup():
        import jax, jax.numpy as jnp
        import numpy as np
        H = 256
        I = 512
        E = 8
        TOP_K = 2
        NUM_SHARED = 1
        key = jax.random.key(seed)
        ks = jax.random.split(key, 9)
        s = 0.02
        x = jax.random.normal(ks[0], (2, 512, H), dtype=jnp.float32)
        sg_w = jax.random.normal(ks[1], (I, H), dtype=jnp.float32) * s
        su_w = jax.random.normal(ks[2], (I, H), dtype=jnp.float32) * s
        sd_w = jax.random.normal(ks[3], (H, I), dtype=jnp.float32) * s
        router_w = jax.random.normal(ks[4], (E, H), dtype=jnp.float32) * s
        routing_bias = jnp.zeros((E,), dtype=jnp.float32)
        wg = jax.random.normal(ks[5], (E, I, H), dtype=jnp.float32) * s
        wu = jax.random.normal(ks[6], (E, I, H), dtype=jnp.float32) * s
        wd = jax.random.normal(ks[7], (E, H, I), dtype=jnp.float32) * s
        return {'x': x, 'sg_w': sg_w, 'su_w': su_w, 'sd_w': sd_w, 'router_w': router_w, 'routing_bias': routing_bias, 'wg': wg, 'wu': wu, 'wd': wd}
    _L1_ffn_in = _L1_ffn_setup()
    _L1_c = _w((lambda *s: np.random.randn(*s).astype(np.float32) * 0.05)(8, 256))
    _L1_wmod = _w((lambda *s: np.random.randn(*s).astype(np.float32) * 0.05)(256, 6 * 256) * 256 ** (-0.5))
    _d = {'L0_attn_x': _L0_attn_in['x'], 'L0_attn_W_ret': _L0_attn_in['W_ret'], 'L0_attn_b_ret': _L0_attn_in['b_ret'], 'L0_attn_ln1_scale': _L0_attn_in['ln1_scale'], 'L0_attn_ln1_bias': _L0_attn_in['ln1_bias'], 'L0_attn_W1': _L0_attn_in['W1'], 'L0_attn_b1': _L0_attn_in['b1'], 'L0_attn_W2': _L0_attn_in['W2'], 'L0_attn_b2': _L0_attn_in['b2'], 'L0_attn_ln2_scale': _L0_attn_in['ln2_scale'], 'L0_attn_ln2_bias': _L0_attn_in['ln2_bias'], 'L0_ffn_gate_w': _L0_ffn_in['gate_w'], 'L0_ffn_w1': _L0_ffn_in['w1'], 'L0_ffn_b1': _L0_ffn_in['b1'], 'L0_ffn_w2': _L0_ffn_in['w2'], 'L0_ffn_b2': _L0_ffn_in['b2'], 'L0_c': _L0_c, 'L0_wmod': _L0_wmod, 'L1_attn_q_w': _L1_attn_in['q_w'], 'L1_attn_q_b': _L1_attn_in['q_b'], 'L1_attn_k_w': _L1_attn_in['k_w'], 'L1_attn_k_b': _L1_attn_in['k_b'], 'L1_attn_v_w': _L1_attn_in['v_w'], 'L1_attn_v_b': _L1_attn_in['v_b'], 'L1_attn_o_w': _L1_attn_in['o_w'], 'L1_attn_o_b': _L1_attn_in['o_b'], 'L1_attn_qn_scale': _L1_attn_in['qn_scale'], 'L1_attn_kn_scale': _L1_attn_in['kn_scale'], 'L1_ffn_sg_w': _L1_ffn_in['sg_w'], 'L1_ffn_su_w': _L1_ffn_in['su_w'], 'L1_ffn_sd_w': _L1_ffn_in['sd_w'], 'L1_ffn_router_w': _L1_ffn_in['router_w'], 'L1_ffn_routing_bias': _L1_ffn_in['routing_bias'], 'L1_ffn_wg': _L1_ffn_in['wg'], 'L1_ffn_wu': _L1_ffn_in['wu'], 'L1_ffn_wd': _L1_ffn_in['wd'], 'L1_c': _L1_c, 'L1_wmod': _L1_wmod}
    _x0 = _d['L0_attn_x']
    _d['L0_attn_x'] = jax.random.normal(jax.random.fold_in(jax.random.key(seed), 1), (8, 512, 256), dtype=_x0.dtype)
    del _x0
    return _d

def reference(L0_attn_x, L0_attn_W_ret, L0_attn_b_ret, L0_attn_ln1_scale, L0_attn_ln1_bias, L0_attn_W1, L0_attn_b1, L0_attn_W2, L0_attn_b2, L0_attn_ln2_scale, L0_attn_ln2_bias, L0_ffn_gate_w, L0_ffn_w1, L0_ffn_b1, L0_ffn_w2, L0_ffn_b2, L0_c, L0_wmod, L1_attn_q_w, L1_attn_q_b, L1_attn_k_w, L1_attn_k_b, L1_attn_v_w, L1_attn_v_b, L1_attn_o_w, L1_attn_o_b, L1_attn_qn_scale, L1_attn_kn_scale, L1_ffn_sg_w, L1_ffn_su_w, L1_ffn_sd_w, L1_ffn_router_w, L1_ffn_routing_bias, L1_ffn_wg, L1_ffn_wu, L1_ffn_wd, L1_c, L1_wmod):

    def _L0_attn_ref(x, W_ret, b_ret, ln1_scale, ln1_bias, W1, b1, W2, b2, ln2_scale, ln2_bias):
        import jax, jax.numpy as jnp
        import numpy as np
        H = 256
        F = 1024
        B, S = (4, 1024)
        EPS = 1e-05

        def _layernorm(x, scale, bias):
            mu = jnp.mean(x, axis=-1, keepdims=True)
            var = jnp.var(x, axis=-1, keepdims=True)
            return (x - mu) * jax.lax.rsqrt(var + EPS) * scale + bias
        sig = jax.nn.sigmoid(jnp.einsum('bsh,hk->bsk', x, W_ret) + b_ret)

        def ema_step(carry, s_t):
            xi = 0.5 * s_t + 0.5 * carry
            return (xi, xi)
        _, ret = jax.lax.scan(ema_step, jnp.zeros((x.shape[0], x.shape[2]), x.dtype), jnp.transpose(sig, (1, 0, 2)))
        retention_output = jnp.transpose(ret, (1, 0, 2))
        h = _layernorm(x + retention_output, ln1_scale, ln1_bias)
        ffn = jnp.einsum('bsf,fh->bsh', jax.nn.gelu(jnp.einsum('bsh,hf->bsf', h, W1) + b1), W2) + b2
        out = _layernorm(h + ffn, ln2_scale, ln2_bias)
        return out

    def _L0_ffn_ref(x, gate_w, w1, b1, w2, b2):
        import jax, jax.numpy as jnp
        import numpy as np
        NUM_EXPERTS = 8
        TOP_K = 2
        D_MODEL = 256
        EXPERT_CAP = 128
        B, S = (4, 512)
        Bx, Sx, D = x.shape
        xt = x.reshape(-1, D)
        gates = jax.nn.softmax(xt @ gate_w, axis=-1)
        topk_g, topk_i = jax.lax.top_k(gates, TOP_K)
        tok_w = topk_g.sum(axis=-1)
        sel = (topk_i[:, :, None] == jnp.arange(NUM_EXPERTS)[None, None, :]).any(axis=1)
        h = jax.nn.gelu(jnp.einsum('nd,edh->enh', xt, w1) + b1[:, None, :], approximate=False)
        y = jnp.einsum('enh,ehd->end', h, w2) + b2[:, None, :]
        out = jnp.einsum('end,ne,n->nd', y, sel.astype(x.dtype), tok_w)
        return out.reshape(Bx, Sx, D)

    def _L1_attn_ref(x, q_w, q_b, k_w, k_b, v_w, v_b, o_w, o_b, qn_scale, kn_scale):
        import jax, jax.numpy as jnp
        import numpy as np
        D = 256
        H = 16
        HD = D // H
        ROPE_BASE = 10000.0
        EPS_RMS = 1e-08
        EPS_RENORM = 1e-08

        def rms_norm(x, scale):
            norm = jnp.mean(x * x, axis=-1, keepdims=True)
            return scale * (x * jax.lax.rsqrt(norm + EPS_RMS))

        def rope_tables(seq_len):
            inv_freq = 1.0 / ROPE_BASE ** (jnp.arange(0, HD, 2, dtype=jnp.float32) / HD)
            t = jnp.arange(seq_len, dtype=jnp.float32)
            freqs = t[:, None] * inv_freq[None, :]
            emb = jnp.concatenate([freqs, freqs], axis=-1)
            return (jnp.cos(emb), jnp.sin(emb))

        def apply_rotary(x, cos, sin):
            x1 = x[..., ::2]
            x2 = x[..., 1::2]
            x_rot = jnp.stack([-x2, x1], axis=-1).reshape(x.shape)
            return x * cos + x_rot * sin
        B, L, _ = x.shape
        q = rms_norm(x, qn_scale) @ q_w.T + q_b
        k = rms_norm(x, kn_scale) @ k_w.T + k_b
        v = x @ v_w.T + v_b
        q = q.reshape(B, L, H, HD).transpose(0, 2, 1, 3)
        k = k.reshape(B, L, H, HD).transpose(0, 2, 1, 3)
        v = v.reshape(B, L, H, HD).transpose(0, 2, 1, 3)
        cos, sin = rope_tables(L)
        q = apply_rotary(q, cos, sin)
        k = apply_rotary(k, cos, sin)
        scale = 1.0 / np.sqrt(HD)
        scores = jnp.einsum('bhqd,bhkd->bhqk', q, k) * scale
        weights = jax.nn.sigmoid(scores)
        weights = weights / (jnp.sum(weights, axis=-1, keepdims=True) + EPS_RENORM)
        attn = jnp.einsum('bhqk,bhkd->bhqd', weights, v)
        attn = attn.transpose(0, 2, 1, 3).reshape(B, L, D)
        return attn @ o_w.T + o_b

    def _L1_ffn_ref(x, sg_w, su_w, sd_w, router_w, routing_bias, wg, wu, wd):
        import jax, jax.numpy as jnp
        import numpy as np
        H = 256
        I = 512
        E = 8
        TOP_K = 2
        NUM_SHARED = 1
        orig_shape = x.shape
        xt = x.reshape(-1, H)
        T = xt.shape[0]
        shared = jax.nn.silu(xt @ sg_w.T) * (xt @ su_w.T) @ sd_w.T
        shared = shared / NUM_SHARED
        logits = xt @ router_w.T + routing_bias
        probs = jax.nn.sigmoid(logits)
        topk_p, topk_idx = jax.lax.top_k(probs, TOP_K)
        topk_p = topk_p / jnp.sum(topk_p, axis=-1, keepdims=True)
        w = jnp.zeros((T, E), dtype=xt.dtype)
        w = w.at[jnp.arange(T)[:, None], topk_idx].add(topk_p)
        g = jnp.einsum('th,eih->tei', xt, wg)
        u = jnp.einsum('th,eih->tei', xt, wu)
        h = jax.nn.silu(g) * u
        y = jnp.einsum('tei,ehi->teh', h, wd)
        routed = jnp.einsum('te,teh->th', w, y)
        return (shared + routed).reshape(orig_shape)
    x = L0_attn_x
    mod = (_silu(L0_c) @ L0_wmod).reshape(L0_c.shape[0], 6, 1, -1)
    sa, ca, ga, sb, cb, gb = (mod[:, 0], mod[:, 1], mod[:, 2], mod[:, 3], mod[:, 4], mod[:, 5])
    ga = (2 * (ga >= 0) - 1) * jnp.maximum(jnp.abs(ga), 0.25)
    gb = (2 * (gb >= 0) - 1) * jnp.maximum(jnp.abs(gb), 0.25)
    h = _layernorm(x, axis=-1) * (1 + ca) + sa
    x = x + ga * _L0_attn_ref(h, L0_attn_W_ret, L0_attn_b_ret, L0_attn_ln1_scale, L0_attn_ln1_bias, L0_attn_W1, L0_attn_b1, L0_attn_W2, L0_attn_b2, L0_attn_ln2_scale, L0_attn_ln2_bias)
    h = _layernorm(x, axis=-1) * (1 + cb) + sb
    x = x + gb * _L0_ffn_ref(h, L0_ffn_gate_w, L0_ffn_w1, L0_ffn_b1, L0_ffn_w2, L0_ffn_b2)
    mod = (_silu(L1_c) @ L1_wmod).reshape(L1_c.shape[0], 6, 1, -1)
    sa, ca, ga, sb, cb, gb = (mod[:, 0], mod[:, 1], mod[:, 2], mod[:, 3], mod[:, 4], mod[:, 5])
    ga = (2 * (ga >= 0) - 1) * jnp.maximum(jnp.abs(ga), 0.25)
    gb = (2 * (gb >= 0) - 1) * jnp.maximum(jnp.abs(gb), 0.25)
    h = _layernorm(x, axis=-1) * (1 + ca) + sa
    x = x + ga * _L1_attn_ref(h, L1_attn_q_w, L1_attn_q_b, L1_attn_k_w, L1_attn_k_b, L1_attn_v_w, L1_attn_v_b, L1_attn_o_w, L1_attn_o_b, L1_attn_qn_scale, L1_attn_kn_scale)
    h = _layernorm(x, axis=-1) * (1 + cb) + sb
    x = x + gb * _L1_ffn_ref(h, L1_ffn_sg_w, L1_ffn_su_w, L1_ffn_sd_w, L1_ffn_router_w, L1_ffn_routing_bias, L1_ffn_wg, L1_ffn_wu, L1_ffn_wd)
    return x

_drawn_inputs = setup_inputs


def setup_inputs(seed=0):
    import zlib

    import numpy as np

    out = dict(_drawn_inputs(seed))
    spreads = {'L0_attn_b_ret': (0.0, 0.634),
     'L0_attn_ln1_scale': (1.0, 0.2),
     'L0_attn_ln1_bias': (0.0, 0.1),
     'L0_attn_b1': (0.0, 0.49),
     'L0_attn_b2': (0.0, 0.1),
     'L0_attn_ln2_scale': (1.0, 0.2),
     'L0_attn_ln2_bias': (0.0, 0.1),
     'L0_ffn_b1': (0.0, 0.603),
     'L0_ffn_b2': (0.0, 0.401),
     'L1_attn_qn_scale': (1.0, 0.6),
     'L1_attn_kn_scale': (1.0, 0.6),
     'L1_ffn_routing_bias': (0.0, 0.8)}
    factors = {'L0_attn_W_ret': 3.426,
     'L1_attn_q_w': 8.0,
     'L1_attn_q_b': 8.0,
     'L1_attn_k_w': 8.0,
     'L1_attn_k_b': 8.0,
     'L1_attn_v_w': 8.0,
     'L1_attn_v_b': 8.0,
     'L1_attn_o_w': 7.649,
     'L1_attn_o_b': 6.674,
     'L1_ffn_sg_w': 8.0,
     'L1_ffn_su_w': 8.0,
     'L1_ffn_sd_w': 8.0,
     'L1_ffn_router_w': 8.0,
     'L1_ffn_wg': 8.0,
     'L1_ffn_wu': 8.0,
     'L1_ffn_wd': 8.0,
     'L1_c': 4.183,
     'L1_wmod': 4.143}
    for name, (base, spread) in spreads.items():
        noise = np.random.default_rng([zlib.crc32(name.encode()), seed]).standard_normal(out[name].shape)
        drawn = base * np.exp(spread * noise) if base else spread * noise
        out[name] = jnp.asarray(drawn.astype(out[name].dtype))
    for name, factor in factors.items():
        out[name] = (out[name] * factor).astype(out[name].dtype)
    return out
```

```python
from contextlib import ExitStack

import concourse.bass as bass
from concourse import mybir

F32 = mybir.dt.float32
F32R = mybir.dt.float32r
BF16 = mybir.dt.bfloat16
F16 = mybir.dt.float16
ALU = mybir.AluOpType
ACT = mybir.ActivationFunctionType
AX = mybir.AxisListType.X

P = 128
B, S, D = 8, 512, 256
NT = S // P
KC = D // P
F0 = 1024
MC = F0 // P
E = 8
F1 = 512
IC = F1 // P
H, HD = 16, 16
SA, CA, SB, CB = range(4)
MOD_CHUNK = (0, 1, 3, 4)
GA, GB = 2, 5
LN_EPS, RMS_EPS, SUM_EPS = 1e-5, 1e-8, 1e-8
SIG_SCALE = 2.0 ** 14
HEAD, REST = 0, 1
PASSES = ((HEAD, HEAD), (HEAD, REST), (REST, HEAD))


def product(pe, out, terms):
    steps = [(left, right, i, j) for left, right in terms for i, j in PASSES]
    for n, (left, right, i, j) in enumerate(steps):
        last = pe.matmul(out, left(i), right(j), start=n == 0, stop=n == len(steps) - 1)
    return last


class Core:

    def __init__(self, nc, ctx):
        self.nc, self.ctx, self.part_sems = nc, ctx, None
        self.x = self.sb("x", [P, B, NT, D])
        self.hT = self.sb("hT", [P, KC, B, S])
        self.logits = self.sb("logits", [P, B, NT, E])
        self.coef = self.sb("coef", [P, B, NT, E])
        self.square_sum = self.sb("square_sum", [P, B, NT])
        self.mod = self.sb("mod", [P, 2, 4, KC, B])
        self.gate = self.sb("gate", [P, B, D])
        self.ident = self.sb("ident", [P, P])
        self.neg_half = self.sb("neg_half", [P, B * NT])
        self.gates_dram = nc.dram_tensor("gates", [2, 2, B, D], F32, kind="Internal").ap()
        self.x_first, self.x_rest = self.sem("x_first"), self.sem("x_rest")
        self.constants = self.sem("constants")
        self.start = self.sem("start")
        self.passed = self.sem("passed")

    def sb(self, name, shape, dt=F32, ctx=None):
        return (ctx or self.ctx).enter_context(self.nc.sbuf_tensor(name, shape, dt))

    def sem(self, name):
        sem = self.nc.alloc_semaphore(name)
        if self.part_sems is not None:
            self.part_sems.append(sem)
        return sem

    def begin_part(self):
        self.part_sems = []

    def end_part(self):
        self.nc.clear_and_free_semaphores(self.part_sems)
        self.nc.all_engine_barrier()
        self.part_sems = None

    def psum(self, name, n, ctx):
        return ctx.enter_context(self.nc.psum_tensor(name, [P, n, 512], F32))


def modulation_and_weights(c, a, w_ret, w_in, w_out):
    nc = c.nc
    with ExitStack() as ctx:
        cT = c.sb("cT", [P, 2, KC, B], ctx=ctx)
        silu_c = c.sb("silu_c", [P, 2, KC, B], ctx=ctx)
        wmod = c.sb("wmod", [P, 2, KC, 6 * D], ctx=ctx)
        raw_ret = c.sb("raw_ret", [P, KC, D], ctx=ctx)
        raw_in = c.sb("raw_in", [P, KC, F0], ctx=ctx)
        raw_out = c.sb("raw_out", [P, MC, D], ctx=ctx)
        gate_rows = c.sb("gate_rows", [B, 2, 2, D], ctx=ctx)
        gate_sign = c.sb("gate_sign", [B, 2, 2, D], ctx=ctx)
        ones = c.sb("ones_setup", [P, P], ctx=ctx)
        mod_ps = c.psum("mod_ps", 2, ctx)
        gate_ps = c.psum("gate_ps", 2, ctx)
        cond_loaded, wmod_loaded = c.sem("cond_loaded"), c.sem("wmod_loaded")
        raw_loaded = [c.sem(f"raw_loaded_{n}") for n in range(3)]
        silu_done, mod_done, gates_done = c.sem("silu_done"), c.sem("mod_done"), c.sem("gates_done")
        mod_scales, sign_done, size_done = c.sem("mod_scales"), c.sem("sign_done"), c.sem("size_done")
        rows_done, rows_stored = c.sem("rows_done"), c.sem("rows_stored")
        heads_split, rests_split, ones_set = c.sem("heads_split"), c.sem("rests_split"), c.sem("ones_set")
        weights = ((raw_ret, w_ret), (raw_in, w_in), (raw_out, w_out))

        with nc.Block() as block:
            @block.sync
            def _(sp):
                sp.dma_start(cT[:], a["cT"]).then_inc(cond_loaded, 16)
                for l in range(2):
                    sp.dma_start(wmod[:, l], a[f"L{l}_wmod"].rearrange("(k p) n -> p k n", p=P)).then_inc(wmod_loaded, 16)
                x_in = a["L0_attn_x"].rearrange("b (t p) d -> p b t d", p=P)
                sp.dma_start(c.x[:, 0], x_in[:, 0]).then_inc(c.x_first, 16)
                sp.dma_start(raw_ret[:], a["L0_attn_W_ret"].rearrange("(k p) n -> p k n", p=P)).then_inc(raw_loaded[0], 16)
                sp.dma_start(raw_in[:], a["L0_attn_W1"].rearrange("(k p) n -> p k n", p=P)).then_inc(raw_loaded[1], 16)
                sp.dma_start(raw_out[:], a["L0_attn_W2"].rearrange("(k p) n -> p k n", p=P)).then_inc(raw_loaded[2], 16)
                for b in range(1, B):
                    sp.dma_start(c.x[:, b], x_in[:, b]).then_inc(c.x_rest, 16)
                sp.wait_ge(rows_done, 1)
                sp.dma_start(c.gates_dram.rearrange("l k b d -> b l k d"), gate_rows[:]).then_inc(rows_stored, 16)
                sp.wait_ge(rows_stored, 16)
                sp.dma_start(c.gate[:], c.gates_dram[0, 0].unsqueeze(0).broadcast_to([P, B, D])).then_inc(c.constants, 16)

            @block.gpsimd
            def _(pool):
                pool.memset(c.neg_half[:], -0.5).then_inc(c.start, 1)
                pool.memset(ones[:], 1.0).then_inc(ones_set, 1)
                pool.wait_ge(ones_set, 1)
                pool.affine_select(out=c.ident[:], in_=ones[:], compare_op=ALU.is_equal, fill=0.0, base=0,
                                   pattern=[[-1, P]], channel_multiplier=1).then_inc(ones_set, 1)

            @block.scalar
            def _(act):
                act.wait_ge(cond_loaded, 16)
                nc.scalar.activation(silu_c[:], cT[:], ACT.Silu).then_inc(silu_done, 1)
                for n, (raw, split) in enumerate(weights):
                    act.wait_ge(raw_loaded[n], 16)
                    nc.scalar.activation(split[:, HEAD], raw[:], ACT.Copy).then_inc(heads_split, 1)

            @block.tensor
            def _(pe):
                pe.wait_ge(silu_done, 1)
                pe.wait_ge(wmod_loaded, 32)
                for l in range(2):
                    for kind, chunk in enumerate(MOD_CHUNK):
                        for m in range(KC):
                            at = (kind * KC + m) * B
                            col = chunk * D + m * P
                            for k in range(KC):
                                last = nc.tensor.matmul(mod_ps[:, l, at:at + B], wmod[:, l, k, col:col + P],
                                                        silu_c[:, l, k, :], start=k == 0, stop=k == KC - 1)
                    last.then_inc(mod_done, 1)
                    for n, chunk in enumerate((GA, GB)):
                        for k in range(KC):
                            last = nc.tensor.matmul(gate_ps[0:B, l, n * D:(n + 1) * D], silu_c[:, l, k, :],
                                                    wmod[:, l, k, chunk * D:(chunk + 1) * D],
                                                    start=k == 0, stop=k == KC - 1)
                    last.then_inc(gates_done, 1)

            @block.vector
            def _(dve):
                dve.wait_ge(gates_done, 2)
                g = gate_ps[0:B, :, :].rearrange("b l n -> b (l n)")
                sign = gate_sign[:].rearrange("b l k d -> b (l k d)")
                rows = gate_rows[:].rearrange("b l k d -> b (l k d)")
                nc.vector.tensor_scalar(sign, g, 0.0, 2.0, ALU.is_ge, ALU.mult).then_inc(sign_done, 1)
                dve.wait_ge(sign_done, 1)
                nc.vector.tensor_scalar(sign, sign, -1.0, None, ALU.add).then_inc(sign_done, 1)
                dve.wait_ge(sign_done, 2)
                nc.vector.tensor_tensor(rows, g, sign, ALU.mult).then_inc(size_done, 1)
                dve.wait_ge(size_done, 1)
                nc.vector.scalar_tensor_tensor(out=rows, in0=rows, scalar=0.25, in1=sign, op0=ALU.max,
                                               op1=ALU.mult).then_inc(rows_done, 1)
                dve.wait_ge(mod_done, 2)
                for l in range(2):
                    m = mod_ps[:, l, 0:4 * KC * B].rearrange("p (i k b) -> p i k b", i=4, k=KC)
                    for i in range(4):
                        nc.vector.tensor_scalar(c.mod[:, l, i], m[:, i], 1.0 if i in (CA, CB) else 0.0, None,
                                                ALU.add).then_inc(mod_scales, 1)
                for n, (raw, split) in enumerate(weights):
                    dve.wait_ge(heads_split, n + 1)
                    nc.vector.tensor_tensor(split[:, REST], raw[:], split[:, HEAD].bitcast(F32),
                                            ALU.subtract).then_inc(rests_split, 1)


class Norm:

    def __init__(self, c, ctx, name, eps):
        self.c, self.nc = c, c.nc
        self.stats = c.sb(name + "_stats", [P, NT, 6], ctx=ctx)
        self.moments = c.sb(name + "_moments", [P, NT, 2], ctx=ctx)
        self.eps = eps
        self.shifted = c.sb(name + "_shifted", [P, NT], ctx=ctx)
        self.inv_std = c.sb(name + "_inv_std", [P, NT], ctx=ctx)
        self.stats_done, self.moments_done = c.sem(name + "_stats_done"), c.sem(name + "_moments_done")
        self.shifted_done, self.inv_done = c.sem(name + "_shifted_done"), c.sem(name + "_inv_done")

    def gather(self, tile, tiles=range(NT)):
        for t in tiles:
            last = self.nc.vector.bn_stats(self.stats[:, t, :], tile(t))
        if t == NT - 1:
            last.then_inc(self.stats_done, 1)

    def aggregate(self, dve, b):
        dve.drain()
        for t in range(NT):
            last = self.nc.vector.bn_aggr(self.moments[:, t, :], self.stats[:, t, :])
        last.then_inc(self.moments_done, 1)

    def invert(self, pool, b):
        pool.wait_ge(self.moments_done, b + 1)
        self.nc.gpsimd.tensor_tensor(self.shifted[:], self.moments[:, :, 1], self.eps, ALU.add).then_inc(
            self.shifted_done, 1)
        pool.wait_ge(self.shifted_done, b + 1)
        self.nc.gpsimd.tensor_tensor(self.inv_std[:], self.shifted[:], self.c.neg_half[:, 0:NT], ALU.pow).then_inc(
            self.inv_done, 1)

    def apply(self, dve, b, to, tile, done):
        dve.wait_ge(self.inv_done, b + 1)
        for t in range(NT):
            last = self.nc.vector.tensor_scalar(to[:, t, :], tile(t), self.moments[:, t, 0:1], self.inv_std[:, t:t + 1],
                                                ALU.subtract, ALU.mult)
        last.then_inc(done, 1)


def transposes(pe, c, to, tiles):
    for k in range(KC):
        for t in range(NT):
            last = pe.transpose(to[:, k, t * P:(t + 1) * P], tiles[:, t, k * P:(k + 1) * P], c.ident[:])
    return last


def rows_of(ps, t):
    return ps[:, t // 2, (t % 2) * D:(t % 2 + 1) * D]


def retention_part(c, a, w_ret, w_in, w_out):
    nc = c.nc
    with ExitStack() as ctx:
        def sb(name, shape, dt=F32):
            return c.sb(name, shape, dt, ctx)

        b_ret, ln1_scale, ln1_bias = sb("b_ret", [P, KC]), sb("ln1_scale", [P, KC]), sb("ln1_bias", [P, KC])
        b_in, gate_w = sb("b_in", [P, MC]), sb("gate_w", [P, KC, E])
        ln2_scale, ln2_bias, b_out = sb("ln2_scale", [P, D]), sb("ln2_bias", [P, D]), sb("b_out", [1, D])
        half, eps = sb("half", [P, S]), sb("ln_eps", [P, NT])
        ident_wide = sb("ident_wide", [P, KC, D], F32R)
        ones, b_out_row = sb("ones", [P, P], F32R), sb("b_out_row", [P, D], F32R)
        norm_x, norm_1 = Norm(c, ctx, "norm_x", eps[:]), Norm(c, ctx, "norm_1", eps[:])
        norm_2, norm_next = Norm(c, ctx, "norm_2", eps[:]), Norm(c, ctx, "norm_next", eps[:])
        xn, xn_next = sb("xn", [P, NT, D]), sb("xn_next", [P, NT, D])
        h, h0_parts, h1_parts = sb("h", [P, KC, S]), sb("h0_parts", [P, 2, KC, S], F32R), sb("h1_parts", [P, 2, KC, S], F32R)
        sig, average = sb("sig", [P, KC, S]), sb("average", [P, KC, S])
        G_BUFS = 4
        g = sb("g", [P, G_BUFS, S])
        hidden = sb("hidden", [P, 2, MC, S], F32R)
        gate_scale, gate_bias, y_scaled = sb("gate_scale", [P, D]), sb("gate_bias", [P, D]), sb("y_scaled", [P, NT, D])
        tp_ps = c.psum("tp_ps", 2, ctx)
        ret_ps = c.psum("ret_ps", 2, ctx)
        in_ps = c.psum("in_ps", 2, ctx)
        out_ps = c.psum("out_ps", 2, ctx)

        tables_loaded, tables_set, b_out_head = c.sem("tables_loaded"), c.sem("tables_set"), c.sem("b_out_head")
        xn_done, xT_done, h0_done, h0_split = c.sem("xn_done"), c.sem("xT_done"), c.sem("h0_done"), c.sem("h0_split")
        ret_done, sig_done, average_done = c.sem("ret_done"), c.sem("sig_done"), c.sem("average_done")
        sum_done, sumT_done, n1_done, n1T_done = c.sem("sum_done"), c.sem("sumT_done"), c.sem("n1_done"), c.sem("n1T_done")
        h1_done, h1_split, in_done, g_done = c.sem("h1_done"), c.sem("h1_split"), c.sem("in_done"), c.sem("g_done")
        hidden_split, out_done = c.sem("hidden_split"), c.sem("out_done")
        gate_rows_done, x_biased, scaled_done, x_done = (c.sem("gate_rows_done"), c.sem("x_biased"),
                                                         c.sem("scaled_done"), c.sem("x_done"))
        next_done, nextT_done = c.sem("next_done"), c.sem("nextT_done")
        next_h_done, hT_kept = c.sem("next_h_done"), c.sem("hT_kept")
        logits_done, logits_kept, sums_read = c.sem("logits_done"), c.sem("logits_kept"), c.sem("sums_read")

        COLUMNS = (("b_ret", b_ret), ("ln1_scale", ln1_scale), ("ln1_bias", ln1_bias), ("b_in", b_in))
        ROWS = (("L0_attn_ln2_scale", ln2_scale), ("L0_attn_ln2_bias", ln2_bias))
        N_TABLES = 16 * (len(COLUMNS) + len(ROWS) + 2)
        SET_BY_POOL = 2

        with nc.Block() as block:
            @block.sync
            def _(sp):
                for name, to in COLUMNS:
                    sp.dma_start(to[:], a[name]).then_inc(tables_loaded, 16)
                for name, to in ROWS:
                    sp.dma_start(to[:], a[name].unsqueeze(0).broadcast_to([P, D])).then_inc(tables_loaded, 16)
                sp.dma_start(b_out[:], a["L0_attn_b2"].unsqueeze(0)).then_inc(tables_loaded, 16)
                sp.dma_start(gate_w[:], a["L0_ffn_gate_w"].rearrange("(k p) e -> p k e", p=P)).then_inc(tables_loaded, 16)

            @block.gpsimd
            def _(pool):
                pool.memset(eps[:], LN_EPS)
                pool.memset(half[:], 0.5)
                pool.memset(ident_wide[:].bitcast(F32), 0.0)
                pool.memset(ones[:].bitcast(F32), 1.0)
                pool.memset(b_out_row[:].bitcast(F32), 0.0).then_inc(tables_set, 1)
                pool.wait_ge(tables_set, 1)
                for k in range(KC):
                    last = nc.gpsimd.tensor_copy(ident_wide[:, k, k * P:(k + 1) * P], c.ident[:])
                last.then_inc(tables_set, 1)
                pool.wait_ge(tables_loaded, N_TABLES)

                def keep_hT(b):
                    pool.wait_ge(c.start, 1)
                    pool.wait_ge(next_h_done, b + 1)
                    nc.gpsimd.tensor_copy(c.hT[:, :, b, :], h[:]).then_inc(hT_kept, 1)

                def front(b):
                    pool.wait_ge(h0_done, b + 1)
                    nc.gpsimd.tensor_tensor(h0_parts[:, REST], h[:], h0_parts[:, HEAD].bitcast(F32),
                                            ALU.subtract).then_inc(h0_split, 1)
                    norm_1.invert(pool, b)

                def gate_tables(b):
                    pool.wait_ge(c.start, 1)
                    if not (isinstance(b, int) and b == 0):
                        pool.wait_ge(scaled_done, b)
                    nc.gpsimd.tensor_tensor(gate_scale[:], c.gate[:, b, :], ln2_scale[:], ALU.mult)
                    nc.gpsimd.tensor_tensor(gate_bias[:], c.gate[:, b, :], ln2_bias[:], ALU.mult).then_inc(
                        gate_rows_done, 1)
                    pool.wait_ge(c.start, 1)
                    pool.wait_ge(gate_rows_done, b + 1)
                    nc.gpsimd.tensor_tensor(c.x[:, b], c.x[:, b], gate_bias[:].unsqueeze(1).broadcast_to([P, NT, D]),
                                            ALU.add).then_inc(x_biased, 1)

                def tail(b):
                    norm_2.invert(pool, b)
                    norm_next.invert(pool, b)

                norm_x.invert(pool, 0)
                front(0)
                gate_tables(0)
                norm_x.invert(pool, 1)
                front(1)
                with pool.Fori(1, B - 1) as b:
                    tail(b - 1)
                    gate_tables(b)
                    norm_x.invert(pool, b + 1)
                    keep_hT(b - 1)
                    front(b + 1)
                tail(B - 2)
                gate_tables(B - 1)
                keep_hT(B - 2)
                tail(B - 1)
                keep_hT(B - 1)

            @block.tensor
            def _(pe):
                def retention(b):
                    pe.wait_ge(xn_done, b + 1)
                    transposes(nc.tensor, c, tp_ps, xn).then_inc(xT_done, 1)
                    pe.wait_ge(h0_split, b + 1)
                    for m in range(KC):
                        product(nc.tensor, ret_ps[:, m, :],
                                [(lambda i, k=k: w_ret[:, i, k, m * P:(m + 1) * P],
                                  lambda j, k=k: h0_parts[:, j, k, :]) for k in range(KC)]).then_inc(ret_done, 1)

                def sum_by_token(b):
                    pe.wait_ge(sum_done, b + 1)
                    for t in range(NT):
                        for k in range(KC):
                            last = nc.tensor.transpose(rows_of(ret_ps, t)[:, k * P:(k + 1) * P],
                                                       sig[:, k, t * P:(t + 1) * P], c.ident[:])
                    last.then_inc(sumT_done, 1)

                def h1_by_feature(b):
                    pe.wait_ge(n1_done, b + 1)
                    transposes(nc.tensor, c, tp_ps, xn).then_inc(n1T_done, 1)

                def widen(b, ms):
                    for m in ms:
                        if m == 0:
                            pe.wait_ge(h1_split, b + 1)
                        if m >= 2 or not (isinstance(b, int) and b == 0):
                            pe.wait_ge(g_done, MC * b + m - 1)
                        product(nc.tensor, in_ps[:, m % 2, :],
                                [(lambda i, k=k: w_in[:, i, k, m * P:(m + 1) * P],
                                  lambda j, k=k: h1_parts[:, j, k, :]) for k in range(KC)]).then_inc(in_done, 1)

                def narrow(b, ts):
                    if ts[0] == 0:
                        pe.wait_ge(hidden_split, MC * (b + 1))
                    for t in ts:
                        cols = slice(t * P, (t + 1) * P)
                        to = rows_of(out_ps, t)
                        nc.tensor.matmul(to, ones[:], b_out_row[:], start=True, stop=False)
                        for k in range(KC):
                            for part in (HEAD, REST):
                                nc.tensor.matmul(to, h1_parts[:, part, k, cols], ident_wide[:, k, :], start=False,
                                                 stop=False)
                        for m in range(MC):
                            for n, (i, j) in enumerate(PASSES):
                                last = nc.tensor.matmul(to, hidden[:, i, m, cols], w_out[:, j, m, :], start=False,
                                                        stop=m == MC - 1 and n == 2)
                    last.then_inc(out_done, 1)

                def next_by_feature(b):
                    pe.wait_ge(next_done, b + 1)
                    transposes(nc.tensor, c, tp_ps, xn_next).then_inc(nextT_done, 1)

                def route(b):
                    pe.wait_ge(next_h_done, b + 1)
                    for t in range(NT):
                        for k in range(KC):
                            last = nc.tensor.matmul(tp_ps[:, 0, t * E:(t + 1) * E], h[:, k, t * P:(t + 1) * P],
                                                    gate_w[:, k, :], start=k == 0, stop=k == KC - 1)
                    last.then_inc(logits_done, 1)

                def iteration(b, first=False, final=False):
                    widen(b, range(0, 7))
                    if not first:
                        next_by_feature(b - 1)
                    widen(b, range(7, MC))
                    if not first:
                        route(b - 1)
                    if not final:
                        if not first:
                            pe.wait_ge(logits_kept, b)
                        retention(b + 1)
                    narrow(b, (0, 1))
                    if not final:
                        sum_by_token(b + 1)
                    narrow(b, (2, 3))
                    if not final:
                        h1_by_feature(b + 1)

                pe.wait_ge(tables_loaded, N_TABLES)
                pe.wait_ge(tables_set, SET_BY_POOL)
                pe.wait_ge(b_out_head, 2)
                retention(0)
                sum_by_token(0)
                h1_by_feature(0)
                iteration(0, first=True)
                with pe.Fori(1, B - 1) as b:
                    iteration(b)
                iteration(B - 1, final=True)
                next_by_feature(B - 1)
                route(B - 1)

            @block.scalar
            def _(act):
                def front(b, first=False):
                    act.wait_ge(c.start, 1)
                    if not first:
                        act.wait_ge(hT_kept, b - 1)
                    act.wait_ge(xT_done, b + 1)
                    for to in (h, h0_parts[:, HEAD]):
                        for k in range(KC):
                            last = nc.scalar.activation(to[:, k, :], tp_ps[:, k, :], ACT.Identity,
                                                        bias=c.mod[:, 0, SA, k, bass.ds(b, 1)],
                                                        scale=c.mod[:, 0, CA, k, bass.ds(b, 1)])
                    last.then_inc(h0_done, 1)
                    for m in range(KC):
                        act.wait_ge(ret_done, KC * b + m + 1)
                        nc.scalar.activation(sig[:, m, :], ret_ps[:, m, :], ACT.Sigmoid,
                                             bias=b_ret[:, m:m + 1]).then_inc(sig_done, 1)
                    act.wait_ge(n1T_done, b + 1)
                    for to in (h, h1_parts[:, HEAD]):
                        for k in range(KC):
                            last = nc.scalar.activation(to[:, k, :], tp_ps[:, k, :], ACT.Identity,
                                                        bias=ln1_bias[:, k:k + 1], scale=ln1_scale[:, k:k + 1])
                    last.then_inc(h1_done, 1)

                def gelu(b, ms):
                    for m in ms:
                        act.wait_ge(in_done, MC * b + m + 1)
                        if not (isinstance(b, int) and b == 0 and m < G_BUFS):
                            act.wait_ge(hidden_split, MC * b + m + 1 - G_BUFS)
                        nc.scalar.activation(g[:, m % G_BUFS, :], in_ps[:, m % 2, :], ACT.Gelu_apprx_tanh,
                                             bias=b_in[:, m:m + 1])
                        nc.scalar.activation(hidden[:, HEAD, m, :], in_ps[:, m % 2, :], ACT.Gelu_apprx_tanh,
                                             bias=b_in[:, m:m + 1]).then_inc(g_done, 1)

                def tail(b):
                    act.wait_ge(c.start, 1)
                    act.wait_ge(nextT_done, b + 1)
                    for k in range(KC):
                        last = nc.scalar.activation(h[:, k, :], tp_ps[:, k, :], ACT.Identity,
                                                    bias=c.mod[:, 0, SB, k, bass.ds(b, 1)], scale=c.mod[:, 0, CB, k, bass.ds(b, 1)])
                    last.then_inc(next_h_done, 1)

                def iteration(b, first=False, final=False):
                    gelu(b, range(0, 7))
                    if not first:
                        tail(b - 1)
                    gelu(b, range(7, MC))
                    if not final:
                        front(b + 1, first)

                act.wait_ge(tables_loaded, N_TABLES)
                front(0, True)
                iteration(0, first=True)
                with act.Fori(1, B - 1) as b:
                    iteration(b)
                iteration(B - 1, final=True)
                tail(B - 1)

            @block.vector
            def _(dve):
                def x_tile(b):
                    return lambda t: c.x[:, b, t, :]

                def moments_x(b):
                    b = b if isinstance(b, int) else dve.snap(b)
                    norm_x.gather(x_tile(b))
                    norm_x.aggregate(dve, b)

                def normalise_x(b):
                    norm_x.apply(dve, b, xn, x_tile(b), xn_done)

                def average_and_sum(b):
                    for k in range(KC):
                        dve.wait_ge(sig_done, KC * b + k + 1)
                        nc.vector.tensor_tensor_scan(average[:, k, :], half[:], sig[:, k, :], 0.0, ALU.mult,
                                                     ALU.add).then_inc(average_done, 1)
                    dve.wait_ge(average_done, KC * (b + 1))
                    nc.vector.scalar_tensor_tensor(out=sig[:].rearrange("p k s -> p (k s)"),
                                                   in0=average[:].rearrange("p k s -> p (k s)"), scalar=0.5,
                                                   in1=h[:].rearrange("p k s -> p (k s)"),
                                                   op0=ALU.mult, op1=ALU.add).then_inc(sum_done, 1)

                def normalise_1(b):
                    dve.wait_ge(sumT_done, b + 1)
                    norm_1.gather(lambda t: rows_of(ret_ps, t))
                    norm_1.aggregate(dve, b)
                    norm_1.apply(dve, b, xn, lambda t: rows_of(ret_ps, t), n1_done)

                def rest_h1(b):
                    dve.wait_ge(h1_done, b + 1)
                    nc.vector.tensor_tensor(h1_parts[:, REST], h[:], h1_parts[:, HEAD].bitcast(F32),
                                            ALU.subtract).then_inc(h1_split, 1)

                def rest_hidden(b, ms):
                    for m in ms:
                        dve.wait_ge(g_done, MC * b + m + 1)
                        nc.vector.tensor_tensor(hidden[:, REST, m, :], g[:, m % G_BUFS, :],
                                                hidden[:, HEAD, m, :].bitcast(F32), ALU.subtract).then_inc(hidden_split, 1)

                def moments_2(b, ts):
                    dve.wait_ge(out_done, 2 * b + 1 + ts[0] // 2)
                    norm_2.gather(lambda t: rows_of(out_ps, t), ts)
                    if ts[-1] == NT - 1:
                        norm_2.aggregate(dve, b)

                def update_x(b):
                    dve.wait_ge(norm_2.moments_done, b + 1)
                    dve.wait_ge(gate_rows_done, b + 1)
                    for t in range(NT):
                        last = nc.vector.scalar_tensor_tensor(out=y_scaled[:, t, :], in0=rows_of(out_ps, t),
                                                              scalar=norm_2.moments[:, t, 0:1], in1=gate_scale[:],
                                                              op0=ALU.subtract, op1=ALU.mult)
                    last.then_inc(scaled_done, 1)
                    dve.wait_ge(c.start, 1)
                    dve.wait_ge(norm_2.inv_done, b + 1)
                    dve.wait_ge(x_biased, b + 1)
                    dve.wait_ge(scaled_done, b + 1)
                    for t in range(NT):
                        last = nc.vector.scalar_tensor_tensor(out=c.x[:, b, t, :], in0=y_scaled[:, t, :],
                                                              scalar=norm_2.inv_std[:, t:t + 1], in1=c.x[:, b, t, :],
                                                              op0=ALU.mult, op1=ALU.add)
                    last.then_inc(x_done, 1)
                    dve.wait_ge(c.start, 1)
                    dve.wait_ge(x_done, b + 1)
                    norm_next.gather(x_tile(b))
                    norm_next.aggregate(dve, b)

                def normalise_next(b):
                    norm_next.apply(dve, b, xn_next, x_tile(b), next_done)

                def keep_logits(b):
                    dve.wait_ge(c.start, 1)
                    dve.wait_ge(logits_done, b + 1)
                    nc.vector.tensor_copy(c.logits[:, b], tp_ps[:, 0, 0:NT * E].rearrange("p (t e) -> p t e", t=NT)
                                          ).then_inc(logits_kept, 1)

                def iteration(b, first=False, final=False):
                    if not first:
                        moments_2(b - 1, (2, 3))
                    rest_hidden(b, (0, 1))
                    if not first:
                        update_x(b - 1)
                    rest_hidden(b, (2, 3))
                    if not first:
                        normalise_next(b - 1)
                    rest_hidden(b, (4, 5))
                    if not final:
                        moments_x(b + 1)
                    rest_hidden(b, (6,))
                    if not final:
                        normalise_x(b + 1)
                    rest_hidden(b, (7,))
                    if not first:
                        keep_logits(b - 1)
                    if not final:
                        average_and_sum(b + 1)
                    moments_2(b, (0, 1))
                    if not final:
                        normalise_1(b + 1)
                        rest_h1(b + 1)

                dve.wait_ge(tables_loaded, N_TABLES)
                dve.wait_ge(tables_set, SET_BY_POOL)
                nc.vector.tensor_copy(b_out_row[0:1, :], b_out[:]).then_inc(b_out_head, 1)
                dve.wait_ge(b_out_head, 1)
                nc.vector.tensor_tensor(b_out_row[32:33, :], b_out[:], b_out_row[0:1, :].bitcast(F32),
                                        ALU.subtract).then_inc(b_out_head, 1)
                dve.wait_ge(c.x_first, 16)
                moments_x(0)
                normalise_x(0)
                average_and_sum(0)
                normalise_1(0)
                rest_h1(0)
                dve.wait_ge(c.x_rest, 16 * (B - 1))
                iteration(0, first=True)
                with dve.Fori(1, B - 1) as b:
                    iteration(b)
                iteration(B - 1, final=True)
                moments_2(B - 1, (2, 3))
                update_x(B - 1)
                normalise_next(B - 1)
                keep_logits(B - 1)


def split_weights(c, name, weights):
    nc = c.nc
    with ExitStack() as ctx:
        raw = [c.sb(f"{name}_raw_{n}", [P, split.shape[2], split.shape[3]], ctx=ctx) for n, (_, split, _) in enumerate(weights)]
        scales = [c.sb(f"{name}_scale_{n}", [P, split.shape[2]], ctx=ctx) for n, (_, split, _) in enumerate(weights)]
        loaded = [c.sem(f"{name}_loaded_{n}") for n in range(len(weights))]
        scaled, heads_done, rests_done = c.sem(name + "_scaled"), c.sem(name + "_heads"), c.sem(name + "_rests")
        with nc.Block() as block:
            @block.sync
            def _(sp):
                for n, (view, split, scale) in enumerate(weights):
                    if scale is not None:
                        sp.dma_start(scales[n][:], scale).then_inc(loaded[n], 16)
                    sp.dma_start(raw[n][:], view).then_inc(loaded[n], 16)

            @block.vector
            def _(dve):
                for n, (view, split, scale) in enumerate(weights):
                    dve.wait_ge(loaded[n], 16 if scale is None else 32)
                    for k in range(split.shape[2]):
                        last = nc.vector.tensor_scalar(raw[n][:, k, :], raw[n][:, k, :],
                                                       1.0 if scale is None else scales[n][:, k:k + 1], None, ALU.mult)
                    last.then_inc(scaled, 1)
                for n, (view, split, scale) in enumerate(weights):
                    dve.wait_ge(heads_done, n + 1)
                    nc.vector.tensor_tensor(split[:, REST], raw[n][:], split[:, HEAD].bitcast(F32),
                                            ALU.subtract).then_inc(rests_done, 1)

            @block.scalar
            def _(act):
                for n, (view, split, scale) in enumerate(weights):
                    act.wait_ge(scaled, n + 1)
                    nc.scalar.activation(split[:, HEAD], raw[n][:], ACT.Copy).then_inc(heads_done, 1)


def choose(nc, dve, value, better, count, chosen, weight_sum, coef):
    for f in range(E):
        for lo, hi, op in ((0, f, ALU.is_gt), (f + 1, E, ALU.is_ge)):
            if lo < hi:
                nc.vector.tensor_tensor(better[:, :, lo:hi, f], value[:, :, f:f + 1].broadcast_to([P, B * NT, hi - lo]),
                                        value[:, :, lo:hi], op)
    dve.drain()
    nc.vector.tensor_reduce(count, better[:, :, :, :], AX, ALU.add)
    dve.drain()
    nc.vector.tensor_scalar(coef, count, 2.0, None, ALU.is_lt)
    dve.drain()
    nc.vector.tensor_tensor(chosen, coef, value, ALU.mult)
    dve.drain()
    nc.vector.tensor_reduce(weight_sum, chosen, AX, ALU.add)
    dve.drain()


def softmax_router(c):
    nc = c.nc
    N = B * NT
    with ExitStack() as ctx:
        peak, total, inv_total = (c.sb("gate_" + n, [P, N], ctx=ctx) for n in ("peak", "total", "inv_total"))
        shifted, power, gates, count, chosen = (c.sb("gate_" + n, [P, N, E], ctx=ctx)
                                                for n in ("shifted", "power", "values", "count", "chosen"))
        weight_sum, better = c.sb("gate_weight_sum", [P, N], ctx=ctx), c.sb("gate_better", [P, N, E, E], ctx=ctx)
        shifted_done, power_done = c.sem("gate_shifted_done"), c.sem("gate_power_done")
        logits, coef = c.logits[:].rearrange("p b t e -> p (b t) e"), c.coef[:].rearrange("p b t e -> p (b t) e")

        def spread(v):
            return v[:].unsqueeze(2).broadcast_to([P, N, E])

        with nc.Block() as block:
            @block.sync
            def _(sp):
                sp.dma_start(c.gate[:], c.gates_dram[0, 1].unsqueeze(0).broadcast_to([P, B, D])).then_inc(c.constants, 16)

            @block.scalar
            def _(act):
                act.wait_ge(shifted_done, 1)
                nc.scalar.activation(power[:], shifted[:], ACT.Exp).then_inc(power_done, 1)

            @block.vector
            def _(dve):
                nc.vector.memset(better[:], 0.0)
                nc.vector.tensor_reduce(peak[:], logits, AX, ALU.max)
                dve.drain()
                nc.vector.tensor_tensor(shifted[:], logits, spread(peak), ALU.subtract).then_inc(shifted_done, 1)
                dve.wait_ge(power_done, 1)
                nc.vector.tensor_reduce(total[:], power[:], AX, ALU.add)
                dve.drain()
                nc.vector.reciprocal(inv_total[:], total[:])
                dve.drain()
                nc.vector.tensor_tensor(gates[:], power[:], spread(inv_total), ALU.mult)
                dve.drain()
                choose(nc, dve, gates[:], better, count[:], chosen[:], weight_sum[:], coef)
                nc.vector.tensor_tensor(coef, coef, spread(weight_sum), ALU.mult)


def gelu_experts_part(c, a, w_up, w_down):
    nc = c.nc
    with ExitStack() as ctx:
        def sb(name, shape, dt=F32):
            return c.sb("e0_" + name, shape, dt, ctx)

        b_up, b_down, ones, eps = sb("b_up", [P, E]), sb("b_down", [E, D]), sb("ones", [P, 1]), sb("eps", [P, NT])
        norm = Norm(c, ctx, "e0_norm", eps[:])
        h_parts, coef = sb("h_parts", [P, 2, KC, S], F32R), sb("coef", [P, NT, E])
        coefT, acc, y = sb("coefT", [E, S]), sb("acc", [P, NT, D]), sb("y", [P, NT, D])
        g, hidden = sb("g", [P, 2, S]), sb("hidden", [P, 2, 2, S], F32R)
        xn, squares = sb("xn", [P, NT, D]), sb("squares", [P, KC, S])
        tp_ps = c.psum("e0_tp_ps", 2, ctx)
        up_ps = c.psum("e0_up_ps", 2, ctx)
        down_ps = [c.psum(f"e0_down_ps_{n}", 2, ctx) for n in range(2)]
        (tables_loaded, tables_set, head_done, h_split, coef_done, coefT_done, coefT_kept, bias_done, acc_set, up_done,
         g_done, hidden_split, down_done, acc_done, y_done, x_done, xn_done, xT_done, next_done, squares_done, kept) = (
            c.sem("e0_" + n) for n in
            ("tables_loaded tables_set head_done h_split coef_done coefT_done coefT_kept bias_done acc_set up_done "
             "g_done hidden_split down_done acc_done y_done x_done xn_done xT_done next_done squares_done kept").split())

        with nc.Block() as block:
            @block.sync
            def _(sp):
                sp.dma_start(b_up[:], a["e0_b_up"]).then_inc(tables_loaded, 16)
                sp.dma_start(b_down[:], a["L0_ffn_b2"]).then_inc(tables_loaded, 16)

            @block.gpsimd
            def _(pool):
                pool.memset(ones[:], 1.0)
                pool.memset(eps[:], LN_EPS).then_inc(tables_set, 1)
                pool.wait_ge(tables_set, 1)
                with pool.Fori(0, B) as b:
                    norm.invert(pool, b)

            @block.tensor
            def _(pe):
                def up(b, e):
                    if e >= 2:
                        pe.wait_ge(g_done, E * b + e - 1)
                    product(nc.tensor, up_ps[:, e % 2, :],
                            [(lambda i, k=k: w_up[:, i, e * KC + k, :],
                              lambda j, k=k: h_parts[:, j, k, :]) for k in range(KC)]).then_inc(up_done, 1)

                def down(b, e):
                    pe.wait_ge(hidden_split, E * b + e + 1)
                    if e >= 2:
                        pe.wait_ge(acc_done, E * b + e - 1)
                    for t in range(NT):
                        last = product(nc.tensor, rows_of(down_ps[e % 2], t),
                                       [(lambda i: hidden[:, i, e % 2, t * P:(t + 1) * P],
                                         lambda j: w_down[:, j, e, :])])
                    last.then_inc(down_done, 1)

                pe.wait_ge(tables_loaded, 32)
                pe.wait_ge(tables_set, 1)
                with pe.Fori(0, B) as b:
                    pe.wait_ge(coef_done, b + 1)
                    for t in range(NT):
                        last = nc.tensor.transpose(tp_ps[0:E, 0, t * P:(t + 1) * P], coef[:, t, :], c.ident[:])
                    last.then_inc(coefT_done, 1)
                    pe.wait_ge(h_split, b + 1)
                    up(b, 0)
                    pe.wait_ge(coefT_kept, b + 1)
                    for t in range(NT):
                        last = nc.tensor.matmul(rows_of(tp_ps, t), coefT[:, t * P:(t + 1) * P], b_down[:], start=True,
                                                stop=True)
                    last.then_inc(bias_done, 1)
                    for e in range(E):
                        if e + 1 < E:
                            up(b, e + 1)
                        down(b, e)
                    pe.wait_ge(xn_done, b + 1)
                    transposes(nc.tensor, c, tp_ps, xn).then_inc(xT_done, 1)
                    pe.wait_ge(next_done, b + 1)
                    for t in range(NT):
                        for k in range(KC):
                            last = nc.tensor.matmul(tp_ps[:, 0, t:t + 1], squares[:, k, t * P:(t + 1) * P], ones[:],
                                                    start=k == 0, stop=k == KC - 1)
                    last.then_inc(squares_done, 1)

            @block.scalar
            def _(act):
                act.wait_ge(tables_loaded, 32)
                with act.Fori(0, B) as b:
                    nc.scalar.activation(h_parts[:, HEAD], c.hT[:, :, b, :], ACT.Copy).then_inc(head_done, 1)
                    act.wait_ge(coefT_done, b + 1)
                    nc.scalar.activation(coefT[:], tp_ps[0:E, 0, :], ACT.Copy).then_inc(coefT_kept, 1)
                    act.wait_ge(bias_done, b + 1)
                    nc.scalar.activation(acc[:].rearrange("p t d -> p (t d)"), tp_ps[:].rearrange("p n s -> p (n s)"),
                                         ACT.Copy).then_inc(acc_set, 1)
                    for e in range(E):
                        act.wait_ge(up_done, E * b + e + 1)
                        if e >= 2:
                            act.wait_ge(down_done, E * b + e - 1)
                        nc.scalar.activation(g[:, e % 2, :], up_ps[:, e % 2, :], ACT.Gelu, bias=b_up[:, e:e + 1])
                        nc.scalar.activation(hidden[:, HEAD, e % 2, :], up_ps[:, e % 2, :], ACT.Gelu,
                                             bias=b_up[:, e:e + 1]).then_inc(g_done, 1)
                    act.wait_ge(c.start, 1)
                    act.wait_ge(xT_done, b + 1)
                    for k in range(KC):
                        shift, scale = c.mod[:, 1, SA, k, bass.ds(b, 1)], c.mod[:, 1, CA, k, bass.ds(b, 1)]
                        nc.scalar.activation(c.hT[:, k, b, :], tp_ps[:, k, :], ACT.Identity, bias=shift, scale=scale)
                        last = nc.scalar.activation(squares[:, k, :], tp_ps[:, k, :], ACT.Square, bias=shift, scale=scale)
                    last.then_inc(next_done, 1)

            @block.vector
            def _(dve):
                def rest_hidden(b, e):
                    dve.wait_ge(g_done, E * b + e + 1)
                    nc.vector.tensor_tensor(hidden[:, REST, e % 2, :], g[:, e % 2, :],
                                            hidden[:, HEAD, e % 2, :].bitcast(F32), ALU.subtract).then_inc(hidden_split, 1)

                dve.wait_ge(c.constants, 32)
                with dve.Fori(0, B) as b:
                    nc.vector.tensor_copy(coef[:], c.coef[:, b]).then_inc(coef_done, 1)
                    dve.wait_ge(head_done, b + 1)
                    nc.vector.tensor_tensor(h_parts[:, REST], c.hT[:, :, b, :], h_parts[:, HEAD].bitcast(F32),
                                            ALU.subtract).then_inc(h_split, 1)
                    dve.wait_ge(acc_set, b + 1)
                    rest_hidden(b, 0)
                    for e in range(E):
                        if e + 1 < E:
                            rest_hidden(b, e + 1)
                        dve.wait_ge(down_done, E * b + e + 1)
                        for t in range(NT):
                            last = nc.vector.scalar_tensor_tensor(out=acc[:, t, :], in0=rows_of(down_ps[e % 2], t),
                                                                  scalar=coef[:, t, e:e + 1], in1=acc[:, t, :],
                                                                  op0=ALU.mult, op1=ALU.add)
                        last.then_inc(acc_done, 1)
                        dve.wait_ge(acc_done, E * b + e + 1)
                    nc.vector.tensor_tensor(y[:], acc[:], c.gate[:, b, :].unsqueeze(1).broadcast_to([P, NT, D]),
                                            ALU.mult).then_inc(y_done, 1)
                    dve.wait_ge(y_done, b + 1)
                    nc.vector.tensor_tensor(c.x[:, b], c.x[:, b], y[:], ALU.add).then_inc(x_done, 1)
                    dve.wait_ge(c.start, 1)
                    dve.wait_ge(x_done, b + 1)
                    norm.gather(lambda t: c.x[:, b, t, :])
                    norm.aggregate(dve, b)
                    norm.apply(dve, b, xn, lambda t: c.x[:, b, t, :], xn_done)
                    dve.wait_ge(c.start, 1)
                    dve.wait_ge(squares_done, b + 1)
                    nc.vector.tensor_copy(c.square_sum[:, b], tp_ps[:, 0, 0:NT]).then_inc(kept, 1)


def attention_part(c, a, w_qk, w_v, w_o):
    nc = c.nc
    PAIRS = H // 2
    VW = 3 * HD + 1
    with ExitStack() as ctx:
        def sb(name, shape, dt=F32):
            return c.sb("at_" + name, shape, dt, ctx)

        qk_bias, v_bias, o_bias = sb("qk_bias", [P, 2 * D]), sb("v_bias", [P, D]), sb("o_bias", [P, D])
        cos, sin, router_w = sb("cos", [P, NT, HD]), sb("sin", [P, NT, HD]), sb("router_w", [P, KC, E])
        eps, rms_eps = sb("eps", [P, NT]), sb("rms_eps", [P, B * NT])
        norm = Norm(c, ctx, "at_norm", eps[:])
        mean_square, inv_rms = sb("mean_square", [P, B * NT]), sb("inv_rms", [P, B, NT])
        h_parts = sb("h_parts", [P, 2, KC, S], F32R)
        qk, turned, rotated = sb("qk", [P, 2, 2 * D]), sb("turned", [P, 2, 2 * D]), sb("rotated", [P, 2, 2 * D])
        wide = sb("wide", [P, 2, 4 * S])
        qkT = sb("qkT", [P, 2, PAIRS, S], F32R)
        v, v_left = sb("v", [P, NT, D]), sb("v_left", [P, NT, D])
        v_parts = sb("v_parts", [P, NT, H, VW], BF16)
        sig_head, sig_rest = sb("sig_head", [P, 2, NT, S], F16), sb("sig_rest", [P, 2, NT, S], F16)
        o_sum, denom, inv_denom = sb("o_sum", [P, 2, 2, NT, HD]), sb("denom", [P, 2, 2 * NT]), sb("inv_denom", [P, 2, 2 * NT])
        rows, gate_bias = sb("rows", [P, NT, D]), sb("gate_bias", [P, D])
        h = qk[:].rearrange("p k s -> p k s")
        a_ps = c.psum("at_a_ps", 2, ctx)
        sc_ps = c.psum("at_sc_ps", 4, ctx)
        o_ps = c.psum("at_o_ps", 2, ctx)
        (tables_loaded, tables_set, ms_done, inv_rms_done, head_done, h_split, qk_done, v_done, qk_scaled, v_kept,
         cos_done, rot_done, sin_done, qk_head_done, qk_split, qkT_done, qkT_kept, v1_done, v_split, score_done, sig_done, sig_head_done,
         sig_split, av_done, sum_done, inv_done, heads_done, oT_done, o_head_done, o_split, proj_done, gated,
         x_biased, x_done, xn_done, xT_done, next_done, hT_kept, logits_done, logits_kept, gb_done) = (
            c.sem("at_" + n) for n in
            ("tables_loaded tables_set ms_done inv_rms_done head_done h_split qk_done v_done qk_scaled v_kept "
             "cos_done rot_done sin_done qk_head_done qk_split qkT_done qkT_kept v1_done v_split score_done sig_done sig_head_done "
             "sig_split av_done sum_done inv_done heads_done oT_done o_head_done o_split proj_done gated "
             "x_biased x_done xn_done xT_done next_done hT_kept logits_done logits_kept gb_done").split())
        N_TABLES = 16 * 6

        def by_head(t):
            return wide[:, t % 2, :].rearrange("p (i h c d) -> p i h c d", i=2, h=H, c=4)

        def heads_of(v):
            return v.rearrange("p (h d) -> p h d", d=HD)

        with nc.Block() as block:
            @block.sync
            def _(sp):
                for name, to, n in (("qk_bias", qk_bias, 2 * D), ("L1_attn_v_b", v_bias, D), ("L1_attn_o_b", o_bias, D)):
                    sp.dma_start(to[:], a[name].unsqueeze(0).broadcast_to([P, n])).then_inc(tables_loaded, 16)
                sp.dma_start(cos[:], a["cos"]).then_inc(tables_loaded, 16)
                sp.dma_start(sin[:], a["sin"]).then_inc(tables_loaded, 16)
                sp.dma_start(router_w[:], a["router_w"].rearrange("(k p) e -> p k e", p=P)).then_inc(tables_loaded, 16)
                sp.dma_start(c.gate[:], c.gates_dram[1, 0].unsqueeze(0).broadcast_to([P, B, D])).then_inc(c.constants, 16)

            @block.gpsimd
            def _(pool):
                pool.memset(eps[:], LN_EPS)
                pool.memset(v_parts[:, :, :, VW - 1], 1.0).then_inc(tables_set, 1)
                pool.wait_ge(ms_done, 1)
                nc.gpsimd.tensor_tensor(inv_rms[:].rearrange("p b t -> p (b t)"), mean_square[:], c.neg_half[:],
                                        ALU.pow).then_inc(inv_rms_done, 1)
                pool.wait_ge(tables_loaded, N_TABLES)
                pool.wait_ge(c.constants, 48)
                pool.wait_ge(tables_set, 1)
                with pool.Fori(0, B) as b:
                    nc.gpsimd.tensor_tensor(gate_bias[:], c.gate[:, b, :], o_bias[:], ALU.mult).then_inc(gb_done, 1)
                    pool.wait_ge(c.start, 1)
                    pool.wait_ge(gb_done, b + 1)
                    nc.gpsimd.tensor_tensor(c.x[:, b], c.x[:, b], gate_bias[:].unsqueeze(1).broadcast_to([P, NT, D]),
                                            ALU.add).then_inc(x_biased, 1)
                    for t in range(NT):
                        pool.wait_ge(qk_scaled, NT * b + t + 1)
                        nc.gpsimd.tensor_tensor(heads_of(rotated[:, t % 2, :]), heads_of(qk[:, t % 2, :]),
                                                cos[:, t, :].unsqueeze(1).broadcast_to([P, 2 * H, HD]),
                                                ALU.mult).then_inc(cos_done, 1)
                    pool.wait_ge(v_kept, 2 * (b + 1))
                    pool.sem_inc(c.passed, 1)
                    vh = v[:].rearrange("p t (h d) -> p (t h) d", d=HD)
                    left = v_left[:].rearrange("p t (h d) -> p (t h) d", d=HD)
                    for part, src in ((0, vh), (1, left), (2, left)):
                        to = v_parts[:, :, :, part * HD:(part + 1) * HD].rearrange("p t h d -> p (t h) d")
                        nc.gpsimd.tensor_copy(to, src).then_inc(v_split, 1)
                        if part < 2:
                            pool.wait_ge(v_split, 3 * b + part + 1)
                            nc.gpsimd.tensor_tensor(left, src, to, ALU.subtract).then_inc(v1_done, 1)
                            pool.wait_ge(v1_done, 2 * b + part + 1)
                            pool.sem_inc(c.passed, 1)
                    for n in range(H):
                        if n >= 2:
                            pool.wait_ge(av_done, H * b + n - 1)
                        pool.wait_ge(sig_done, 2 * (H * b + n + 1))
                        pool.sem_inc(c.passed, 1)
                        nc.gpsimd.tensor_scalar(sig_head[:, n % 2].rearrange("p t s -> p (t s)"), wide[:, n % 2, :],
                                                SIG_SCALE, 1.0, ALU.mult, ALU.mult).then_inc(sig_head_done, 1)
                    norm.invert(pool, b)
                    pool.wait_ge(c.start, 1)
                    pool.wait_ge(next_done, b + 1)
                    nc.gpsimd.tensor_copy(c.hT[:, :, b, :], h).then_inc(hT_kept, 1)

            @block.tensor
            def _(pe):
                def project(t):
                    cols = slice(t * P, (t + 1) * P)
                    product(nc.tensor, a_ps[:, t % 2, :],
                            [(lambda i, k=k: h_parts[:, i, k, cols], lambda j, k=k: w_qk[:, j, k, :])
                             for k in range(KC)]).then_inc(qk_done, 1)
                    last = product(nc.tensor, rows_of(o_ps, t),
                                   [(lambda i, k=k: h_parts[:, i, k, cols], lambda j, k=k: w_v[:, j, k, :])
                                    for k in range(KC)])
                    if t % 2:
                        last.then_inc(v_done, 1)

                def by_feature(t):
                    for i in range(2):
                        for pair in range(PAIRS):
                            n = i * PAIRS + pair
                            last = nc.tensor.transpose(sc_ps[:, n // 4, (n % 4) * P:(n % 4 + 1) * P],
                                                       wide[:, t % 2, n * P:(n + 1) * P], c.ident[:])
                    last.then_inc(qkT_done, 1)

                def scores(b, n):
                    base, pair = 64 * (n % 2), n // 2
                    for j in range(2):
                        if n >= 1:
                            pe.wait_ge(sig_done, 2 * (H * b + n) + j - 1)
                        for k in (2 * j, 2 * j + 1):
                            last = nc.tensor.matmul(sc_ps[:, k, :], qkT[base:base + 64, 1, pair, k * P:(k + 1) * P],
                                                    qkT[base:base + 64, 0, pair, :], start=True, stop=True)
                        last.then_inc(score_done, 1)

                def attend(b, n):
                    pe.wait_ge(sig_split, H * b + n + 1)
                    if n % 2 == 0 and n >= 4:
                        pe.wait_ge(heads_done, PAIRS * b + n // 2 - 1)
                    for t in range(NT):
                        at = (n % 2) * 256 + t * 64
                        for k in range(NT):
                            for part in (sig_head, sig_rest):
                                last = nc.tensor.matmul(o_ps[:, (n // 2) % 2, at:at + VW],
                                                        part[:, n % 2, k, t * P:(t + 1) * P], v_parts[:, k, n, :],
                                                        start=k == 0 and part is sig_head,
                                                        stop=k == NT - 1 and part is sig_rest)
                    last.then_inc(av_done, 1)

                pe.wait_ge(tables_loaded, N_TABLES)
                pe.wait_ge(tables_set, 1)
                with pe.Fori(0, B) as b:
                    pe.wait_ge(h_split, b + 1)
                    project(0)
                    project(1)
                    for t in range(NT):
                        pe.wait_ge(qk_split, NT * b + t + 1)
                        if t:
                            pe.wait_ge(qkT_kept, NT * b + t)
                        by_feature(t)
                        if t < 2:
                            if t == 0:
                                pe.wait_ge(v_kept, 2 * b + 1)
                            project(t + 2)
                    pe.wait_ge(qkT_kept, NT * (b + 1))
                    scores(b, 0)
                    for n in range(H):
                        if n + 1 < H:
                            scores(b, n + 1)
                        if n == 0:
                            pe.wait_ge(v_split, 3 * (b + 1))
                        attend(b, n)
                    pe.wait_ge(heads_done, PAIRS * (b + 1))
                    transposes(nc.tensor, c, a_ps, rows).then_inc(oT_done, 1)
                    pe.wait_ge(o_split, b + 1)
                    for t in range(NT):
                        last = product(nc.tensor, rows_of(sc_ps, t),
                                       [(lambda i, k=k: h_parts[:, i, k, t * P:(t + 1) * P],
                                         lambda j, k=k: w_o[:, j, k, :]) for k in range(KC)])
                    last.then_inc(proj_done, 1)
                    pe.wait_ge(xn_done, b + 1)
                    transposes(nc.tensor, c, a_ps, rows).then_inc(xT_done, 1)
                    pe.wait_ge(next_done, b + 1)
                    for t in range(NT):
                        for k in range(KC):
                            last = nc.tensor.matmul(o_ps[:, 0, t * E:(t + 1) * E], h[:, k, t * P:(t + 1) * P],
                                                    router_w[:, k, :], start=k == 0, stop=k == KC - 1)
                    last.then_inc(logits_done, 1)

            @block.scalar
            def _(act):
                with act.Fori(0, B) as b:
                    nc.scalar.activation(h_parts[:, HEAD], c.hT[:, :, b, :], ACT.Copy).then_inc(head_done, 1)
                    for t in range(NT):
                        act.wait_ge(rot_done, NT * b + t + 1)
                        if t >= 2:
                            act.wait_ge(qkT_done, NT * b + t - 1)
                        src = rotated[:, t % 2, :].rearrange("p (i h d) -> p i h d", i=2, d=HD)
                        to = by_head(t).bitcast(F32R)
                        nc.scalar.activation(to[:, 0, :, 0:3:2, :], src[:, 0].unsqueeze(2).broadcast_to([P, H, 2, HD]),
                                             ACT.Copy)
                        nc.scalar.activation(to[:, 1, :, 0:2, :], src[:, 1].unsqueeze(2).broadcast_to([P, H, 2, HD]),
                                             ACT.Copy).then_inc(qk_head_done, 1)
                        act.wait_ge(qkT_done, NT * b + t + 1)
                        for n in range(4):
                            last = nc.scalar.activation(
                                qkT[:, n // 2, (n % 2) * 4:(n % 2) * 4 + 4, t * P:(t + 1) * P],
                                sc_ps[:, n, :].rearrange("p (g s) -> p g s", g=4), ACT.Copy)
                        last.then_inc(qkT_kept, 1)
                    for n in range(H):
                        if n >= 2:
                            act.wait_ge(sig_split, H * b + n - 1)
                        for j in range(2):
                            act.wait_ge(score_done, 2 * (H * b + n) + j + 1)
                            nc.scalar.activation(wide[:, n % 2, j * 2 * S:(j + 1) * 2 * S],
                                                 sc_ps[:, 2 * j:2 * j + 2, :].rearrange("p n s -> p (n s)"),
                                                 ACT.Sigmoid, scale=float(HD) ** -0.5).then_inc(sig_done, 1)
                    act.wait_ge(oT_done, b + 1)
                    nc.scalar.activation(h_parts[:, HEAD], a_ps[:], ACT.Copy).then_inc(o_head_done, 1)
                    act.wait_ge(c.start, 1)
                    act.wait_ge(xT_done, b + 1)
                    for k in range(KC):
                        last = nc.scalar.activation(h[:, k, :], a_ps[:, k, :], ACT.Identity,
                                                    bias=c.mod[:, 1, SB, k, bass.ds(b, 1)],
                                                    scale=c.mod[:, 1, CB, k, bass.ds(b, 1)])
                    last.then_inc(next_done, 1)

            @block.vector
            def _(dve):
                def scale_and_turn(b, t):
                    dve.wait_ge(c.start, 1)
                    dve.wait_ge(qk_done, NT * b + t + 1)
                    buf = t % 2
                    nc.vector.scalar_tensor_tensor(out=qk[:, buf, :], in0=a_ps[:, buf, :],
                                                   scalar=inv_rms[:, b, t:t + 1], in1=qk_bias[:], op0=ALU.mult,
                                                   op1=ALU.add).then_inc(qk_scaled, 1)
                    dve.wait_ge(qk_scaled, NT * b + t + 1)
                    src = qk[:, buf, :].rearrange("p (h d two) -> p h d two", two=2, d=HD // 2)
                    to = turned[:, buf, :].rearrange("p (h d two) -> p h d two", two=2, d=HD // 2)
                    sines = sin[:, t, :].rearrange("p (d two) -> p d two", two=2)
                    for i in range(2):
                        last = nc.vector.tensor_tensor(to[:, :, :, i], src[:, :, :, 1 - i],
                                                       sines[:, :, i].unsqueeze(1).broadcast_to([P, 2 * H, HD // 2]),
                                                       ALU.mult)
                    last.then_inc(sin_done, 1)
                    dve.wait_ge(sin_done, NT * b + t + 1)
                    dve.wait_ge(cos_done, NT * b + t + 1)
                    nc.vector.tensor_tensor(rotated[:, buf, :], rotated[:, buf, :], turned[:, buf, :],
                                            ALU.add).then_inc(rot_done, 1)

                def keep_values(b, half):
                    dve.wait_ge(v_done, 2 * b + half + 1)
                    nc.vector.tensor_tensor(v[:, 2 * half:2 * half + 2, :], o_ps[:, half, :].rearrange("p (t d) -> p t d", t=2),
                                            v_bias[:].unsqueeze(1).broadcast_to([P, 2, D]), ALU.add).then_inc(v_kept, 1)

                def rests(b, t):
                    dve.wait_ge(qk_head_done, NT * b + t + 1)
                    src = rotated[:, t % 2, :].rearrange("p (i h d) -> p i h d", i=2, d=HD)
                    to, of = by_head(t).bitcast(F32R), by_head(t)
                    nc.vector.tensor_tensor(to[:, 0, :, 1:4:2, :], src[:, 0].unsqueeze(2).broadcast_to([P, H, 2, HD]),
                                            of[:, 0, :, 0:3:2, :], ALU.subtract)
                    nc.vector.tensor_tensor(to[:, 1, :, 2:4, :], src[:, 1].unsqueeze(2).broadcast_to([P, H, 2, HD]),
                                            of[:, 1, :, 0:2, :], ALU.subtract).then_inc(qk_split, 1)

                def sum_parts(b, pair):
                    dve.wait_ge(av_done, H * b + 2 * pair + 2)
                    got = o_ps[:, pair % 2, :].rearrange("p (n w) -> p n w", w=64)
                    buf = pair % 2
                    nc.vector.tensor_reduce(o_sum[:, buf].rearrange("p n t d -> p (n t) d"),
                                            got[:, :, 0:3 * HD].rearrange("p n (c d) -> p n d c", c=3), AX, ALU.add)
                    nc.vector.tensor_scalar(denom[:, buf, :], got[:, :, 3 * HD], SUM_EPS * SIG_SCALE, None,
                                            ALU.add).then_inc(sum_done, 1)
                    dve.wait_ge(sum_done, PAIRS * b + pair + 1)
                    nc.vector.reciprocal(inv_denom[:, buf, :], denom[:, buf, :]).then_inc(inv_done, 1)
                    dve.wait_ge(inv_done, PAIRS * b + pair + 1)
                    to = rows[:, :, 2 * pair * HD:(2 * pair + 2) * HD].rearrange("p t (n d) -> p n t d", n=2)
                    for n in range(2):
                        last = nc.vector.tensor_tensor(to[:, n], o_sum[:, buf, n],
                                                       inv_denom[:, buf, n * NT:(n + 1) * NT].unsqueeze(2).broadcast_to(
                                                           [P, NT, HD]), ALU.mult)
                    last.then_inc(heads_done, 1)

                nc.vector.tensor_scalar(mean_square[:], c.square_sum[:].rearrange("p b t -> p (b t)"), 1.0 / D, RMS_EPS,
                                        ALU.mult, ALU.add).then_inc(ms_done, 1)
                dve.wait_ge(inv_rms_done, 1)
                dve.wait_ge(tables_loaded, N_TABLES)
                dve.wait_ge(c.constants, 48)
                with dve.Fori(0, B) as b:
                    dve.wait_ge(head_done, b + 1)
                    nc.vector.tensor_tensor(h_parts[:, REST], c.hT[:, :, b, :], h_parts[:, HEAD].bitcast(F32),
                                            ALU.subtract).then_inc(h_split, 1)
                    for t in range(NT):
                        scale_and_turn(b, t)
                        if t % 2:
                            keep_values(b, t // 2)
                        rests(b, t)
                    for n in range(H):
                        dve.wait_ge(sig_head_done, H * b + n + 1)
                        nc.vector.scalar_tensor_tensor(out=sig_rest[:, n % 2].rearrange("p t s -> p (t s)"),
                                                       in0=wide[:, n % 2, :], scalar=SIG_SCALE,
                                                       in1=sig_head[:, n % 2].rearrange("p t s -> p (t s)"),
                                                       op0=ALU.mult, op1=ALU.subtract).then_inc(sig_split, 1)
                        if n % 2 == 1 and n >= 3:
                            sum_parts(b, n // 2 - 1)
                    sum_parts(b, PAIRS - 1)
                    dve.wait_ge(o_head_done, b + 1)
                    nc.vector.tensor_tensor(h_parts[:, REST], a_ps[:], h_parts[:, HEAD].bitcast(F32),
                                            ALU.subtract).then_inc(o_split, 1)
                    dve.wait_ge(proj_done, b + 1)
                    gated_rows = v
                    nc.vector.tensor_tensor(gated_rows[:], sc_ps[:, 0:2, :].rearrange("p n (t d) -> p (n t) d", d=D),
                                            c.gate[:, b, :].unsqueeze(1).broadcast_to([P, NT, D]),
                                            ALU.mult).then_inc(gated, 1)
                    dve.wait_ge(c.start, 1)
                    dve.wait_ge(gated, b + 1)
                    dve.wait_ge(x_biased, b + 1)
                    nc.vector.tensor_tensor(c.x[:, b], c.x[:, b], gated_rows[:], ALU.add).then_inc(x_done, 1)
                    dve.wait_ge(c.start, 1)
                    dve.wait_ge(x_done, b + 1)
                    norm.gather(lambda t: c.x[:, b, t, :])
                    norm.aggregate(dve, b)
                    norm.apply(dve, b, rows, lambda t: c.x[:, b, t, :], xn_done)
                    dve.wait_ge(c.start, 1)
                    dve.wait_ge(logits_done, b + 1)
                    nc.vector.tensor_copy(c.logits[:, b], o_ps[:, 0, 0:NT * E].rearrange("p (t e) -> p t e", t=NT)
                                          ).then_inc(logits_kept, 1)
                    dve.wait_ge(hT_kept, b + 1)


def sigmoid_router(c, a):
    nc = c.nc
    N = B * NT
    with ExitStack() as ctx:
        weight_sum, inv_sum = c.sb("route_weight_sum", [P, N], ctx=ctx), c.sb("route_inv_sum", [P, N], ctx=ctx)
        biased, probs, count, chosen = (c.sb("route_" + n, [P, N, E], ctx=ctx)
                                        for n in ("biased", "probs", "count", "chosen"))
        bias, better = c.sb("route_bias", [P, E], ctx=ctx), c.sb("route_better", [P, N, E, E], ctx=ctx)
        bias_loaded, biased_done, probs_done = c.sem("route_bias_loaded"), c.sem("route_biased_done"), c.sem("route_probs_done")
        logits, coef = c.logits[:].rearrange("p b t e -> p (b t) e"), c.coef[:].rearrange("p b t e -> p (b t) e")

        with nc.Block() as block:
            @block.sync
            def _(sp):
                sp.dma_start(bias[:], a["L1_ffn_routing_bias"].unsqueeze(0).broadcast_to([P, E])).then_inc(bias_loaded, 16)
                sp.dma_start(c.gate[:], c.gates_dram[1, 1].unsqueeze(0).broadcast_to([P, B, D])).then_inc(c.constants, 16)

            @block.scalar
            def _(act):
                act.wait_ge(biased_done, 1)
                nc.scalar.activation(probs[:], biased[:], ACT.Sigmoid).then_inc(probs_done, 1)

            @block.vector
            def _(dve):
                nc.vector.memset(better[:], 0.0)
                dve.wait_ge(bias_loaded, 16)
                nc.vector.tensor_tensor(biased[:], logits, bias[:].unsqueeze(1).broadcast_to([P, N, E]),
                                        ALU.add).then_inc(biased_done, 1)
                dve.wait_ge(probs_done, 1)
                choose(nc, dve, probs[:], better, count[:], chosen[:], weight_sum[:], coef)
                nc.vector.reciprocal(inv_sum[:], weight_sum[:])
                dve.drain()
                nc.vector.tensor_tensor(coef, chosen[:], inv_sum[:].unsqueeze(2).broadcast_to([P, N, E]), ALU.mult)


def silu_experts_part(c, a, out):
    nc = c.nc
    NX = E + 1
    CHUNK = (2 * KC * F1 + IC * D) // B
    with ExitStack() as ctx:
        def sb(name, shape, dt=F32):
            return c.sb("e1_" + name, shape, dt, ctx)

        raw, w = sb("raw", [P, B, CHUNK]), sb("w", [P, 2, 2, B, CHUNK], F32R)
        h_parts, hidden = sb("h_parts", [P, 2, KC, S], F32R), sb("hidden", [P, 2, IC, S], F32R)
        silu, gu = sb("silu", [P, 2, S]), sb("gu", [P, 2, S])
        acc, coef = sb("acc", [P, B, NT, D]), sb("coef", [P, NX * B, NT])
        gate_ps = c.psum("e1_gate_ps", 2, ctx)
        up_ps = c.psum("e1_up_ps", 2, ctx)
        down_ps = c.psum("e1_down_ps", NT, ctx)
        (raw_loaded, w_head_done, w_split, h_head_done, h_split, gate_done, up_done, silu_done, gu_done, hidden_head_done,
         hidden_split, down_done, acc_done, y_done, x_done, stored) = (
            c.sem("e1_" + n) for n in
            ("raw_loaded w_head_done w_split h_head_done h_split gate_done up_done silu_done gu_done hidden_head_done "
             "hidden_split down_done acc_done y_done x_done stored").split())

        def weights(buf, part):
            return w[:, buf, part].rearrange("p b c -> p (b c)")

        def gate_up(buf, part, k, which, i):
            at = (2 * k + which) * F1 + i * P
            return weights(buf, part)[:, at:at + P]

        def down_rows(buf, part, i):
            at = 2 * KC * F1 + i * D
            return weights(buf, part)[:, at:at + D]

        with nc.Block() as block:
            @block.sync
            def _(sp):
                sp.dma_start(raw[:], a["experts"][0]).then_inc(raw_loaded, 16)
                with sp.Fori(1, NX) as x:
                    sp.wait_ge(w_split, B * x)
                    sp.dma_start(raw[:], a["experts"][x]).then_inc(raw_loaded, 16)
                view = out.rearrange("b (t p) d -> b p t d", p=P)
                with sp.Fori(0, B) as b:
                    sp.wait_ge(x_done, b + 1)
                    sp.dma_start(view[b], c.x[:, b]).then_inc(stored, 16)
                sp.wait_ge(stored, 16 * B)

            @block.tensor
            def _(pe):
                def step(n, buf, chunks):
                    pe.wait_ge(w_split, chunks)
                    pe.wait_ge(h_split, n + 1)
                    for i in range(IC):
                        if i >= 2:
                            pe.wait_ge(gu_done, IC * n + i - 1)
                        for which, ps, done in ((0, gate_ps, gate_done), (1, up_ps, up_done)):
                            product(nc.tensor, ps[:, i % 2, :],
                                    [(lambda p, k=k: gate_up(buf, p, k, which, i),
                                      lambda p, k=k: h_parts[:, p, k, :]) for k in range(KC)]).then_inc(done, 1)
                    pe.wait_ge(acc_done, n + 1)
                    for i in range(IC):
                        pe.wait_ge(hidden_split, IC * n + i + 1)
                        for t in range(NT):
                            for m, (p, r) in enumerate(PASSES):
                                last = nc.tensor.matmul(down_ps[:, t, 0:D], hidden[:, p, i, t * P:(t + 1) * P],
                                                        down_rows(buf, r, i), start=i == 0 and m == 0,
                                                        stop=i == IC - 1 and m == 2)
                    last.then_inc(down_done, 1)

                with pe.Fori(0, E // 2) as q:
                    for buf in range(2):
                        with pe.Fori(0, B) as b:
                            step(q * (2 * B) + buf * B + b, buf, q * (2 * B) + (buf + 1) * B)
                with pe.Fori(0, B) as b:
                    step(b + E * B, E % 2, NX * B)

            @block.scalar
            def _(act):
                def split_weight_heads(b, buf):
                    nc.scalar.activation(w[:, buf, HEAD, b], raw[:, b], ACT.Copy).then_inc(w_head_done, 1)

                def head_of_h(b):
                    nc.scalar.activation(h_parts[:, HEAD], c.hT[:, :, b, :], ACT.Copy).then_inc(h_head_done, 1)

                def step(n, b, buf, after, more_weights):
                    def silu_of(i):
                        act.wait_ge(gate_done, IC * n + i + 1)
                        nc.scalar.activation(silu[:, i % 2, :], gate_ps[:, i % 2, :], ACT.Silu).then_inc(silu_done, 1)

                    silu_of(0)
                    act.wait_ge(acc_done, n + 1)
                    for i in range(IC):
                        if i + 1 < IC:
                            silu_of(i + 1)
                        act.wait_ge(gu_done, IC * n + i + 1)
                        nc.scalar.activation(hidden[:, HEAD, i, :], gu[:, i % 2, :], ACT.Copy).then_inc(hidden_head_done, 1)
                    if after is not None:
                        act.wait_ge(up_done, IC * (n + 1))
                        head_of_h(after)
                    if more_weights:
                        split_weight_heads(b, 1 - buf)

                act.wait_ge(raw_loaded, 16)
                for b in range(B):
                    split_weight_heads(b, 0)
                head_of_h(0)
                with act.Fori(0, E // 2) as q:
                    for buf in range(2):
                        act.wait_ge(raw_loaded, q * 32 + 16 * (buf + 2))
                        with act.Fori(0, B - 1) as b:
                            step(q * (2 * B) + buf * B + b, b, buf, b + 1, True)
                        step(q * (2 * B) + (buf + 1) * B - 1, B - 1, buf, 0, True)
                with act.Fori(0, B - 1) as b:
                    step(b + E * B, b, 0, b + 1, False)
                step(NX * B - 1, B - 1, 0, None, False)

            @block.vector
            def _(dve):
                def split_weight_rests(m, b, buf):
                    dve.wait_ge(w_head_done, m + 1)
                    nc.vector.tensor_tensor(w[:, buf, REST, b], raw[:, b], w[:, buf, HEAD, b].bitcast(F32),
                                            ALU.subtract).then_inc(w_split, 1)

                def rest_of_h(n, b):
                    dve.wait_ge(h_head_done, n + 1)
                    nc.vector.tensor_tensor(h_parts[:, REST], c.hT[:, :, b, :], h_parts[:, HEAD].bitcast(F32),
                                            ALU.subtract).then_inc(h_split, 1)

                def step(n, b, buf, after, more_weights):
                    def times_up(i):
                        if i < 2:
                            dve.wait_ge(acc_done, n + 1)
                        else:
                            dve.wait_ge(hidden_split, IC * n + i - 1)
                        dve.wait_ge(silu_done, IC * n + i + 1)
                        dve.wait_ge(up_done, IC * n + i + 1)
                        nc.vector.tensor_tensor(gu[:, i % 2, :], silu[:, i % 2, :], up_ps[:, i % 2, :],
                                                ALU.mult).then_inc(gu_done, 1)

                    times_up(0)
                    for i in range(IC):
                        if i + 1 < IC:
                            times_up(i + 1)
                        dve.wait_ge(hidden_head_done, IC * n + i + 1)
                        nc.vector.tensor_tensor(hidden[:, REST, i, :], gu[:, i % 2, :],
                                                hidden[:, HEAD, i, :].bitcast(F32), ALU.subtract).then_inc(hidden_split, 1)
                    if after is not None:
                        rest_of_h(n + 1, after)
                    if more_weights:
                        split_weight_rests(n + B, b, 1 - buf)
                    dve.wait_ge(down_done, n + 1)
                    for t in range(NT):
                        last = nc.vector.scalar_tensor_tensor(out=acc[:, b, t, :], in0=down_ps[:, t, 0:D],
                                                              scalar=coef[:, n, t:t + 1], in1=acc[:, b, t, :],
                                                              op0=ALU.mult, op1=ALU.add)
                    last.then_inc(acc_done, 1)

                def finish(b):
                    dve.wait_ge(acc_done, b + E * B + 2)
                    nc.vector.tensor_tensor(acc[:, b], acc[:, b], c.gate[:, b, :].unsqueeze(1).broadcast_to([P, NT, D]),
                                            ALU.mult).then_inc(y_done, 1)
                    dve.wait_ge(y_done, b + 1)
                    nc.vector.tensor_tensor(c.x[:, b], c.x[:, b], acc[:, b], ALU.add).then_inc(x_done, 1)

                nc.vector.memset(acc[:], 0.0).then_inc(acc_done, 1)
                nc.vector.memset(coef[:, 0:B, :], 1.0)
                nc.vector.tensor_copy(coef[:, B:, :].rearrange("p (e b) t -> p (b t) e", e=E),
                                      c.coef[:].rearrange("p b t e -> p (b t) e"))
                dve.drain()
                for b in range(B):
                    split_weight_rests(b, b, 0)
                rest_of_h(0, 0)
                dve.wait_ge(c.constants, 64)
                with dve.Fori(0, E // 2) as q:
                    for buf in range(2):
                        with dve.Fori(0, B - 1) as b:
                            step(q * (2 * B) + buf * B + b, b, buf, b + 1, True)
                        step(q * (2 * B) + (buf + 1) * B - 1, B - 1, buf, 0, True)
                with dve.Fori(0, B - 1) as b:
                    step(b + E * B, b, 0, b + 1, False)
                    finish(b)
                step(NX * B - 1, B - 1, 0, None, False)
                finish(B - 1)


def program(nc, a, out):
    with ExitStack() as ctx:
        c = Core(nc, ctx)
        with ExitStack() as weights:
            w_ret = c.sb("w_ret", [P, 2, KC, D], F32R, weights)
            w_in = c.sb("w_in", [P, 2, KC, F0], F32R, weights)
            w_out = c.sb("w_out", [P, 2, MC, D], F32R, weights)
            modulation_and_weights(c, a, w_ret, w_in, w_out)
            c.begin_part()
            retention_part(c, a, w_ret, w_in, w_out)
            c.end_part()
        with ExitStack() as weights:
            w_up = c.sb("e0_w_up", [P, 2, E * KC, P], F32R, weights)
            w_down = c.sb("e0_w_down", [P, 2, E, D], F32R, weights)
            split_weights(c, "e0_w", ((a["L0_ffn_w1"].rearrange("e (k p) n -> p (e k) n", p=P), w_up, None),
                                      (a["L0_ffn_w2"].rearrange("e p n -> p e n"), w_down, None)))
            softmax_router(c)
            gelu_experts_part(c, a, w_up, w_down)
        with ExitStack() as weights:
            w_qk = c.sb("w_qk", [P, 2, KC, 2 * D], F32R, weights)
            w_v = c.sb("w_v", [P, 2, KC, D], F32R, weights)
            w_o = c.sb("w_o", [P, 2, KC, D], F32R, weights)
            chunks = "(k p) n -> p k n"
            split_weights(c, "at_w", ((a["wqT"].rearrange(chunks, p=P), w_qk[:, :, :, 0:D], a["qn_scale"]),
                                      (a["wkT"].rearrange(chunks, p=P), w_qk[:, :, :, D:2 * D], a["kn_scale"]),
                                      (a["wvT"].rearrange(chunks, p=P), w_v, None),
                                      (a["woT"].rearrange(chunks, p=P), w_o, None)))
            attention_part(c, a, w_qk, w_v, w_o)
        sigmoid_router(c, a)
        silu_experts_part(c, a, out)


def _columns(v):
    import numpy as np
    return np.ascontiguousarray(v.reshape(-1, P).T)


def layout(i):
    import numpy as np
    o = {"cT": np.ascontiguousarray(np.stack([i[f"L{l}_c"].T.reshape(KC, P, B).transpose(1, 0, 2) for l in range(2)], 1))}
    for name, of in (("b_ret", "L0_attn_b_ret"), ("ln1_scale", "L0_attn_ln1_scale"), ("ln1_bias", "L0_attn_ln1_bias"),
                     ("b_in", "L0_attn_b1"), ("e0_b_up", "L0_ffn_b1"), ("qn_scale", "L1_attn_qn_scale"),
                     ("kn_scale", "L1_attn_kn_scale")):
        o[name] = _columns(i[of])
    for name in ("L0_wmod", "L1_wmod", "L0_attn_x", "L0_attn_W_ret", "L0_attn_W1", "L0_attn_W2", "L0_attn_ln2_scale",
                 "L0_attn_ln2_bias", "L0_attn_b2", "L0_ffn_gate_w",
                 "L0_ffn_w1", "L0_ffn_w2", "L0_ffn_b2", "L1_attn_v_b", "L1_attn_o_b"):
        o[name] = np.ascontiguousarray(i[name])
    for name, of in (("wqT", "L1_attn_q_w"), ("wkT", "L1_attn_k_w"), ("wvT", "L1_attn_v_w"), ("woT", "L1_attn_o_w"),
                     ("router_w", "L1_ffn_router_w")):
        o[name] = np.ascontiguousarray(i[of].T)
    o["qk_bias"] = np.concatenate([i["L1_attn_q_b"], i["L1_attn_k_b"]])
    o["L1_ffn_routing_bias"] = np.ascontiguousarray(i["L1_ffn_routing_bias"])
    experts = []
    for gate, up, down in [tuple(i["L1_ffn_" + n] for n in ("sg_w", "su_w", "sd_w"))] + [
            tuple(i["L1_ffn_" + n][e] for n in ("wg", "wu", "wd")) for e in range(E)]:
        both = np.concatenate([gate.T, up.T], axis=1).reshape(KC, P, 2 * F1).transpose(1, 0, 2).reshape(P, -1)
        experts.append(np.concatenate([both, down.T.reshape(IC, P, D).transpose(1, 0, 2).reshape(P, -1)], axis=1))
    o["experts"] = np.ascontiguousarray(np.stack(experts).reshape(E + 1, P, B, -1))
    o["cos"], o["sin"] = rope_tables()
    return o


def rope_tables():
    import numpy as np
    inv_freq = np.float32(1.0) / np.float32(10000.0) ** (np.arange(0, HD, 2, dtype=np.float32) / np.float32(HD))
    freqs = np.arange(S, dtype=np.float32)[:, None] * inv_freq[None, :].astype(np.float32)
    emb = np.concatenate([freqs, freqs], axis=-1).astype(np.float64)
    sign = np.where(np.arange(HD) % 2 == 0, -1.0, 1.0)
    return tuple(np.ascontiguousarray(v.astype(np.float32).reshape(NT, P, HD).transpose(1, 0, 2))
                 for v in (np.cos(emb), np.sin(emb) * sign))


def kernel(**inputs):
    import numpy as np
    import concourse.bacc as bacc
    from concourse.bass_utils import run_bass_kernel_spmd

    nc = bacc.Bacc("TRN2", target_bir_lowering=False, num_devices=1)
    arrays = layout({k: np.asarray(v) for k, v in inputs.items()})
    a = {k: nc.dram_tensor("in_" + k, v.shape, mybir.dt.from_np(v.dtype), kind="ExternalInput").ap() for k, v in arrays.items()}
    out = nc.dram_tensor("out", (B, S, D), F32, kind="ExternalOutput").ap()
    program(nc, a, out)
    return run_bass_kernel_spmd(nc, [{"in_" + k: v for k, v in arrays.items()}], core_ids=[0]).results[0]["out"]
```

```python
from contextlib import ExitStack

import concourse.bass as bass
from concourse import mybir

F32 = mybir.dt.float32
F32R = mybir.dt.float32r
BF16 = mybir.dt.bfloat16
F16 = mybir.dt.float16
ALU = mybir.AluOpType
ACT = mybir.ActivationFunctionType
AX = mybir.AxisListType.X

P = 128
B, S, D = 8, 512, 256
NT = S // P
KC = D // P
F0 = 1024
MC = F0 // P
E = 8
F1 = 512
IC = F1 // P
H, HD = 16, 16
SA, CA, SB, CB = range(4)
MOD_CHUNK = (0, 1, 3, 4)
GA, GB = 2, 5
LN_EPS, RMS_EPS, SUM_EPS = 1e-5, 1e-8, 1e-8
SIG_SCALE = 2.0 ** 14
HEAD, REST = 0, 1
PASSES = ((HEAD, HEAD), (HEAD, REST), (REST, HEAD))


def product(pe, out, terms):
    steps = [(left, right, i, j) for left, right in terms for i, j in PASSES]
    for n, (left, right, i, j) in enumerate(steps):
        last = pe.matmul(out, left(i), right(j), start=n == 0, stop=n == len(steps) - 1)
    return last


class Core:

    def __init__(self, nc, ctx):
        self.nc, self.ctx, self.part_sems = nc, ctx, None
        self.x = self.sb("x", [P, B, NT, D])
        self.hT = self.sb("hT", [P, KC, B, S])
        self.logits = self.sb("logits", [P, B, NT, E])
        self.coef = self.sb("coef", [P, B, NT, E])
        self.square_sum = self.sb("square_sum", [P, B, NT])
        self.mod = self.sb("mod", [P, 2, 4, KC, B])
        self.gate = self.sb("gate", [P, B, D])
        self.ident = self.sb("ident", [P, P])
        self.neg_half = self.sb("neg_half", [P, B * NT])
        self.gates_dram = nc.dram_tensor("gates", [2, 2, B, D], F32, kind="Internal").ap()
        self.x_first, self.x_rest = self.sem("x_first"), self.sem("x_rest")
        self.constants = self.sem("constants")
        self.start = self.sem("start")
        self.passed = self.sem("passed")

    def sb(self, name, shape, dt=F32, ctx=None):
        return (ctx or self.ctx).enter_context(self.nc.sbuf_tensor(name, shape, dt))

    def sem(self, name):
        sem = self.nc.alloc_semaphore(name)
        if self.part_sems is not None:
            self.part_sems.append(sem)
        return sem

    def begin_part(self):
        self.part_sems = []

    def end_part(self):
        self.nc.clear_and_free_semaphores(self.part_sems)
        self.nc.all_engine_barrier()
        self.part_sems = None

    def psum(self, name, n, ctx):
        return ctx.enter_context(self.nc.psum_tensor(name, [P, n, 512], F32))


def modulation_and_weights(c, a, w_ret, w_in, w_out):
    nc = c.nc
    with ExitStack() as ctx:
        cT = c.sb("cT", [P, 2, KC, B], ctx=ctx)
        silu_c = c.sb("silu_c", [P, 2, KC, B], ctx=ctx)
        wmod = c.sb("wmod", [P, 2, KC, 6 * D], ctx=ctx)
        raw_ret = c.sb("raw_ret", [P, KC, D], ctx=ctx)
        raw_in = c.sb("raw_in", [P, KC, F0], ctx=ctx)
        raw_out = c.sb("raw_out", [P, MC, D], ctx=ctx)
        gate_rows = c.sb("gate_rows", [B, 2, 2, D], ctx=ctx)
        gate_sign = c.sb("gate_sign", [B, 2, 2, D], ctx=ctx)
        ones = c.sb("ones_setup", [P, P], ctx=ctx)
        mod_ps = c.psum("mod_ps", 2, ctx)
        gate_ps = c.psum("gate_ps", 2, ctx)
        cond_loaded, wmod_loaded = c.sem("cond_loaded"), c.sem("wmod_loaded")
        raw_loaded = [c.sem(f"raw_loaded_{n}") for n in range(3)]
        silu_done, mod_done, gates_done = c.sem("silu_done"), c.sem("mod_done"), c.sem("gates_done")
        mod_scales, sign_done, size_done = c.sem("mod_scales"), c.sem("sign_done"), c.sem("size_done")
        rows_done, rows_stored = c.sem("rows_done"), c.sem("rows_stored")
        heads_split, rests_split, ones_set = c.sem("heads_split"), c.sem("rests_split"), c.sem("ones_set")
        weights = ((raw_ret, w_ret), (raw_in, w_in), (raw_out, w_out))

        with nc.Block() as block:
            @block.sync
            def _(sp):
                sp.dma_start(cT[:], a["cT"]).then_inc(cond_loaded, 16)
                for l in range(2):
                    sp.dma_start(wmod[:, l], a[f"L{l}_wmod"].rearrange("(k p) n -> p k n", p=P)).then_inc(wmod_loaded, 16)
                x_in = a["L0_attn_x"].rearrange("b (t p) d -> p b t d", p=P)
                sp.dma_start(c.x[:, 0], x_in[:, 0]).then_inc(c.x_first, 16)
                sp.dma_start(raw_ret[:], a["L0_attn_W_ret"].rearrange("(k p) n -> p k n", p=P)).then_inc(raw_loaded[0], 16)
                sp.dma_start(raw_in[:], a["L0_attn_W1"].rearrange("(k p) n -> p k n", p=P)).then_inc(raw_loaded[1], 16)
                sp.dma_start(raw_out[:], a["L0_attn_W2"].rearrange("(k p) n -> p k n", p=P)).then_inc(raw_loaded[2], 16)
                for b in range(1, B):
                    sp.dma_start(c.x[:, b], x_in[:, b]).then_inc(c.x_rest, 16)
                sp.wait_ge(rows_done, 1)
                sp.dma_start(c.gates_dram.rearrange("l k b d -> b l k d"), gate_rows[:]).then_inc(rows_stored, 16)
                sp.wait_ge(rows_stored, 16)
                sp.dma_start(c.gate[:], c.gates_dram[0, 0].unsqueeze(0).broadcast_to([P, B, D])).then_inc(c.constants, 16)

            @block.gpsimd
            def _(pool):
                pool.memset(c.neg_half[:], -0.5).then_inc(c.start, 1)
                pool.memset(ones[:], 1.0).then_inc(ones_set, 1)
                pool.wait_ge(ones_set, 1)
                pool.affine_select(out=c.ident[:], in_=ones[:], compare_op=ALU.is_equal, fill=0.0, base=0,
                                   pattern=[[-1, P]], channel_multiplier=1).then_inc(ones_set, 1)

            @block.scalar
            def _(act):
                act.wait_ge(cond_loaded, 16)
                nc.scalar.activation(silu_c[:], cT[:], ACT.Silu).then_inc(silu_done, 1)
                for n, (raw, split) in enumerate(weights):
                    act.wait_ge(raw_loaded[n], 16)
                    nc.scalar.activation(split[:, HEAD], raw[:], ACT.Copy).then_inc(heads_split, 1)

            @block.tensor
            def _(pe):
                pe.wait_ge(silu_done, 1)
                pe.wait_ge(wmod_loaded, 32)
                for l in range(2):
                    for kind, chunk in enumerate(MOD_CHUNK):
                        for m in range(KC):
                            at = (kind * KC + m) * B
                            col = chunk * D + m * P
                            for k in range(KC):
                                last = nc.tensor.matmul(mod_ps[:, l, at:at + B], wmod[:, l, k, col:col + P],
                                                        silu_c[:, l, k, :], start=k == 0, stop=k == KC - 1)
                    last.then_inc(mod_done, 1)
                    for n, chunk in enumerate((GA, GB)):
                        for k in range(KC):
                            last = nc.tensor.matmul(gate_ps[0:B, l, n * D:(n + 1) * D], silu_c[:, l, k, :],
                                                    wmod[:, l, k, chunk * D:(chunk + 1) * D],
                                                    start=k == 0, stop=k == KC - 1)
                    last.then_inc(gates_done, 1)

            @block.vector
            def _(dve):
                dve.wait_ge(gates_done, 2)
                g = gate_ps[0:B, :, :].rearrange("b l n -> b (l n)")
                sign = gate_sign[:].rearrange("b l k d -> b (l k d)")
                rows = gate_rows[:].rearrange("b l k d -> b (l k d)")
                nc.vector.tensor_scalar(sign, g, 0.0, 2.0, ALU.is_ge, ALU.mult).then_inc(sign_done, 1)
                dve.wait_ge(sign_done, 1)
                nc.vector.tensor_scalar(sign, sign, -1.0, None, ALU.add).then_inc(sign_done, 1)
                dve.wait_ge(sign_done, 2)
                nc.vector.tensor_tensor(rows, g, sign, ALU.mult).then_inc(size_done, 1)
                dve.wait_ge(size_done, 1)
                nc.vector.scalar_tensor_tensor(out=rows, in0=rows, scalar=0.25, in1=sign, op0=ALU.max,
                                               op1=ALU.mult).then_inc(rows_done, 1)
                dve.wait_ge(mod_done, 2)
                for l in range(2):
                    m = mod_ps[:, l, 0:4 * KC * B].rearrange("p (i k b) -> p i k b", i=4, k=KC)
                    for i in range(4):
                        nc.vector.tensor_scalar(c.mod[:, l, i], m[:, i], 1.0 if i in (CA, CB) else 0.0, None,
                                                ALU.add).then_inc(mod_scales, 1)
                for n, (raw, split) in enumerate(weights):
                    dve.wait_ge(heads_split, n + 1)
                    nc.vector.tensor_tensor(split[:, REST], raw[:], split[:, HEAD].bitcast(F32),
                                            ALU.subtract).then_inc(rests_split, 1)


class Norm:

    def __init__(self, c, ctx, name, eps):
        self.c, self.nc = c, c.nc
        self.stats = c.sb(name + "_stats", [P, NT, 6], ctx=ctx)
        self.moments = c.sb(name + "_moments", [P, NT, 2], ctx=ctx)
        self.eps = eps
        self.shifted = c.sb(name + "_shifted", [P, NT], ctx=ctx)
        self.inv_std = c.sb(name + "_inv_std", [P, NT], ctx=ctx)
        self.stats_done, self.moments_done = c.sem(name + "_stats_done"), c.sem(name + "_moments_done")
        self.shifted_done, self.inv_done = c.sem(name + "_shifted_done"), c.sem(name + "_inv_done")

    def gather(self, tile, tiles=range(NT)):
        for t in tiles:
            last = self.nc.vector.bn_stats(self.stats[:, t, :], tile(t))
        if t == NT - 1:
            last.then_inc(self.stats_done, 1)

    def aggregate(self, dve, b):
        dve.drain()
        for t in range(NT):
            last = self.nc.vector.bn_aggr(self.moments[:, t, :], self.stats[:, t, :])
        last.then_inc(self.moments_done, 1)

    def invert(self, pool, b):
        pool.wait_ge(self.moments_done, b + 1)
        self.nc.gpsimd.tensor_tensor(self.shifted[:], self.moments[:, :, 1], self.eps, ALU.add).then_inc(
            self.shifted_done, 1)
        pool.wait_ge(self.shifted_done, b + 1)
        self.nc.gpsimd.tensor_tensor(self.inv_std[:], self.shifted[:], self.c.neg_half[:, 0:NT], ALU.pow).then_inc(
            self.inv_done, 1)

    def apply(self, dve, b, to, tile, done):
        dve.wait_ge(self.inv_done, b + 1)
        for t in range(NT):
            last = self.nc.vector.tensor_scalar(to[:, t, :], tile(t), self.moments[:, t, 0:1], self.inv_std[:, t:t + 1],
                                                ALU.subtract, ALU.mult)
        last.then_inc(done, 1)


def transposes(pe, c, to, tiles):
    for k in range(KC):
        for t in range(NT):
            last = pe.transpose(to[:, k, t * P:(t + 1) * P], tiles[:, t, k * P:(k + 1) * P], c.ident[:])
    return last


def rows_of(ps, t):
    return ps[:, t // 2, (t % 2) * D:(t % 2 + 1) * D]


def retention_part(c, a, w_ret, w_in, w_out):
    nc = c.nc
    with ExitStack() as ctx:
        def sb(name, shape, dt=F32):
            return c.sb(name, shape, dt, ctx)

        b_ret, ln1_scale, ln1_bias = sb("b_ret", [P, KC]), sb("ln1_scale", [P, KC]), sb("ln1_bias", [P, KC])
        b_in, gate_w = sb("b_in", [P, MC]), sb("gate_w", [P, KC, E])
        ln2_scale, ln2_bias, b_out = sb("ln2_scale", [P, D]), sb("ln2_bias", [P, D]), sb("b_out", [1, D])
        half, eps = sb("half", [P, S]), sb("ln_eps", [P, NT])
        ident_wide = sb("ident_wide", [P, KC, D], F32R)
        ones, b_out_row = sb("ones", [P, P], F32R), sb("b_out_row", [P, D], F32R)
        norm_x, norm_1 = Norm(c, ctx, "norm_x", eps[:]), Norm(c, ctx, "norm_1", eps[:])
        norm_2, norm_next = Norm(c, ctx, "norm_2", eps[:]), Norm(c, ctx, "norm_next", eps[:])
        xn, xn_next = sb("xn", [P, NT, D]), sb("xn_next", [P, NT, D])
        h, h_next = sb("h", [P, KC, S]), sb("h_next", [P, KC, S])
        h0_parts, h1_parts = sb("h0_parts", [P, 2, KC, S], F32R), sb("h1_parts", [P, 2, KC, S], F32R)
        sig, average = sb("sig", [P, KC, S]), sb("average", [P, KC, S])
        G_BUFS = 4
        g = sb("g", [P, G_BUFS, S])
        hidden = sb("hidden", [P, 2, MC, S], F32R)
        gate_scale, gate_bias, y_scaled = sb("gate_scale", [P, D]), sb("gate_bias", [P, D]), sb("y_scaled", [P, NT, D])
        tp_ps = c.psum("tp_ps", 2, ctx)
        ret_ps = c.psum("ret_ps", 2, ctx)
        in_ps = c.psum("in_ps", 2, ctx)
        out_ps = c.psum("out_ps", 2, ctx)

        tables_loaded, tables_set, b_out_head = c.sem("tables_loaded"), c.sem("tables_set"), c.sem("b_out_head")
        xn_done, xT_done, h0_done, h0_split = c.sem("xn_done"), c.sem("xT_done"), c.sem("h0_done"), c.sem("h0_split")
        ret_done, sig_done, average_done = c.sem("ret_done"), c.sem("sig_done"), c.sem("average_done")
        sum_done, sumT_done, n1_done, n1T_done = c.sem("sum_done"), c.sem("sumT_done"), c.sem("n1_done"), c.sem("n1T_done")
        h1_done, h1_split, in_done, g_done = c.sem("h1_done"), c.sem("h1_split"), c.sem("in_done"), c.sem("g_done")
        hidden_split, out_done = c.sem("hidden_split"), c.sem("out_done")
        gate_rows_done, x_biased, scaled_done, x_done = (c.sem("gate_rows_done"), c.sem("x_biased"),
                                                         c.sem("scaled_done"), c.sem("x_done"))
        next_done, nextT_done = c.sem("next_done"), c.sem("nextT_done")
        next_h_done, hT_kept = c.sem("next_h_done"), c.sem("hT_kept")
        logits_done, logits_kept, sums_read = c.sem("logits_done"), c.sem("logits_kept"), c.sem("sums_read")

        COLUMNS = (("b_ret", b_ret), ("ln1_scale", ln1_scale), ("ln1_bias", ln1_bias), ("b_in", b_in))
        ROWS = (("L0_attn_ln2_scale", ln2_scale), ("L0_attn_ln2_bias", ln2_bias))
        N_TABLES = 16 * (len(COLUMNS) + len(ROWS) + 2)
        SET_BY_POOL = 2

        with nc.Block() as block:
            @block.sync
            def _(sp):
                for name, to in COLUMNS:
                    sp.dma_start(to[:], a[name]).then_inc(tables_loaded, 16)
                for name, to in ROWS:
                    sp.dma_start(to[:], a[name].unsqueeze(0).broadcast_to([P, D])).then_inc(tables_loaded, 16)
                sp.dma_start(b_out[:], a["L0_attn_b2"].unsqueeze(0)).then_inc(tables_loaded, 16)
                sp.dma_start(gate_w[:], a["L0_ffn_gate_w"].rearrange("(k p) e -> p k e", p=P)).then_inc(tables_loaded, 16)

            @block.gpsimd
            def _(pool):
                pool.memset(eps[:], LN_EPS)
                pool.memset(half[:], 0.5)
                pool.memset(ident_wide[:].bitcast(F32), 0.0)
                pool.memset(ones[:].bitcast(F32), 1.0)
                pool.memset(b_out_row[:].bitcast(F32), 0.0).then_inc(tables_set, 1)
                pool.wait_ge(tables_set, 1)
                for k in range(KC):
                    last = nc.gpsimd.tensor_copy(ident_wide[:, k, k * P:(k + 1) * P], c.ident[:])
                last.then_inc(tables_set, 1)
                pool.wait_ge(tables_loaded, N_TABLES)

                def keep_hT(b):
                    pool.wait_ge(c.start, 1)
                    pool.wait_ge(next_h_done, b + 1)
                    nc.gpsimd.tensor_copy(c.hT[:, :, b, :], h_next[:]).then_inc(hT_kept, 1)

                def rest_h0(b):
                    pool.wait_ge(h0_done, b + 1)
                    nc.gpsimd.tensor_tensor(h0_parts[:, REST], h[:], h0_parts[:, HEAD].bitcast(F32),
                                            ALU.subtract).then_inc(h0_split, 1)

                def gate_tables(b):
                    pool.wait_ge(c.start, 1)
                    if not (isinstance(b, int) and b == 0):
                        pool.wait_ge(scaled_done, b)
                    nc.gpsimd.tensor_tensor(gate_scale[:], c.gate[:, b, :], ln2_scale[:], ALU.mult)
                    nc.gpsimd.tensor_tensor(gate_bias[:], c.gate[:, b, :], ln2_bias[:], ALU.mult).then_inc(
                        gate_rows_done, 1)
                    pool.wait_ge(c.start, 1)
                    pool.wait_ge(gate_rows_done, b + 1)
                    nc.gpsimd.tensor_tensor(c.x[:, b], c.x[:, b], gate_bias[:].unsqueeze(1).broadcast_to([P, NT, D]),
                                            ALU.add).then_inc(x_biased, 1)

                norm_x.invert(pool, 0)
                rest_h0(0)
                norm_1.invert(pool, 0)
                norm_x.invert(pool, 1)
                rest_h0(1)
                gate_tables(0)
                norm_1.invert(pool, 1)
                with pool.Fori(1, B - 1) as b:
                    norm_2.invert(pool, b - 1)
                    norm_x.invert(pool, b + 1)
                    norm_next.invert(pool, b - 1)
                    rest_h0(b + 1)
                    gate_tables(b)
                    keep_hT(b - 1)
                    norm_1.invert(pool, b + 1)
                norm_2.invert(pool, B - 2)
                norm_next.invert(pool, B - 2)
                gate_tables(B - 1)
                keep_hT(B - 2)
                norm_2.invert(pool, B - 1)
                norm_next.invert(pool, B - 1)
                keep_hT(B - 1)

            @block.tensor
            def _(pe):
                def x_by_feature(b):
                    pe.wait_ge(xn_done, b + 1)
                    transposes(nc.tensor, c, tp_ps, xn).then_inc(xT_done, 1)

                def retention(b):
                    pe.wait_ge(h0_split, b + 1)
                    for m in range(KC):
                        product(nc.tensor, ret_ps[:, m, :],
                                [(lambda i, k=k: w_ret[:, i, k, m * P:(m + 1) * P],
                                  lambda j, k=k: h0_parts[:, j, k, :]) for k in range(KC)]).then_inc(ret_done, 1)

                def sum_by_token(b):
                    pe.wait_ge(sum_done, b + 1)
                    for t in range(NT):
                        for k in range(KC):
                            last = nc.tensor.transpose(rows_of(ret_ps, t)[:, k * P:(k + 1) * P],
                                                       sig[:, k, t * P:(t + 1) * P], c.ident[:])
                    last.then_inc(sumT_done, 1)

                def h1_by_feature(b):
                    pe.wait_ge(n1_done, b + 1)
                    transposes(nc.tensor, c, tp_ps, xn).then_inc(n1T_done, 1)

                def widen(b, ms):
                    for m in ms:
                        if m == 0:
                            pe.wait_ge(h1_split, b + 1)
                        if m >= 2 or not (isinstance(b, int) and b == 0):
                            pe.wait_ge(g_done, MC * b + m - 1)
                        product(nc.tensor, in_ps[:, m % 2, :],
                                [(lambda i, k=k: w_in[:, i, k, m * P:(m + 1) * P],
                                  lambda j, k=k: h1_parts[:, j, k, :]) for k in range(KC)]).then_inc(in_done, 1)

                def bias_and_residual(t):
                    nc.tensor.matmul(rows_of(out_ps, t), ones[:], b_out_row[:], start=True, stop=False)
                    for k in range(KC):
                        for part in (HEAD, REST):
                            nc.tensor.matmul(rows_of(out_ps, t), h1_parts[:, part, k, t * P:(t + 1) * P],
                                             ident_wide[:, k, :], start=False, stop=False)

                def narrow(b, *ts):
                    for t in ts:
                        if t == 0:
                            pe.wait_ge(hidden_split, MC * (b + 1))
                        cols = slice(t * P, (t + 1) * P)
                        to = rows_of(out_ps, t)
                        if t != NT - 1:
                            bias_and_residual(t)
                        for m in range(MC):
                            for n, (i, j) in enumerate(PASSES):
                                last = nc.tensor.matmul(to, hidden[:, i, m, cols], w_out[:, j, m, :], start=False,
                                                        stop=m == MC - 1 and n == 2)
                        last.then_inc(out_done, 1)

                def next_by_feature(b):
                    pe.wait_ge(next_done, b + 1)
                    transposes(nc.tensor, c, ret_ps, xn_next).then_inc(nextT_done, 1)

                def route(b):
                    pe.wait_ge(next_h_done, b + 1)
                    for t in range(NT):
                        for k in range(KC):
                            last = nc.tensor.matmul(tp_ps[:, 0, t * E:(t + 1) * E], h_next[:, k, t * P:(t + 1) * P],
                                                    gate_w[:, k, :], start=k == 0, stop=k == KC - 1)
                    last.then_inc(logits_done, 1)

                def iteration(b, first=False, final=False):
                    widen(b, range(0, 4))
                    if not final:
                        x_by_feature(b + 1)
                    widen(b, range(4, 7))
                    if not first:
                        next_by_feature(b - 1)
                    widen(b, range(7, MC))
                    if not final:
                        if not first:
                            pe.wait_ge(next_h_done, b)
                        retention(b + 1)
                    if not first:
                        route(b - 1)
                    narrow(b, 0)
                    if not final:
                        sum_by_token(b + 1)
                    narrow(b, 1, 2)
                    bias_and_residual(NT - 1)
                    if not final:
                        if not first:
                            pe.wait_ge(logits_kept, b)
                        h1_by_feature(b + 1)
                    narrow(b, 3)

                pe.wait_ge(tables_loaded, N_TABLES)
                pe.wait_ge(tables_set, SET_BY_POOL)
                pe.wait_ge(b_out_head, 2)
                x_by_feature(0)
                retention(0)
                sum_by_token(0)
                h1_by_feature(0)
                iteration(0, first=True)
                with pe.Fori(1, B - 1) as b:
                    iteration(b)
                iteration(B - 1, final=True)
                next_by_feature(B - 1)
                route(B - 1)

            @block.scalar
            def _(act):
                def modulate_x(b):
                    act.wait_ge(c.start, 1)
                    act.wait_ge(xT_done, b + 1)
                    for to in (h, h0_parts[:, HEAD]):
                        for k in range(KC):
                            last = nc.scalar.activation(to[:, k, :], tp_ps[:, k, :], ACT.Identity,
                                                        bias=c.mod[:, 0, SA, k, bass.ds(b, 1)],
                                                        scale=c.mod[:, 0, CA, k, bass.ds(b, 1)])
                    last.then_inc(h0_done, 1)

                def sigmoids(b):
                    for m in range(KC):
                        act.wait_ge(ret_done, KC * b + m + 1)
                        nc.scalar.activation(sig[:, m, :], ret_ps[:, m, :], ACT.Sigmoid,
                                             bias=b_ret[:, m:m + 1]).then_inc(sig_done, 1)

                def scale_h1(b):
                    act.wait_ge(n1T_done, b + 1)
                    for to in (h, h1_parts[:, HEAD]):
                        for k in range(KC):
                            last = nc.scalar.activation(to[:, k, :], tp_ps[:, k, :], ACT.Identity,
                                                        bias=ln1_bias[:, k:k + 1], scale=ln1_scale[:, k:k + 1])
                    last.then_inc(h1_done, 1)

                def gelu(b, ms):
                    for m in ms:
                        act.wait_ge(in_done, MC * b + m + 1)
                        if not (isinstance(b, int) and b == 0 and m < G_BUFS):
                            act.wait_ge(hidden_split, MC * b + m + 1 - G_BUFS)
                        nc.scalar.activation(g[:, m % G_BUFS, :], in_ps[:, m % 2, :], ACT.Gelu_apprx_tanh,
                                             bias=b_in[:, m:m + 1])
                        nc.scalar.activation(hidden[:, HEAD, m, :], in_ps[:, m % 2, :], ACT.Gelu_apprx_tanh,
                                             bias=b_in[:, m:m + 1]).then_inc(g_done, 1)

                def tail(b):
                    act.wait_ge(c.start, 1)
                    act.wait_ge(nextT_done, b + 1)
                    if not (isinstance(b, int) and b == 0):
                        act.wait_ge(hT_kept, b)
                    for k in range(KC):
                        last = nc.scalar.activation(h_next[:, k, :], ret_ps[:, k, :], ACT.Identity,
                                                    bias=c.mod[:, 0, SB, k, bass.ds(b, 1)], scale=c.mod[:, 0, CB, k, bass.ds(b, 1)])
                    last.then_inc(next_h_done, 1)

                def iteration(b, first=False, final=False):
                    gelu(b, range(0, 4))
                    if not final:
                        modulate_x(b + 1)
                    gelu(b, range(4, 7))
                    if not first:
                        tail(b - 1)
                    gelu(b, range(7, MC))
                    if not final:
                        sigmoids(b + 1)
                        scale_h1(b + 1)

                act.wait_ge(tables_loaded, N_TABLES)
                modulate_x(0)
                sigmoids(0)
                scale_h1(0)
                iteration(0, first=True)
                with act.Fori(1, B - 1) as b:
                    iteration(b)
                iteration(B - 1, final=True)
                tail(B - 1)

            @block.vector
            def _(dve):
                def x_tile(b):
                    return lambda t: c.x[:, b, t, :]

                def moments_x(b):
                    b = b if isinstance(b, int) else dve.snap(b)
                    norm_x.gather(x_tile(b))
                    norm_x.aggregate(dve, b)

                def normalise_x(b):
                    norm_x.apply(dve, b, xn, x_tile(b), xn_done)

                def average_and_sum(b):
                    for k in range(KC):
                        dve.wait_ge(sig_done, KC * b + k + 1)
                        nc.vector.tensor_tensor_scan(average[:, k, :], half[:], sig[:, k, :], 0.0, ALU.mult,
                                                     ALU.add).then_inc(average_done, 1)
                    dve.wait_ge(average_done, KC * (b + 1))
                    nc.vector.scalar_tensor_tensor(out=sig[:].rearrange("p k s -> p (k s)"),
                                                   in0=average[:].rearrange("p k s -> p (k s)"), scalar=0.5,
                                                   in1=h[:].rearrange("p k s -> p (k s)"),
                                                   op0=ALU.mult, op1=ALU.add).then_inc(sum_done, 1)

                def normalise_1(b):
                    dve.wait_ge(sumT_done, b + 1)
                    norm_1.gather(lambda t: rows_of(ret_ps, t))
                    norm_1.aggregate(dve, b)
                    norm_1.apply(dve, b, xn, lambda t: rows_of(ret_ps, t), n1_done)

                def rest_h1(b):
                    dve.wait_ge(h1_done, b + 1)
                    nc.vector.tensor_tensor(h1_parts[:, REST], h[:], h1_parts[:, HEAD].bitcast(F32),
                                            ALU.subtract).then_inc(h1_split, 1)

                def rest_hidden(b, ms):
                    for m in ms:
                        dve.wait_ge(g_done, MC * b + m + 1)
                        nc.vector.tensor_tensor(hidden[:, REST, m, :], g[:, m % G_BUFS, :],
                                                hidden[:, HEAD, m, :].bitcast(F32), ALU.subtract).then_inc(hidden_split, 1)

                def moments_2(b, ts):
                    dve.wait_ge(out_done, NT * b + ts[-1] + 1)
                    norm_2.gather(lambda t: rows_of(out_ps, t), ts)
                    if ts[-1] == NT - 1:
                        norm_2.aggregate(dve, b)

                def update_x(b):
                    dve.wait_ge(norm_2.moments_done, b + 1)
                    dve.wait_ge(gate_rows_done, b + 1)
                    for t in range(NT):
                        last = nc.vector.scalar_tensor_tensor(out=y_scaled[:, t, :], in0=rows_of(out_ps, t),
                                                              scalar=norm_2.moments[:, t, 0:1], in1=gate_scale[:],
                                                              op0=ALU.subtract, op1=ALU.mult)
                    last.then_inc(scaled_done, 1)
                    dve.wait_ge(c.start, 1)
                    dve.wait_ge(norm_2.inv_done, b + 1)
                    dve.wait_ge(x_biased, b + 1)
                    dve.wait_ge(scaled_done, b + 1)
                    for t in range(NT):
                        last = nc.vector.scalar_tensor_tensor(out=c.x[:, b, t, :], in0=y_scaled[:, t, :],
                                                              scalar=norm_2.inv_std[:, t:t + 1], in1=c.x[:, b, t, :],
                                                              op0=ALU.mult, op1=ALU.add)
                    last.then_inc(x_done, 1)

                def moments_next(b):
                    dve.wait_ge(c.start, 1)
                    dve.wait_ge(x_done, b + 1)
                    norm_next.gather(x_tile(b))
                    norm_next.aggregate(dve, b)

                def normalise_next(b):
                    norm_next.apply(dve, b, xn_next, x_tile(b), next_done)

                def keep_logits(b):
                    dve.wait_ge(c.start, 1)
                    dve.wait_ge(logits_done, b + 1)
                    nc.vector.tensor_copy(c.logits[:, b], tp_ps[:, 0, 0:NT * E].rearrange("p (t e) -> p t e", t=NT)
                                          ).then_inc(logits_kept, 1)

                def iteration(b, first=False, final=False):
                    if not first:
                        moments_2(b - 1, (2, 3))
                    if not final:
                        moments_x(b + 1)
                    rest_hidden(b, (0,))
                    if not final:
                        normalise_x(b + 1)
                    rest_hidden(b, (1,))
                    if not first:
                        update_x(b - 1)
                    rest_hidden(b, (2, 3))
                    if not first:
                        moments_next(b - 1)
                    rest_hidden(b, (4,))
                    if not first:
                        normalise_next(b - 1)
                    rest_hidden(b, range(5, MC))
                    if not final:
                        average_and_sum(b + 1)
                    if not first:
                        keep_logits(b - 1)
                    if not final:
                        normalise_1(b + 1)
                    moments_2(b, (0, 1))
                    if not final:
                        rest_h1(b + 1)

                dve.wait_ge(tables_loaded, N_TABLES)
                dve.wait_ge(tables_set, SET_BY_POOL)
                nc.vector.tensor_copy(b_out_row[0:1, :], b_out[:]).then_inc(b_out_head, 1)
                dve.wait_ge(b_out_head, 1)
                nc.vector.tensor_tensor(b_out_row[32:33, :], b_out[:], b_out_row[0:1, :].bitcast(F32),
                                        ALU.subtract).then_inc(b_out_head, 1)
                dve.wait_ge(c.x_first, 16)
                moments_x(0)
                normalise_x(0)
                average_and_sum(0)
                normalise_1(0)
                rest_h1(0)
                dve.wait_ge(c.x_rest, 16 * (B - 1))
                iteration(0, first=True)
                with dve.Fori(1, B - 1) as b:
                    iteration(b)
                iteration(B - 1, final=True)
                moments_2(B - 1, (2, 3))
                update_x(B - 1)
                moments_next(B - 1)
                normalise_next(B - 1)
                keep_logits(B - 1)


def split_weights(c, name, weights):
    nc = c.nc
    with ExitStack() as ctx:
        raw = [c.sb(f"{name}_raw_{n}", [P, split.shape[2], split.shape[3]], ctx=ctx) for n, (_, split, _) in enumerate(weights)]
        scales = [c.sb(f"{name}_scale_{n}", [P, split.shape[2]], ctx=ctx) for n, (_, split, _) in enumerate(weights)]
        loaded = [c.sem(f"{name}_loaded_{n}") for n in range(len(weights))]
        scaled, heads_done, rests_done = c.sem(name + "_scaled"), c.sem(name + "_heads"), c.sem(name + "_rests")
        with nc.Block() as block:
            @block.sync
            def _(sp):
                for n, (view, split, scale) in enumerate(weights):
                    if scale is not None:
                        sp.dma_start(scales[n][:], scale).then_inc(loaded[n], 16)
                    sp.dma_start(raw[n][:], view).then_inc(loaded[n], 16)

            @block.vector
            def _(dve):
                for n, (view, split, scale) in enumerate(weights):
                    dve.wait_ge(loaded[n], 16 if scale is None else 32)
                    for k in range(split.shape[2]):
                        last = nc.vector.tensor_scalar(raw[n][:, k, :], raw[n][:, k, :],
                                                       1.0 if scale is None else scales[n][:, k:k + 1], None, ALU.mult)
                    last.then_inc(scaled, 1)
                for n, (view, split, scale) in enumerate(weights):
                    dve.wait_ge(heads_done, n + 1)
                    nc.vector.tensor_tensor(split[:, REST], raw[n][:], split[:, HEAD].bitcast(F32),
                                            ALU.subtract).then_inc(rests_done, 1)

            @block.scalar
            def _(act):
                for n, (view, split, scale) in enumerate(weights):
                    act.wait_ge(scaled, n + 1)
                    nc.scalar.activation(split[:, HEAD], raw[n][:], ACT.Copy).then_inc(heads_done, 1)


def choose(nc, dve, value, better, count, chosen, weight_sum, coef):
    for f in range(E):
        for lo, hi, op in ((0, f, ALU.is_gt), (f + 1, E, ALU.is_ge)):
            if lo < hi:
                nc.vector.tensor_tensor(better[:, :, lo:hi, f], value[:, :, f:f + 1].broadcast_to([P, B * NT, hi - lo]),
                                        value[:, :, lo:hi], op)
    dve.drain()
    nc.vector.tensor_reduce(count, better[:, :, :, :], AX, ALU.add)
    dve.drain()
    nc.vector.tensor_scalar(coef, count, 2.0, None, ALU.is_lt)
    dve.drain()
    nc.vector.tensor_tensor(chosen, coef, value, ALU.mult)
    dve.drain()
    nc.vector.tensor_reduce(weight_sum, chosen, AX, ALU.add)
    dve.drain()


def softmax_router(c):
    nc = c.nc
    N = B * NT
    with ExitStack() as ctx:
        peak, total, inv_total = (c.sb("gate_" + n, [P, N], ctx=ctx) for n in ("peak", "total", "inv_total"))
        shifted, power, gates, count, chosen = (c.sb("gate_" + n, [P, N, E], ctx=ctx)
                                                for n in ("shifted", "power", "values", "count", "chosen"))
        weight_sum, better = c.sb("gate_weight_sum", [P, N], ctx=ctx), c.sb("gate_better", [P, N, E, E], ctx=ctx)
        shifted_done, power_done = c.sem("gate_shifted_done"), c.sem("gate_power_done")
        logits, coef = c.logits[:].rearrange("p b t e -> p (b t) e"), c.coef[:].rearrange("p b t e -> p (b t) e")

        def spread(v):
            return v[:].unsqueeze(2).broadcast_to([P, N, E])

        with nc.Block() as block:
            @block.sync
            def _(sp):
                sp.dma_start(c.gate[:], c.gates_dram[0, 1].unsqueeze(0).broadcast_to([P, B, D])).then_inc(c.constants, 16)

            @block.scalar
            def _(act):
                act.wait_ge(shifted_done, 1)
                nc.scalar.activation(power[:], shifted[:], ACT.Exp).then_inc(power_done, 1)

            @block.vector
            def _(dve):
                nc.vector.memset(better[:], 0.0)
                nc.vector.tensor_reduce(peak[:], logits, AX, ALU.max)
                dve.drain()
                nc.vector.tensor_tensor(shifted[:], logits, spread(peak), ALU.subtract).then_inc(shifted_done, 1)
                dve.wait_ge(power_done, 1)
                nc.vector.tensor_reduce(total[:], power[:], AX, ALU.add)
                dve.drain()
                nc.vector.reciprocal(inv_total[:], total[:])
                dve.drain()
                nc.vector.tensor_tensor(gates[:], power[:], spread(inv_total), ALU.mult)
                dve.drain()
                choose(nc, dve, gates[:], better, count[:], chosen[:], weight_sum[:], coef)
                nc.vector.tensor_tensor(coef, coef, spread(weight_sum), ALU.mult)


def gelu_experts_part(c, a, w_up, w_down):
    nc = c.nc
    with ExitStack() as ctx:
        def sb(name, shape, dt=F32):
            return c.sb("e0_" + name, shape, dt, ctx)

        b_up, b_down, ones, eps = sb("b_up", [P, E]), sb("b_down", [E, D]), sb("ones", [P, 1]), sb("eps", [P, NT])
        norm = Norm(c, ctx, "e0_norm", eps[:])
        h_parts, coef = sb("h_parts", [P, 2, KC, S], F32R), sb("coef", [P, NT, E])
        coefT, acc, y = sb("coefT", [E, S]), sb("acc", [P, NT, D]), sb("y", [P, NT, D])
        g, hidden = sb("g", [P, 2, S]), sb("hidden", [P, 2, 2, S], F32R)
        xn, squares = sb("xn", [P, NT, D]), sb("squares", [P, KC, S])
        tp_ps = c.psum("e0_tp_ps", 2, ctx)
        up_ps = c.psum("e0_up_ps", 2, ctx)
        down_ps = [c.psum(f"e0_down_ps_{n}", 2, ctx) for n in range(2)]
        (tables_loaded, tables_set, head_done, h_split, coef_done, coefT_done, coefT_kept, bias_done, acc_set, up_done,
         g_done, hidden_split, down_done, acc_done, y_done, x_done, xn_done, xT_done, next_done, squares_done, kept) = (
            c.sem("e0_" + n) for n in
            ("tables_loaded tables_set head_done h_split coef_done coefT_done coefT_kept bias_done acc_set up_done "
             "g_done hidden_split down_done acc_done y_done x_done xn_done xT_done next_done squares_done kept").split())

        with nc.Block() as block:
            @block.sync
            def _(sp):
                sp.dma_start(b_up[:], a["e0_b_up"]).then_inc(tables_loaded, 16)
                sp.dma_start(b_down[:], a["L0_ffn_b2"]).then_inc(tables_loaded, 16)

            @block.gpsimd
            def _(pool):
                def take_coef(b):
                    if not (isinstance(b, int) and b == 0):
                        pool.wait_ge(c.start, 1)
                        pool.wait_ge(coefT_done, b)
                    nc.gpsimd.tensor_copy(coef[:], c.coef[:, b]).then_inc(coef_done, 1)

                pool.memset(ones[:], 1.0)
                pool.memset(eps[:], LN_EPS).then_inc(tables_set, 1)
                pool.wait_ge(tables_set, 1)
                take_coef(0)
                with pool.Fori(0, B - 1) as b:
                    take_coef(b + 1)
                    norm.invert(pool, b)
                norm.invert(pool, B - 1)

            @block.tensor
            def _(pe):
                def up(b, e):
                    if e == 0:
                        pe.wait_ge(h_split, b + 1)
                    if e >= 2 or not (isinstance(b, int) and b == 0):
                        pe.wait_ge(g_done, E * b + e - 1)
                    product(nc.tensor, up_ps[:, e % 2, :],
                            [(lambda i, k=k: w_up[:, i, e * KC + k, :],
                              lambda j, k=k: h_parts[:, j, k, :]) for k in range(KC)]).then_inc(up_done, 1)

                def down(b, e):
                    pe.wait_ge(hidden_split, E * b + e + 1)
                    if e >= 2 or not (isinstance(b, int) and b == 0):
                        pe.wait_ge(acc_done, E * b + e - 1)
                    for t in range(NT):
                        last = product(nc.tensor, rows_of(down_ps[e % 2], t),
                                       [(lambda i: hidden[:, i, e % 2, t * P:(t + 1) * P],
                                         lambda j: w_down[:, j, e, :])])
                    last.then_inc(down_done, 1)

                def coef_by_expert(b):
                    pe.wait_ge(coef_done, b + 1)
                    for t in range(NT):
                        last = nc.tensor.transpose(tp_ps[0:E, 0, t * P:(t + 1) * P], coef[:, t, :], c.ident[:])
                    last.then_inc(coefT_done, 1)

                def biases(b):
                    pe.wait_ge(coefT_kept, b + 1)
                    for t in range(NT):
                        last = nc.tensor.matmul(rows_of(tp_ps, t), coefT[:, t * P:(t + 1) * P], b_down[:], start=True,
                                                stop=True)
                    last.then_inc(bias_done, 1)

                def next_by_feature(b):
                    pe.wait_ge(xn_done, b + 1)
                    transposes(nc.tensor, c, tp_ps, xn).then_inc(xT_done, 1)

                def sum_squares(b):
                    pe.wait_ge(next_done, b + 1)
                    for t in range(NT):
                        for k in range(KC):
                            last = nc.tensor.matmul(tp_ps[:, 0, t:t + 1], squares[:, k, t * P:(t + 1) * P], ones[:],
                                                    start=k == 0, stop=k == KC - 1)
                    last.then_inc(squares_done, 1)

                def iteration(b, first=False, final=False):
                    for e in range(E):
                        if e + 1 < E:
                            up(b, e + 1)
                        if e == 4 and not first:
                            next_by_feature(b - 1)
                        down(b, e)
                        if e == 6 and not first:
                            sum_squares(b - 1)
                    if not final:
                        if not first:
                            pe.wait_ge(kept, b)
                        coef_by_expert(b + 1)
                        up(b + 1, 0)
                        biases(b + 1)

                pe.wait_ge(tables_loaded, 32)
                pe.wait_ge(tables_set, 1)
                coef_by_expert(0)
                up(0, 0)
                biases(0)
                iteration(0, first=True)
                with pe.Fori(1, B - 1) as b:
                    iteration(b)
                iteration(B - 1, final=True)
                next_by_feature(B - 1)
                sum_squares(B - 1)

            @block.scalar
            def _(act):
                def head_of_h(b):
                    if not (isinstance(b, int) and b == 0):
                        act.wait_ge(c.start, 1)
                        act.wait_ge(up_done, E * b)
                    nc.scalar.activation(h_parts[:, HEAD], c.hT[:, :, b, :], ACT.Identity).then_inc(head_done, 1)

                def keep_coefT(b):
                    act.wait_ge(coefT_done, b + 1)
                    if not (isinstance(b, int) and b == 0):
                        act.wait_ge(bias_done, b)
                    nc.scalar.activation(coefT[:], tp_ps[0:E, 0, :], ACT.Identity).then_inc(coefT_kept, 1)

                def gelu(b, e):
                    act.wait_ge(up_done, E * b + e + 1)
                    if e >= 2 or not (isinstance(b, int) and b == 0):
                        act.wait_ge(down_done, E * b + e - 1)
                    nc.scalar.activation(g[:, e % 2, :], up_ps[:, e % 2, :], ACT.Gelu, bias=b_up[:, e:e + 1])
                    nc.scalar.activation(hidden[:, HEAD, e % 2, :], up_ps[:, e % 2, :], ACT.Gelu,
                                         bias=b_up[:, e:e + 1]).then_inc(g_done, 1)

                def set_acc(b, first):
                    act.wait_ge(bias_done, b + 1)
                    if not first:
                        act.wait_ge(y_done, b)
                    nc.scalar.activation(acc[:].rearrange("p t d -> p (t d)"), tp_ps[:].rearrange("p n s -> p (n s)"),
                                         ACT.Identity).then_inc(acc_set, 1)

                def modulate(b, k):
                    act.wait_ge(c.start, 1)
                    act.wait_ge(xT_done, b + 1)
                    shift, scale = c.mod[:, 1, SA, k, bass.ds(b, 1)], c.mod[:, 1, CA, k, bass.ds(b, 1)]
                    nc.scalar.activation(c.hT[:, k, b, :], tp_ps[:, k, :], ACT.Identity, bias=shift, scale=scale)
                    last = nc.scalar.activation(squares[:, k, :], tp_ps[:, k, :], ACT.Square, bias=shift, scale=scale)
                    if k == KC - 1:
                        last.then_inc(next_done, 1)

                def iteration(b, first=False, final=False):
                    for e in range(E):
                        gelu(b, e)
                        if e == 0:
                            set_acc(b, first)
                        if e in (5, 6) and not first:
                            modulate(b - 1, e - 5)
                    if not final:
                        head_of_h(b + 1)
                        keep_coefT(b + 1)

                act.wait_ge(tables_loaded, 32)
                head_of_h(0)
                keep_coefT(0)
                iteration(0, first=True)
                with act.Fori(1, B - 1) as b:
                    iteration(b)
                iteration(B - 1, final=True)
                for k in range(KC):
                    modulate(B - 1, k)

            @block.vector
            def _(dve):
                def rest_of_h(b):
                    dve.wait_ge(head_done, b + 1)
                    nc.vector.tensor_tensor(h_parts[:, REST], c.hT[:, :, b, :], h_parts[:, HEAD].bitcast(F32),
                                            ALU.subtract).then_inc(h_split, 1)

                def rest_hidden(b, e):
                    dve.wait_ge(g_done, E * b + e + 1)
                    nc.vector.tensor_tensor(hidden[:, REST, e % 2, :], g[:, e % 2, :],
                                            hidden[:, HEAD, e % 2, :].bitcast(F32), ALU.subtract).then_inc(hidden_split, 1)

                def accumulate(b, e):
                    if e == 0:
                        dve.wait_ge(acc_set, b + 1)
                    else:
                        dve.wait_ge(acc_done, E * b + e)
                    dve.wait_ge(down_done, E * b + e + 1)
                    for t in range(NT):
                        last = nc.vector.scalar_tensor_tensor(out=acc[:, t, :], in0=rows_of(down_ps[e % 2], t),
                                                              scalar=c.coef[:, b, t, e:e + 1],
                                                              in1=acc[:, t, :],
                                                              op0=ALU.mult, op1=ALU.add)
                    last.then_inc(acc_done, 1)

                def gate_rows(b):
                    dve.wait_ge(acc_done, E * (b + 1))
                    nc.vector.tensor_tensor(y[:], acc[:], c.gate[:, b, :].unsqueeze(1).broadcast_to([P, NT, D]),
                                            ALU.mult).then_inc(y_done, 1)

                def update_x(b):
                    dve.wait_ge(c.start, 1)
                    dve.wait_ge(y_done, b + 1)
                    nc.vector.tensor_tensor(c.x[:, b], c.x[:, b], y[:], ALU.add).then_inc(x_done, 1)

                def moments(b):
                    dve.wait_ge(c.start, 1)
                    dve.wait_ge(x_done, b + 1)
                    norm.gather(lambda t: c.x[:, b, t, :])
                    norm.aggregate(dve, b)

                def normalise(b):
                    norm.apply(dve, b, xn, lambda t: c.x[:, b, t, :], xn_done)

                def keep_sums(b):
                    dve.wait_ge(c.start, 1)
                    dve.wait_ge(squares_done, b + 1)
                    nc.vector.tensor_copy(c.square_sum[:, b], tp_ps[:, 0, 0:NT]).then_inc(kept, 1)

                TAIL = {0: update_x, 1: moments, 2: normalise, 6: keep_sums}

                def iteration(b, first=False, final=False):
                    rest_hidden(b, 0)
                    for e in range(E):
                        if e + 1 < E:
                            rest_hidden(b, e + 1)
                        if e == E - 2 and not final:
                            rest_of_h(b + 1)
                        accumulate(b, e)
                        if e in TAIL and not first:
                            TAIL[e](b - 1)
                    gate_rows(b)

                dve.wait_ge(c.constants, 32)
                rest_of_h(0)
                iteration(0, first=True)
                with dve.Fori(1, B - 1) as b:
                    iteration(b)
                iteration(B - 1, final=True)
                update_x(B - 1)
                moments(B - 1)
                normalise(B - 1)
                keep_sums(B - 1)


def attention_part(c, a, w_qk, w_v, w_o):
    nc = c.nc
    PAIRS = H // 2
    VW = 3 * HD + 1
    with ExitStack() as ctx:
        def sb(name, shape, dt=F32):
            return c.sb("at_" + name, shape, dt, ctx)

        qk_bias, v_bias, o_bias = sb("qk_bias", [P, 2 * D]), sb("v_bias", [P, D]), sb("o_bias", [P, D])
        cos, sin, router_w = sb("cos", [P, NT, HD]), sb("sin", [P, NT, HD]), sb("router_w", [P, KC, E])
        eps, rms_eps = sb("eps", [P, NT]), sb("rms_eps", [P, B * NT])
        norm = Norm(c, ctx, "at_norm", eps[:])
        mean_square, inv_rms = sb("mean_square", [P, B * NT]), sb("inv_rms", [P, B, NT])
        h_parts = sb("h_parts", [P, 2, KC, S], F32R)
        qk, turned, rotated = sb("qk", [P, 2, 2 * D]), sb("turned", [P, 2, 2 * D]), sb("rotated", [P, 2, 2 * D])
        wide = sb("wide", [P, 2, 4 * S])
        qkT = sb("qkT", [P, 2, PAIRS, S], F32R)
        v = sb("v", [P, NT, D])
        v_parts = sb("v_parts", [P, NT, H, VW], BF16)
        sig_head_mem, sig_rest_mem = sb("sig_head", [P, 2 * NT * D]), sb("sig_rest", [P, 2 * NT * D])
        sig_head = sig_head_mem[:].bitcast(F16).rearrange("p (u t s) -> p u t s", u=2, t=NT)
        sig_rest = sig_rest_mem[:].bitcast(F16).rearrange("p (u t s) -> p u t s", u=2, t=NT)
        v_left = sig_head_mem[:, 0:NT * D].rearrange("p (t d) -> p t d", t=NT)
        gated_rows = sig_rest_mem[:, 0:NT * D].rearrange("p (t d) -> p t d", t=NT)
        h = sig_rest_mem[:, NT * D:].rearrange("p (k s) -> p k s", k=KC)
        o_sum, denom, inv_denom = sb("o_sum", [P, 2, 2, NT, HD]), sb("denom", [P, 2, 2 * NT]), sb("inv_denom", [P, 2, 2 * NT])
        o_parts = sb("o_parts", [P, 2, KC, S], F32R)
        rows, gate_bias = sb("rows", [P, NT, D]), sb("gate_bias", [P, D])
        a_ps = c.psum("at_a_ps", 2, ctx)
        sc_ps = c.psum("at_sc_ps", 4, ctx)
        o_ps = c.psum("at_o_ps", 2, ctx)
        (tables_loaded, tables_set, ms_done, inv_rms_done, head_done, h_split, qk_done, v_done, qk_scaled, v_kept,
         cos_done, rot_done, sin_done, qk_head_done, qk_split, qkT_done, qkT_kept, v1_done, v_split, score_done, sig_done, sig_head_done,
         sig_split, av_done, sum_done, inv_done, heads_done, oT_done, o_head_done, o_split, proj_done, gated,
         x_biased, x_done, xn_done, xT_done, next_done, hT_kept, logits_done, logits_kept, gb_done) = (
            c.sem("at_" + n) for n in
            ("tables_loaded tables_set ms_done inv_rms_done head_done h_split qk_done v_done qk_scaled v_kept "
             "cos_done rot_done sin_done qk_head_done qk_split qkT_done qkT_kept v1_done v_split score_done sig_done sig_head_done "
             "sig_split av_done sum_done inv_done heads_done oT_done o_head_done o_split proj_done gated "
             "x_biased x_done xn_done xT_done next_done hT_kept logits_done logits_kept gb_done").split())
        N_TABLES = 16 * 6

        def by_head(t):
            return wide[:, t % 2, :].rearrange("p (i h c d) -> p i h c d", i=2, h=H, c=4)

        def heads_of(v):
            return v.rearrange("p (h d) -> p h d", d=HD)

        with nc.Block() as block:
            @block.sync
            def _(sp):
                for name, to, n in (("qk_bias", qk_bias, 2 * D), ("L1_attn_v_b", v_bias, D), ("L1_attn_o_b", o_bias, D)):
                    sp.dma_start(to[:], a[name].unsqueeze(0).broadcast_to([P, n])).then_inc(tables_loaded, 16)
                sp.dma_start(cos[:], a["cos"]).then_inc(tables_loaded, 16)
                sp.dma_start(sin[:], a["sin"]).then_inc(tables_loaded, 16)
                sp.dma_start(router_w[:], a["router_w"].rearrange("(k p) e -> p k e", p=P)).then_inc(tables_loaded, 16)
                sp.dma_start(c.gate[:], c.gates_dram[1, 0].unsqueeze(0).broadcast_to([P, B, D])).then_inc(c.constants, 16)

            @block.gpsimd
            def _(pool):
                vh = v[:].rearrange("p t (h d) -> p (t h) d", d=HD)
                left = v_left.rearrange("p t (h d) -> p (t h) d", d=HD)
                v_sources = (vh, left, left)

                def v_part(part):
                    return v_parts[:, :, :, part * HD:(part + 1) * HD].rearrange("p t h d -> p (t h) d")

                def bias_x(b):
                    nc.gpsimd.tensor_tensor(gate_bias[:], c.gate[:, b, :], o_bias[:], ALU.mult).then_inc(gb_done, 1)
                    pool.wait_ge(c.start, 1)
                    pool.wait_ge(gb_done, b + 1)
                    nc.gpsimd.tensor_tensor(c.x[:, b], c.x[:, b], gate_bias[:].unsqueeze(1).broadcast_to([P, NT, D]),
                                            ALU.add).then_inc(x_biased, 1)

                def times_cos(b, t):
                    pool.wait_ge(qk_scaled, NT * b + t + 1)
                    nc.gpsimd.tensor_tensor(heads_of(rotated[:, t % 2, :]), heads_of(qk[:, t % 2, :]),
                                            cos[:, t, :].unsqueeze(1).broadcast_to([P, 2 * H, HD]),
                                            ALU.mult).then_inc(cos_done, 1)

                def keep_v_part(b, part):
                    if part == 0:
                        pool.wait_ge(v_kept, 2 * (b + 1))
                        if not (isinstance(b, int) and b == 0):
                            pool.wait_ge(av_done, H * b)
                    else:
                        pool.wait_ge(v1_done, 2 * b + part)
                    pool.sem_inc(c.passed, 1)
                    nc.gpsimd.tensor_copy(v_part(part), v_sources[part]).then_inc(v_split, 1)

                def left_of_v(b, part):
                    pool.wait_ge(v_split, 3 * b + part + 1)
                    nc.gpsimd.tensor_tensor(left, v_sources[part], v_part(part), ALU.subtract).then_inc(v1_done, 1)

                def sigmoid_heads(b, n):
                    for j in range(2):
                        if j == 0 and n == 0:
                            pool.wait_ge(v_split, 3 * (b + 1))
                        if j == 0 and n >= 2:
                            pool.wait_ge(av_done, H * b + n - 1)
                        pool.wait_ge(sig_done, 2 * (H * b + n) + j + 1)
                        pool.sem_inc(c.passed, 1)
                        nc.gpsimd.tensor_scalar(sig_head[:, n % 2, 2 * j:2 * j + 2].rearrange("p t s -> p (t s)"),
                                                wide[:, n % 2, 2 * j * S:(2 * j + 2) * S],
                                                SIG_SCALE, 1.0, ALU.mult, ALU.mult).then_inc(sig_head_done, 1)

                def iteration(b, after):
                    for n in range(H):
                        sigmoid_heads(b, n)
                        if n == 6:
                            bias_x(b)
                        if after is not None and n in (10, 11):
                            times_cos(after, n - 10)
                    if after is not None:
                        keep_v_part(after, 0)
                        left_of_v(after, 0)
                        times_cos(after, 2)
                        keep_v_part(after, 1)
                        times_cos(after, 3)
                        left_of_v(after, 1)
                    norm.invert(pool, b)
                    if after is not None:
                        keep_v_part(after, 2)

                pool.memset(eps[:], LN_EPS)
                pool.memset(v_parts[:, :, :, VW - 1], 1.0).then_inc(tables_set, 1)
                pool.wait_ge(ms_done, 1)
                nc.gpsimd.tensor_tensor(inv_rms[:].rearrange("p b t -> p (b t)"), mean_square[:], c.neg_half[:],
                                        ALU.pow).then_inc(inv_rms_done, 1)
                pool.wait_ge(tables_loaded, N_TABLES)
                pool.wait_ge(c.constants, 48)
                pool.wait_ge(tables_set, 1)
                for t in range(NT):
                    times_cos(0, t)
                for part in range(3):
                    keep_v_part(0, part)
                    if part < 2:
                        left_of_v(0, part)
                with pool.Fori(0, B - 1) as b:
                    iteration(b, b + 1)
                iteration(B - 1, None)

            @block.tensor
            def _(pe):
                def values(b, t):
                    if t == 0:
                        pe.wait_ge(h_split, b + 1)
                    last = product(nc.tensor, rows_of(a_ps, t),
                                   [(lambda i, k=k: h_parts[:, i, k, t * P:(t + 1) * P], lambda j, k=k: w_v[:, j, k, :])
                                    for k in range(KC)])
                    if t % 2:
                        last.then_inc(v_done, 1)

                def queries_keys(b, t):
                    if t < 2:
                        pe.wait_ge(v_kept, 2 * b + t + 1)
                    product(nc.tensor, a_ps[:, t % 2, :],
                            [(lambda i, k=k: h_parts[:, i, k, t * P:(t + 1) * P], lambda j, k=k: w_qk[:, j, k, :])
                             for k in range(KC)]).then_inc(qk_done, 1)

                def by_feature(b, t, i):
                    if i == 1:
                        pe.wait_ge(qk_split, NT * b + t + 1)
                        if t:
                            pe.wait_ge(qkT_kept, NT * b + t)
                    for pair in range(PAIRS):
                        n = i * PAIRS + pair
                        last = nc.tensor.transpose(sc_ps[:, n // 4, (n % 4) * P:(n % 4 + 1) * P],
                                                   wide[:, t % 2, n * P:(n + 1) * P], c.ident[:])
                    if i == 0:
                        last.then_inc(qkT_done, 1)

                def scores(b, n):
                    base, pair = 64 * (n % 2), n // 2
                    if n == 0:
                        pe.wait_ge(qkT_kept, NT * (b + 1))
                    for j in range(2):
                        if n >= 1:
                            pe.wait_ge(sig_done, 2 * (H * b + n) + j - 1)
                        for k in (2 * j, 2 * j + 1):
                            last = nc.tensor.matmul(sc_ps[:, k, :], qkT[base:base + 64, 1, pair, k * P:(k + 1) * P],
                                                    qkT[base:base + 64, 0, pair, :], start=True, stop=True)
                        last.then_inc(score_done, 1)

                def attend(b, n):
                    if n == 0:
                        pe.wait_ge(v_split, 3 * (b + 1))
                    pe.wait_ge(sig_split, 2 * (H * b + n + 1))
                    if n % 2 == 0 and n >= 4:
                        pe.wait_ge(heads_done, PAIRS * b + n // 2 - 1)
                    for t in range(NT):
                        at = (n % 2) * 256 + t * 64
                        for k in range(NT):
                            for part in (sig_head, sig_rest):
                                last = nc.tensor.matmul(o_ps[:, (n // 2) % 2, at:at + VW],
                                                        part[:, n % 2, k, t * P:(t + 1) * P], v_parts[:, k, n, :],
                                                        start=k == 0 and part is sig_head,
                                                        stop=k == NT - 1 and part is sig_rest)
                    last.then_inc(av_done, 1)

                def output_by_feature(b):
                    pe.wait_ge(heads_done, PAIRS * (b + 1))
                    transposes(nc.tensor, c, sc_ps, rows).then_inc(oT_done, 1)

                def project(b):
                    for t in range(NT):
                        last = product(nc.tensor, rows_of(o_ps, t),
                                       [(lambda i, k=k: o_parts[:, i, k, t * P:(t + 1) * P],
                                         lambda j, k=k: w_o[:, j, k, :]) for k in range(KC)])
                    last.then_inc(proj_done, 1)

                def next_by_feature(b):
                    pe.wait_ge(xn_done, b + 1)
                    transposes(nc.tensor, c, o_ps, rows).then_inc(xT_done, 1)

                def route(b):
                    pe.wait_ge(next_done, b + 1)
                    for t in range(NT):
                        for k in range(KC):
                            last = nc.tensor.matmul(o_ps[:, 0, t * E:(t + 1) * E], h[:, k, t * P:(t + 1) * P],
                                                    router_w[:, k, :], start=k == 0, stop=k == KC - 1)
                    last.then_inc(logits_done, 1)

                def early(b, n):
                    if 2 <= n < 6:
                        values(b, n - 2)
                    elif n in (7, 8):
                        queries_keys(b, n - 7)

                def iteration(b, after):
                    for n in range(H):
                        if n + 2 < H:
                            scores(b, n + 2)
                        attend(b, n)
                        if after is not None:
                            early(after, n)
                    if after is None:
                        output_by_feature(b)
                        pe.wait_ge(o_split, b + 1)
                        project(b)
                        next_by_feature(b)
                        route(b)
                        return
                    by_feature(after, 0, 1)
                    output_by_feature(b)
                    queries_keys(after, 2)
                    pe.wait_ge(o_split, b + 1)
                    by_feature(after, 0, 0)
                    project(b)
                    by_feature(after, 1, 1)
                    by_feature(after, 1, 0)
                    queries_keys(after, 3)
                    for t in (2, 3):
                        by_feature(after, t, 1)
                        by_feature(after, t, 0)
                    next_by_feature(b)
                    scores(after, 0)
                    route(b)
                    scores(after, 1)
                    pe.wait_ge(logits_kept, b + 1)

                pe.wait_ge(tables_loaded, N_TABLES)
                pe.wait_ge(tables_set, 1)
                for t in range(NT):
                    values(0, t)
                for t in range(NT):
                    if t >= 2:
                        by_feature(0, t - 2, 1)
                        by_feature(0, t - 2, 0)
                    queries_keys(0, t)
                for t in (2, 3):
                    by_feature(0, t, 1)
                    by_feature(0, t, 0)
                scores(0, 0)
                scores(0, 1)
                with pe.Fori(0, B - 1) as b:
                    iteration(b, b + 1)
                iteration(B - 1, None)

            @block.scalar
            def _(act):
                def head_of_h(b):
                    if not (isinstance(b, int) and b == 0):
                        act.wait_ge(c.start, 1)
                        act.wait_ge(qk_done, NT * b)
                    nc.scalar.activation(h_parts[:, HEAD], c.hT[:, :, b, :], ACT.Copy).then_inc(head_done, 1)

                def queries_keys_heads(b, t):
                    act.wait_ge(rot_done, NT * b + t + 1)
                    if t >= 2:
                        act.wait_ge(qkT_done, NT * b + t - 1)
                    elif not (isinstance(b, int) and b == 0):
                        act.wait_ge(sig_split, 2 * (H * b - 1 + t))
                    src = rotated[:, t % 2, :].rearrange("p (i h d) -> p i h d", i=2, d=HD)
                    to = by_head(t).bitcast(F32R)
                    nc.scalar.activation(to[:, 0, :, 0:3:2, :], src[:, 0].unsqueeze(2).broadcast_to([P, H, 2, HD]),
                                         ACT.Copy)
                    nc.scalar.activation(to[:, 1, :, 0:2, :], src[:, 1].unsqueeze(2).broadcast_to([P, H, 2, HD]),
                                         ACT.Copy).then_inc(qk_head_done, 1)

                def keep_by_feature(b, t):
                    act.wait_ge(qkT_done, NT * b + t + 1)
                    for n in range(4):
                        last = nc.scalar.activation(
                            qkT[:, n // 2, (n % 2) * 4:(n % 2) * 4 + 4, t * P:(t + 1) * P],
                            sc_ps[:, n, :].rearrange("p (g s) -> p g s", g=4), ACT.Copy)
                    last.then_inc(qkT_kept, 1)

                def sigmoids(b, n):
                    for j in range(2):
                        if n >= 2:
                            act.wait_ge(sig_split, 2 * (H * b + n - 2) + j + 1)
                        act.wait_ge(score_done, 2 * (H * b + n) + j + 1)
                        nc.scalar.activation(wide[:, n % 2, j * 2 * S:(j + 1) * 2 * S],
                                             sc_ps[:, 2 * j:2 * j + 2, :].rearrange("p n s -> p (n s)"),
                                             ACT.Sigmoid, scale=float(HD) ** -0.5).then_inc(sig_done, 1)

                def output_head(b):
                    act.wait_ge(oT_done, b + 1)
                    nc.scalar.activation(o_parts[:, HEAD], sc_ps[:, 0:KC, :], ACT.Copy).then_inc(o_head_done, 1)

                def modulate(b):
                    act.wait_ge(c.start, 1)
                    act.wait_ge(xT_done, b + 1)
                    for k in range(KC):
                        last = nc.scalar.activation(h[:, k, :], o_ps[:, k, :], ACT.Identity,
                                                    bias=c.mod[:, 1, SB, k, bass.ds(b, 1)],
                                                    scale=c.mod[:, 1, CB, k, bass.ds(b, 1)])
                    last.then_inc(next_done, 1)

                def iteration(b, after):
                    for n in range(H):
                        sigmoids(b, n)
                        if after is not None and n == 1:
                            head_of_h(after)
                    if after is not None:
                        queries_keys_heads(after, 0)
                    output_head(b)
                    if after is not None:
                        queries_keys_heads(after, 1)
                        keep_by_feature(after, 0)
                        queries_keys_heads(after, 2)
                        keep_by_feature(after, 1)
                        queries_keys_heads(after, 3)
                        keep_by_feature(after, 2)
                        keep_by_feature(after, 3)
                    modulate(b)

                head_of_h(0)
                for t in range(NT):
                    queries_keys_heads(0, t)
                    keep_by_feature(0, t)
                with act.Fori(0, B - 1) as b:
                    iteration(b, b + 1)
                iteration(B - 1, None)

            @block.vector
            def _(dve):
                def rest_of_h(b):
                    dve.wait_ge(head_done, b + 1)
                    nc.vector.tensor_tensor(h_parts[:, REST], c.hT[:, :, b, :], h_parts[:, HEAD].bitcast(F32),
                                            ALU.subtract).then_inc(h_split, 1)

                def rotate(b, t):
                    dve.wait_ge(c.start, 1)
                    dve.wait_ge(qk_done, NT * b + t + 1)
                    buf = t % 2
                    nc.vector.scalar_tensor_tensor(out=qk[:, buf, :], in0=a_ps[:, buf, :],
                                                   scalar=inv_rms[:, b, t:t + 1], in1=qk_bias[:], op0=ALU.mult,
                                                   op1=ALU.add).then_inc(qk_scaled, 1)
                    dve.wait_ge(qk_scaled, NT * b + t + 1)
                    src = qk[:, buf, :].rearrange("p (h d two) -> p h d two", two=2, d=HD // 2)
                    to = turned[:, buf, :].rearrange("p (h d two) -> p h d two", two=2, d=HD // 2)
                    sines = sin[:, t, :].rearrange("p (d two) -> p d two", two=2)
                    for i in range(2):
                        last = nc.vector.tensor_tensor(to[:, :, :, i], src[:, :, :, 1 - i],
                                                       sines[:, :, i].unsqueeze(1).broadcast_to([P, 2 * H, HD // 2]),
                                                       ALU.mult)
                    last.then_inc(sin_done, 1)

                def add_turned(b, t):
                    buf = t % 2
                    dve.wait_ge(sin_done, NT * b + t + 1)
                    dve.wait_ge(cos_done, NT * b + t + 1)
                    nc.vector.tensor_tensor(rotated[:, buf, :], rotated[:, buf, :], turned[:, buf, :],
                                            ALU.add).then_inc(rot_done, 1)

                def keep_values(b, half):
                    dve.wait_ge(v_done, 2 * b + half + 1)
                    nc.vector.tensor_tensor(v[:, 2 * half:2 * half + 2, :], a_ps[:, half, :].rearrange("p (t d) -> p t d", t=2),
                                            v_bias[:].unsqueeze(1).broadcast_to([P, 2, D]), ALU.add).then_inc(v_kept, 1)

                def rests(b, t):
                    dve.wait_ge(qk_head_done, NT * b + t + 1)
                    src = rotated[:, t % 2, :].rearrange("p (i h d) -> p i h d", i=2, d=HD)
                    to, of = by_head(t).bitcast(F32R), by_head(t)
                    nc.vector.tensor_tensor(to[:, 0, :, 1:4:2, :], src[:, 0].unsqueeze(2).broadcast_to([P, H, 2, HD]),
                                            of[:, 0, :, 0:3:2, :], ALU.subtract)
                    nc.vector.tensor_tensor(to[:, 1, :, 2:4, :], src[:, 1].unsqueeze(2).broadcast_to([P, H, 2, HD]),
                                            of[:, 1, :, 0:2, :], ALU.subtract).then_inc(qk_split, 1)

                def sigmoid_rests(b, n):
                    for j in range(2):
                        dve.wait_ge(sig_head_done, 2 * (H * b + n) + j + 1)
                        nc.vector.scalar_tensor_tensor(out=sig_rest[:, n % 2, 2 * j:2 * j + 2].rearrange("p t s -> p (t s)"),
                                                       in0=wide[:, n % 2, 2 * j * S:(2 * j + 2) * S], scalar=SIG_SCALE,
                                                       in1=sig_head[:, n % 2, 2 * j:2 * j + 2].rearrange("p t s -> p (t s)"),
                                                       op0=ALU.mult, op1=ALU.subtract).then_inc(sig_split, 1)

                def sum_parts(b, pair):
                    dve.wait_ge(av_done, H * b + 2 * pair + 2)
                    got = o_ps[:, pair % 2, :].rearrange("p (n w) -> p n w", w=64)
                    buf = pair % 2
                    nc.vector.tensor_reduce(o_sum[:, buf].rearrange("p n t d -> p (n t) d"),
                                            got[:, :, 0:3 * HD].rearrange("p n (c d) -> p n d c", c=3), AX, ALU.add)
                    nc.vector.tensor_scalar(denom[:, buf, :], got[:, :, 3 * HD], SUM_EPS * SIG_SCALE, None,
                                            ALU.add).then_inc(sum_done, 1)
                    dve.wait_ge(sum_done, PAIRS * b + pair + 1)
                    nc.vector.reciprocal(inv_denom[:, buf, :], denom[:, buf, :]).then_inc(inv_done, 1)
                    dve.wait_ge(inv_done, PAIRS * b + pair + 1)
                    to = rows[:, :, 2 * pair * HD:(2 * pair + 2) * HD].rearrange("p t (n d) -> p n t d", n=2)
                    for n in range(2):
                        last = nc.vector.tensor_tensor(to[:, n], o_sum[:, buf, n],
                                                       inv_denom[:, buf, n * NT:(n + 1) * NT].unsqueeze(2).broadcast_to(
                                                           [P, NT, HD]), ALU.mult)
                    last.then_inc(heads_done, 1)

                def output_rest(b):
                    dve.wait_ge(o_head_done, b + 1)
                    nc.vector.tensor_tensor(o_parts[:, REST], sc_ps[:, 0:KC, :], o_parts[:, HEAD].bitcast(F32),
                                            ALU.subtract).then_inc(o_split, 1)

                def gate_rows(b):
                    dve.wait_ge(proj_done, b + 1)
                    nc.vector.tensor_tensor(gated_rows, o_ps[:].rearrange("p n (t d) -> p (n t) d", d=D),
                                            c.gate[:, b, :].unsqueeze(1).broadcast_to([P, NT, D]),
                                            ALU.mult).then_inc(gated, 1)

                def update_x(b):
                    dve.wait_ge(c.start, 1)
                    dve.wait_ge(gated, b + 1)
                    dve.wait_ge(x_biased, b + 1)
                    nc.vector.tensor_tensor(c.x[:, b], c.x[:, b], gated_rows, ALU.add).then_inc(x_done, 1)
                    dve.wait_ge(c.start, 1)
                    dve.wait_ge(x_done, b + 1)
                    norm.gather(lambda t: c.x[:, b, t, :])
                    norm.aggregate(dve, b)

                def normalise(b):
                    norm.apply(dve, b, rows, lambda t: c.x[:, b, t, :], xn_done)

                def keep_hT(b):
                    dve.wait_ge(c.start, 1)
                    dve.wait_ge(next_done, b + 1)
                    nc.vector.tensor_copy(c.hT[:, :, b, :], h).then_inc(hT_kept, 1)

                def keep_logits(b):
                    dve.wait_ge(c.start, 1)
                    dve.wait_ge(logits_done, b + 1)
                    nc.vector.tensor_copy(c.logits[:, b], o_ps[:, 0, 0:NT * E].rearrange("p (t e) -> p t e", t=NT)
                                          ).then_inc(logits_kept, 1)

                def early(b, n):
                    if n == 1:
                        rest_of_h(b)
                    elif n in (4, 6):
                        keep_values(b, (n - 4) // 2)
                    elif n in (9, 10):
                        rotate(b, n - 9)
                    elif n in (12, 13):
                        add_turned(b, n - 12)

                def iteration(b, after):
                    for n in range(H):
                        sigmoid_rests(b, n)
                        if n % 2 == 1 and n >= 3:
                            sum_parts(b, n // 2 - 1)
                        if after is not None:
                            early(after, n)
                    if after is not None:
                        rests(after, 0)
                    sum_parts(b, PAIRS - 1)
                    if after is None:
                        output_rest(b)
                        gate_rows(b)
                        update_x(b)
                        normalise(b)
                        keep_hT(b)
                        keep_logits(b)
                        return
                    output_rest(b)
                    rests(after, 1)
                    rotate(after, 2)
                    add_turned(after, 2)
                    gate_rows(b)
                    rests(after, 2)
                    rotate(after, 3)
                    add_turned(after, 3)
                    update_x(b)
                    rests(after, 3)
                    normalise(b)
                    keep_hT(b)
                    keep_logits(b)
                    dve.wait_ge(hT_kept, b + 1)

                nc.vector.tensor_scalar(mean_square[:], c.square_sum[:].rearrange("p b t -> p (b t)"), 1.0 / D, RMS_EPS,
                                        ALU.mult, ALU.add).then_inc(ms_done, 1)
                dve.wait_ge(inv_rms_done, 1)
                dve.wait_ge(tables_loaded, N_TABLES)
                dve.wait_ge(c.constants, 48)
                rest_of_h(0)
                keep_values(0, 0)
                keep_values(0, 1)
                for t in range(NT):
                    rotate(0, t)
                    add_turned(0, t)
                    rests(0, t)
                with dve.Fori(0, B - 1) as b:
                    iteration(b, b + 1)
                iteration(B - 1, None)


def sigmoid_router(c, a):
    nc = c.nc
    N = B * NT
    with ExitStack() as ctx:
        weight_sum, inv_sum = c.sb("route_weight_sum", [P, N], ctx=ctx), c.sb("route_inv_sum", [P, N], ctx=ctx)
        biased, probs, count, chosen = (c.sb("route_" + n, [P, N, E], ctx=ctx)
                                        for n in ("biased", "probs", "count", "chosen"))
        bias, better = c.sb("route_bias", [P, E], ctx=ctx), c.sb("route_better", [P, N, E, E], ctx=ctx)
        bias_loaded, biased_done, probs_done = c.sem("route_bias_loaded"), c.sem("route_biased_done"), c.sem("route_probs_done")
        logits, coef = c.logits[:].rearrange("p b t e -> p (b t) e"), c.coef[:].rearrange("p b t e -> p (b t) e")

        with nc.Block() as block:
            @block.sync
            def _(sp):
                sp.dma_start(bias[:], a["L1_ffn_routing_bias"].unsqueeze(0).broadcast_to([P, E])).then_inc(bias_loaded, 16)
                sp.dma_start(c.gate[:], c.gates_dram[1, 1].unsqueeze(0).broadcast_to([P, B, D])).then_inc(c.constants, 16)

            @block.scalar
            def _(act):
                act.wait_ge(biased_done, 1)
                nc.scalar.activation(probs[:], biased[:], ACT.Sigmoid).then_inc(probs_done, 1)

            @block.vector
            def _(dve):
                nc.vector.memset(better[:], 0.0)
                dve.wait_ge(bias_loaded, 16)
                nc.vector.tensor_tensor(biased[:], logits, bias[:].unsqueeze(1).broadcast_to([P, N, E]),
                                        ALU.add).then_inc(biased_done, 1)
                dve.wait_ge(probs_done, 1)
                choose(nc, dve, probs[:], better, count[:], chosen[:], weight_sum[:], coef)
                nc.vector.reciprocal(inv_sum[:], weight_sum[:])
                dve.drain()
                nc.vector.tensor_tensor(coef, chosen[:], inv_sum[:].unsqueeze(2).broadcast_to([P, N, E]), ALU.mult)


def silu_experts_part(c, a, out):
    nc = c.nc
    NX = E + 1
    CHUNK = (2 * KC * F1 + IC * D) // B
    with ExitStack() as ctx:
        def sb(name, shape, dt=F32):
            return c.sb("e1_" + name, shape, dt, ctx)

        raw, w = sb("raw", [P, B, CHUNK]), sb("w", [P, 2, 2, B, CHUNK], F32R)
        h_parts, hidden = sb("h_parts", [P, 2, KC, S], F32R), sb("hidden", [P, 2, IC, S], F32R)
        silu, gu = sb("silu", [P, 2, S]), sb("gu", [P, 2, S])
        acc, coef = sb("acc", [P, B, NT, D]), sb("coef", [P, NX * B, NT])
        gate_ps = c.psum("e1_gate_ps", 2, ctx)
        up_ps = c.psum("e1_up_ps", 2, ctx)
        down_ps = c.psum("e1_down_ps", NT, ctx)
        (raw_loaded, w_head_done, w_split, h_head_done, h_split, gate_done, up_done, silu_done, gu_done, hidden_head_done,
         hidden_split, down_done, acc_done, y_done, x_done, stored) = (
            c.sem("e1_" + n) for n in
            ("raw_loaded w_head_done w_split h_head_done h_split gate_done up_done silu_done gu_done hidden_head_done "
             "hidden_split down_done acc_done y_done x_done stored").split())

        def weights(buf, part):
            return w[:, buf, part].rearrange("p b c -> p (b c)")

        def gate_up(buf, part, k, which, i):
            at = (2 * k + which) * F1 + i * P
            return weights(buf, part)[:, at:at + P]

        def down_rows(buf, part, i):
            at = 2 * KC * F1 + i * D
            return weights(buf, part)[:, at:at + D]

        with nc.Block() as block:
            @block.sync
            def _(sp):
                sp.dma_start(raw[:], a["experts"][0]).then_inc(raw_loaded, 16)
                with sp.Fori(1, NX) as x:
                    sp.wait_ge(w_split, B * x)
                    sp.dma_start(raw[:], a["experts"][x]).then_inc(raw_loaded, 16)
                view = out.rearrange("b (t p) d -> b p t d", p=P)
                with sp.Fori(0, B) as b:
                    sp.wait_ge(x_done, b + 1)
                    sp.dma_start(view[b], c.x[:, b]).then_inc(stored, 16)
                sp.wait_ge(stored, 16 * B)

            @block.tensor
            def _(pe):
                def step(n, buf, chunks):
                    pe.wait_ge(w_split, chunks)
                    pe.wait_ge(h_split, n + 1)
                    for i in range(IC):
                        if i >= 2:
                            pe.wait_ge(gu_done, IC * n + i - 1)
                        for which, ps, done in ((0, gate_ps, gate_done), (1, up_ps, up_done)):
                            product(nc.tensor, ps[:, i % 2, :],
                                    [(lambda p, k=k: gate_up(buf, p, k, which, i),
                                      lambda p, k=k: h_parts[:, p, k, :]) for k in range(KC)]).then_inc(done, 1)
                    pe.wait_ge(acc_done, n + 1)
                    for i in range(IC):
                        pe.wait_ge(hidden_split, IC * n + i + 1)
                        for t in range(NT):
                            for m, (p, r) in enumerate(PASSES):
                                last = nc.tensor.matmul(down_ps[:, t, 0:D], hidden[:, p, i, t * P:(t + 1) * P],
                                                        down_rows(buf, r, i), start=i == 0 and m == 0,
                                                        stop=i == IC - 1 and m == 2)
                    last.then_inc(down_done, 1)

                with pe.Fori(0, E // 2) as q:
                    for buf in range(2):
                        with pe.Fori(0, B) as b:
                            step(q * (2 * B) + buf * B + b, buf, q * (2 * B) + (buf + 1) * B)
                with pe.Fori(0, B) as b:
                    step(b + E * B, E % 2, NX * B)

            @block.scalar
            def _(act):
                def split_weight_heads(b, buf):
                    nc.scalar.activation(w[:, buf, HEAD, b], raw[:, b], ACT.Copy).then_inc(w_head_done, 1)

                def head_of_h(b):
                    nc.scalar.activation(h_parts[:, HEAD], c.hT[:, :, b, :], ACT.Copy).then_inc(h_head_done, 1)

                def step(n, b, buf, after, more_weights):
                    def silu_of(i):
                        act.wait_ge(gate_done, IC * n + i + 1)
                        nc.scalar.activation(silu[:, i % 2, :], gate_ps[:, i % 2, :], ACT.Silu).then_inc(silu_done, 1)

                    silu_of(0)
                    act.wait_ge(acc_done, n + 1)
                    for i in range(IC):
                        if i + 1 < IC:
                            silu_of(i + 1)
                        act.wait_ge(gu_done, IC * n + i + 1)
                        nc.scalar.activation(hidden[:, HEAD, i, :], gu[:, i % 2, :], ACT.Copy).then_inc(hidden_head_done, 1)
                    if after is not None:
                        act.wait_ge(up_done, IC * (n + 1))
                        head_of_h(after)
                    if more_weights:
                        split_weight_heads(b, 1 - buf)

                act.wait_ge(raw_loaded, 16)
                for b in range(B):
                    split_weight_heads(b, 0)
                head_of_h(0)
                with act.Fori(0, E // 2) as q:
                    for buf in range(2):
                        act.wait_ge(raw_loaded, q * 32 + 16 * (buf + 2))
                        with act.Fori(0, B - 1) as b:
                            step(q * (2 * B) + buf * B + b, b, buf, b + 1, True)
                        step(q * (2 * B) + (buf + 1) * B - 1, B - 1, buf, 0, True)
                with act.Fori(0, B - 1) as b:
                    step(b + E * B, b, 0, b + 1, False)
                step(NX * B - 1, B - 1, 0, None, False)

            @block.vector
            def _(dve):
                def split_weight_rests(m, b, buf):
                    dve.wait_ge(w_head_done, m + 1)
                    nc.vector.tensor_tensor(w[:, buf, REST, b], raw[:, b], w[:, buf, HEAD, b].bitcast(F32),
                                            ALU.subtract).then_inc(w_split, 1)

                def rest_of_h(n, b):
                    dve.wait_ge(h_head_done, n + 1)
                    nc.vector.tensor_tensor(h_parts[:, REST], c.hT[:, :, b, :], h_parts[:, HEAD].bitcast(F32),
                                            ALU.subtract).then_inc(h_split, 1)

                def step(n, b, buf, after, more_weights):
                    def times_up(i):
                        if i < 2:
                            dve.wait_ge(acc_done, n + 1)
                        else:
                            dve.wait_ge(hidden_split, IC * n + i - 1)
                        dve.wait_ge(silu_done, IC * n + i + 1)
                        dve.wait_ge(up_done, IC * n + i + 1)
                        nc.vector.tensor_tensor(gu[:, i % 2, :], silu[:, i % 2, :], up_ps[:, i % 2, :],
                                                ALU.mult).then_inc(gu_done, 1)

                    times_up(0)
                    for i in range(IC):
                        if i + 1 < IC:
                            times_up(i + 1)
                        dve.wait_ge(hidden_head_done, IC * n + i + 1)
                        nc.vector.tensor_tensor(hidden[:, REST, i, :], gu[:, i % 2, :],
                                                hidden[:, HEAD, i, :].bitcast(F32), ALU.subtract).then_inc(hidden_split, 1)
                    if after is not None:
                        rest_of_h(n + 1, after)
                    if more_weights:
                        split_weight_rests(n + B, b, 1 - buf)
                    dve.wait_ge(down_done, n + 1)
                    for t in range(NT):
                        last = nc.vector.scalar_tensor_tensor(out=acc[:, b, t, :], in0=down_ps[:, t, 0:D],
                                                              scalar=coef[:, n, t:t + 1], in1=acc[:, b, t, :],
                                                              op0=ALU.mult, op1=ALU.add)
                    last.then_inc(acc_done, 1)

                def finish(b):
                    dve.wait_ge(acc_done, b + E * B + 2)
                    nc.vector.tensor_tensor(acc[:, b], acc[:, b], c.gate[:, b, :].unsqueeze(1).broadcast_to([P, NT, D]),
                                            ALU.mult).then_inc(y_done, 1)
                    dve.wait_ge(y_done, b + 1)
                    nc.vector.tensor_tensor(c.x[:, b], c.x[:, b], acc[:, b], ALU.add).then_inc(x_done, 1)

                nc.vector.memset(acc[:], 0.0).then_inc(acc_done, 1)
                nc.vector.memset(coef[:, 0:B, :], 1.0)
                nc.vector.tensor_copy(coef[:, B:, :].rearrange("p (e b) t -> p (b t) e", e=E),
                                      c.coef[:].rearrange("p b t e -> p (b t) e"))
                dve.drain()
                for b in range(B):
                    split_weight_rests(b, b, 0)
                rest_of_h(0, 0)
                dve.wait_ge(c.constants, 64)
                with dve.Fori(0, E // 2) as q:
                    for buf in range(2):
                        with dve.Fori(0, B - 1) as b:
                            step(q * (2 * B) + buf * B + b, b, buf, b + 1, True)
                        step(q * (2 * B) + (buf + 1) * B - 1, B - 1, buf, 0, True)
                with dve.Fori(0, B - 1) as b:
                    step(b + E * B, b, 0, b + 1, False)
                    finish(b)
                step(NX * B - 1, B - 1, 0, None, False)
                finish(B - 1)


def program(nc, a, out):
    with ExitStack() as ctx:
        c = Core(nc, ctx)
        with ExitStack() as weights:
            w_ret = c.sb("w_ret", [P, 2, KC, D], F32R, weights)
            w_in = c.sb("w_in", [P, 2, KC, F0], F32R, weights)
            w_out = c.sb("w_out", [P, 2, MC, D], F32R, weights)
            modulation_and_weights(c, a, w_ret, w_in, w_out)
            c.begin_part()
            retention_part(c, a, w_ret, w_in, w_out)
            c.end_part()
        with ExitStack() as weights:
            w_up = c.sb("e0_w_up", [P, 2, E * KC, P], F32R, weights)
            w_down = c.sb("e0_w_down", [P, 2, E, D], F32R, weights)
            split_weights(c, "e0_w", ((a["L0_ffn_w1"].rearrange("e (k p) n -> p (e k) n", p=P), w_up, None),
                                      (a["L0_ffn_w2"].rearrange("e p n -> p e n"), w_down, None)))
            softmax_router(c)
            gelu_experts_part(c, a, w_up, w_down)
        with ExitStack() as weights:
            w_qk = c.sb("w_qk", [P, 2, KC, 2 * D], F32R, weights)
            w_v = c.sb("w_v", [P, 2, KC, D], F32R, weights)
            w_o = c.sb("w_o", [P, 2, KC, D], F32R, weights)
            chunks = "(k p) n -> p k n"
            split_weights(c, "at_w", ((a["wqT"].rearrange(chunks, p=P), w_qk[:, :, :, 0:D], a["qn_scale"]),
                                      (a["wkT"].rearrange(chunks, p=P), w_qk[:, :, :, D:2 * D], a["kn_scale"]),
                                      (a["wvT"].rearrange(chunks, p=P), w_v, None),
                                      (a["woT"].rearrange(chunks, p=P), w_o, None)))
            attention_part(c, a, w_qk, w_v, w_o)
        sigmoid_router(c, a)
        silu_experts_part(c, a, out)


def _columns(v):
    import numpy as np
    return np.ascontiguousarray(v.reshape(-1, P).T)


def layout(i):
    import numpy as np
    o = {"cT": np.ascontiguousarray(np.stack([i[f"L{l}_c"].T.reshape(KC, P, B).transpose(1, 0, 2) for l in range(2)], 1))}
    for name, of in (("b_ret", "L0_attn_b_ret"), ("ln1_scale", "L0_attn_ln1_scale"), ("ln1_bias", "L0_attn_ln1_bias"),
                     ("b_in", "L0_attn_b1"), ("e0_b_up", "L0_ffn_b1"), ("qn_scale", "L1_attn_qn_scale"),
                     ("kn_scale", "L1_attn_kn_scale")):
        o[name] = _columns(i[of])
    for name in ("L0_wmod", "L1_wmod", "L0_attn_x", "L0_attn_W_ret", "L0_attn_W1", "L0_attn_W2", "L0_attn_ln2_scale",
                 "L0_attn_ln2_bias", "L0_attn_b2", "L0_ffn_gate_w",
                 "L0_ffn_w1", "L0_ffn_w2", "L0_ffn_b2", "L1_attn_v_b", "L1_attn_o_b"):
        o[name] = np.ascontiguousarray(i[name])
    for name, of in (("wqT", "L1_attn_q_w"), ("wkT", "L1_attn_k_w"), ("wvT", "L1_attn_v_w"), ("woT", "L1_attn_o_w"),
                     ("router_w", "L1_ffn_router_w")):
        o[name] = np.ascontiguousarray(i[of].T)
    o["qk_bias"] = np.concatenate([i["L1_attn_q_b"], i["L1_attn_k_b"]])
    o["L1_ffn_routing_bias"] = np.ascontiguousarray(i["L1_ffn_routing_bias"])
    experts = []
    for gate, up, down in [tuple(i["L1_ffn_" + n] for n in ("sg_w", "su_w", "sd_w"))] + [
            tuple(i["L1_ffn_" + n][e] for n in ("wg", "wu", "wd")) for e in range(E)]:
        both = np.concatenate([gate.T, up.T], axis=1).reshape(KC, P, 2 * F1).transpose(1, 0, 2).reshape(P, -1)
        experts.append(np.concatenate([both, down.T.reshape(IC, P, D).transpose(1, 0, 2).reshape(P, -1)], axis=1))
    o["experts"] = np.ascontiguousarray(np.stack(experts).reshape(E + 1, P, B, -1))
    o["cos"], o["sin"] = rope_tables()
    return o


def rope_tables():
    import numpy as np
    inv_freq = np.float32(1.0) / np.float32(10000.0) ** (np.arange(0, HD, 2, dtype=np.float32) / np.float32(HD))
    freqs = np.arange(S, dtype=np.float32)[:, None] * inv_freq[None, :].astype(np.float32)
    emb = np.concatenate([freqs, freqs], axis=-1).astype(np.float64)
    sign = np.where(np.arange(HD) % 2 == 0, -1.0, 1.0)
    return tuple(np.ascontiguousarray(v.astype(np.float32).reshape(NT, P, HD).transpose(1, 0, 2))
                 for v in (np.cos(emb), np.sin(emb) * sign))


def kernel(**inputs):
    import numpy as np
    import concourse.bacc as bacc
    from concourse.bass_utils import run_bass_kernel_spmd

    nc = bacc.Bacc("TRN2", target_bir_lowering=False, num_devices=1)
    arrays = layout({k: np.asarray(v) for k, v in inputs.items()})
    a = {k: nc.dram_tensor("in_" + k, v.shape, mybir.dt.from_np(v.dtype), kind="ExternalInput").ap() for k, v in arrays.items()}
    out = nc.dram_tensor("out", (B, S, D), F32, kind="ExternalOutput").ap()
    program(nc, a, out)
    return run_bass_kernel_spmd(nc, [{"in_" + k: v for k, v in arrays.items()}], core_ids=[0]).results[0]["out"]
```

```python
from contextlib import ExitStack

import concourse.bass as bass
from concourse import mybir

F32 = mybir.dt.float32
F32R = mybir.dt.float32r
BF16 = mybir.dt.bfloat16
F16 = mybir.dt.float16
ALU = mybir.AluOpType
ACT = mybir.ActivationFunctionType
AX = mybir.AxisListType.X

P = 128
B, S, D = 8, 512, 256
NT = S // P
KC = D // P
F0 = 1024
MC = F0 // P
E = 8
F1 = 512
IC = F1 // P
H, HD = 16, 16
SA, CA, SB, CB = range(4)
MOD_CHUNK = (0, 1, 3, 4)
GA, GB = 2, 5
LN_EPS, RMS_EPS, SUM_EPS = 1e-5, 1e-8, 1e-8
SIG_SCALE = 2.0 ** 14
HEAD, REST = 0, 1
PASSES = ((HEAD, HEAD), (HEAD, REST), (REST, HEAD))


def product(pe, out, terms):
    steps = [(left, right, i, j) for left, right in terms for i, j in PASSES]
    for n, (left, right, i, j) in enumerate(steps):
        last = pe.matmul(out, left(i), right(j), start=n == 0, stop=n == len(steps) - 1)
    return last


def is_first(b):
    return isinstance(b, int) and b == 0


class Core:

    def __init__(self, nc, ctx):
        self.nc, self.ctx, self.part_sems = nc, ctx, None
        self.x = self.sb("x", [P, B, NT, D])
        self.hT = self.sb("hT", [P, KC, B, S])
        self.logits = self.sb("logits", [P, B, NT, E])
        self.coef = self.sb("coef", [P, B, NT, E])
        self.mean_square = self.sb("mean_square", [P, B, NT])
        self.inv_rms = self.sb("inv_rms", [P, B, NT])
        self.mod = self.sb("mod", [P, 2, 4, KC, B])
        self.gate = self.sb("gate", [P, B, D])
        self.ident = self.sb("ident", [P, P])
        self.neg_half = self.sb("neg_half", [P, B * NT])
        self.gates_dram = nc.dram_tensor("gates", [2, 2, B, D], F32, kind="Internal").ap()
        self.x_first, self.x_rest = self.sem("x_first"), self.sem("x_rest")
        self.constants = self.sem("constants")
        self.start = self.sem("start")
        self.passed = self.sem("passed")

    def sb(self, name, shape, dt=F32, ctx=None):
        return (ctx or self.ctx).enter_context(self.nc.sbuf_tensor(name, shape, dt))

    def sem(self, name):
        sem = self.nc.alloc_semaphore(name)
        if self.part_sems is not None:
            self.part_sems.append(sem)
        return sem

    def begin_part(self):
        self.part_sems = []

    def end_part(self):
        self.nc.clear_and_free_semaphores(self.part_sems)
        self.nc.all_engine_barrier()
        self.part_sems = None

    def psum(self, name, n, ctx):
        return ctx.enter_context(self.nc.psum_tensor(name, [P, n, 512], F32))


class Modulation:

    def __init__(self, c, ctx, layer):
        self.c, self.nc, self.layer = c, c.nc, layer
        n = f"mod{layer}_"
        self.cT, self.silu_c = c.sb(n + "cT", [P, KC, B], ctx=ctx), c.sb(n + "silu_c", [P, KC, B], ctx=ctx)
        self.w = c.sb(n + "w", [P, KC, 6 * D], ctx=ctx)
        self.rows, self.sign = c.sb(n + "rows", [B, 2 * D], ctx=ctx), c.sb(n + "sign", [B, 2 * D], ctx=ctx)
        self.mod_ps, self.gate_ps = c.psum(n + "mod_ps", 1, ctx), c.psum(n + "gate_ps", 1, ctx)
        (self.c_loaded, self.w_loaded, self.silu_done, self.mod_done, self.gates_done, self.sign_done, self.size_done,
         self.rows_done, self.rows_stored, self.kept) = (c.sem(n + s) for s in (
            "c_loaded w_loaded silu_done mod_done gates_done sign_done size_done rows_done rows_stored kept").split())

    def load(self, sp, a):
        sp.dma_start(self.cT[:], a["cT"][:, self.layer]).then_inc(self.c_loaded, 16)
        sp.dma_start(self.w[:], a[f"L{self.layer}_wmod"].rearrange("(k p) n -> p k n", p=P)).then_inc(self.w_loaded, 16)

    def store_rows(self, sp):
        sp.wait_ge(self.rows_done, 1)
        sp.dma_start(self.c.gates_dram[self.layer].rearrange("k b d -> b k d"),
                     self.rows[:].rearrange("b (k d) -> b k d", k=2)).then_inc(self.rows_stored, 16)
        sp.wait_ge(self.rows_stored, 16)

    def silu(self, act):
        act.wait_ge(self.c_loaded, 16)
        self.nc.scalar.activation(self.silu_c[:], self.cT[:], ACT.Silu).then_inc(self.silu_done, 1)

    def products(self, pe):
        pe.wait_ge(self.silu_done, 1)
        pe.wait_ge(self.w_loaded, 16)
        for kind, chunk in enumerate(MOD_CHUNK):
            for m in range(KC):
                at = (kind * KC + m) * B
                col = chunk * D + m * P
                for k in range(KC):
                    last = self.nc.tensor.matmul(self.mod_ps[:, 0, at:at + B], self.w[:, k, col:col + P],
                                                 self.silu_c[:, k, :], start=k == 0, stop=k == KC - 1)
        last.then_inc(self.mod_done, 1)
        for n, chunk in enumerate((GA, GB)):
            for k in range(KC):
                last = self.nc.tensor.matmul(self.gate_ps[0:B, 0, n * D:(n + 1) * D], self.silu_c[:, k, :],
                                             self.w[:, k, chunk * D:(chunk + 1) * D], start=k == 0, stop=k == KC - 1)
        last.then_inc(self.gates_done, 1)

    def keep(self, dve):
        dve.wait_ge(self.mod_done, 1)
        m = self.mod_ps[:, 0, 0:4 * KC * B].rearrange("p (i k b) -> p i k b", i=4, k=KC)
        for i in range(4):
            self.nc.vector.tensor_scalar(self.c.mod[:, self.layer, i], m[:, i], 1.0 if i in (CA, CB) else 0.0, None,
                                         ALU.add).then_inc(self.kept, 1)
        dve.wait_ge(self.gates_done, 1)
        g, sign, rows = self.gate_ps[0:B, 0, :], self.sign[:], self.rows[:]
        self.nc.vector.tensor_scalar(sign, g, 0.0, 2.0, ALU.is_ge, ALU.mult).then_inc(self.sign_done, 1)
        dve.wait_ge(self.sign_done, 1)
        self.nc.vector.tensor_scalar(sign, sign, -1.0, None, ALU.add).then_inc(self.sign_done, 1)
        dve.wait_ge(self.sign_done, 2)
        self.nc.vector.tensor_tensor(rows, g, sign, ALU.mult).then_inc(self.size_done, 1)
        dve.wait_ge(self.size_done, 1)
        self.nc.vector.scalar_tensor_tensor(out=rows, in0=rows, scalar=0.25, in1=sign, op0=ALU.max,
                                            op1=ALU.mult).then_inc(self.rows_done, 1)


def modulation_and_weights(c, a, tables, w_ret, w_in, w_out):
    nc = c.nc
    with ExitStack() as ctx:
        modulation = Modulation(c, ctx, 0)
        raw_ret = c.sb("raw_ret", [P, KC, D], ctx=ctx)
        raw_in = c.sb("raw_in", [P, KC, F0], ctx=ctx)
        raw_out = c.sb("raw_out", [P, MC, D], ctx=ctx)
        ones = c.sb("ones_setup", [P, P], ctx=ctx)
        raw_loaded = [c.sem(f"raw_loaded_{n}") for n in range(3)]
        heads_split, rests_split, ones_set = c.sem("heads_split"), c.sem("rests_split"), c.sem("ones_set")
        weights = ((raw_ret, w_ret), (raw_in, w_in), (raw_out, w_out))

        with nc.Block() as block:
            @block.sync
            def _(sp):
                modulation.load(sp, a)
                x_in = a["L0_attn_x"].rearrange("b (t p) d -> p b t d", p=P)
                sp.dma_start(c.x[:, 0], x_in[:, 0]).then_inc(c.x_first, 16)
                sp.dma_start(raw_ret[:], a["L0_attn_W_ret"].rearrange("(k p) n -> p k n", p=P)).then_inc(raw_loaded[0], 16)
                sp.dma_start(raw_in[:], a["L0_attn_W1"].rearrange("(k p) n -> p k n", p=P)).then_inc(raw_loaded[1], 16)
                sp.dma_start(raw_out[:], a["L0_attn_W2"].rearrange("(k p) n -> p k n", p=P)).then_inc(raw_loaded[2], 16)
                tables.load(sp, a)
                for b in range(1, B):
                    sp.dma_start(c.x[:, b], x_in[:, b]).then_inc(c.x_rest, 16)
                modulation.store_rows(sp)
                sp.dma_start(c.gate[:], c.gates_dram[0, 0].unsqueeze(0).broadcast_to([P, B, D])).then_inc(c.constants, 16)

            @block.gpsimd
            def _(pool):
                pool.memset(c.neg_half[:], -0.5).then_inc(c.start, 1)
                pool.memset(ones[:], 1.0).then_inc(ones_set, 1)
                pool.wait_ge(ones_set, 1)
                pool.affine_select(out=c.ident[:], in_=ones[:], compare_op=ALU.is_equal, fill=0.0, base=0,
                                   pattern=[[-1, P]], channel_multiplier=1).then_inc(ones_set, 1)

            @block.scalar
            def _(act):
                modulation.silu(act)
                for n, (raw, split) in enumerate(weights):
                    act.wait_ge(raw_loaded[n], 16)
                    nc.scalar.activation(split[:, HEAD], raw[:], ACT.Copy).then_inc(heads_split, 1)

            @block.tensor
            def _(pe):
                modulation.products(pe)

            @block.vector
            def _(dve):
                for n, (raw, split) in enumerate(weights):
                    if n == 2:
                        modulation.keep(dve)
                    dve.wait_ge(heads_split, n + 1)
                    nc.vector.tensor_tensor(split[:, REST], raw[:], split[:, HEAD].bitcast(F32),
                                            ALU.subtract).then_inc(rests_split, 1)


class RetentionTables:

    def __init__(self, c, ctx):
        self.b_ret, self.ln1_scale, self.ln1_bias = (c.sb(n, [P, KC], ctx=ctx) for n in ("b_ret", "ln1_scale", "ln1_bias"))
        self.b_in, self.gate_w = c.sb("b_in", [P, MC], ctx=ctx), c.sb("gate_w", [P, KC, E], ctx=ctx)
        self.ln2_scale, self.ln2_bias = c.sb("ln2_scale", [P, D], ctx=ctx), c.sb("ln2_bias", [P, D], ctx=ctx)
        self.b_out = c.sb("b_out", [1, D], ctx=ctx)
        self.loaded = c.sem("tables_loaded")
        self.LOADS = 8

    def load(self, sp, a):
        for name, to in (("b_ret", self.b_ret), ("ln1_scale", self.ln1_scale), ("ln1_bias", self.ln1_bias),
                         ("b_in", self.b_in)):
            sp.dma_start(to[:], a[name]).then_inc(self.loaded, 16)
        for name, to in (("ln2_scale", self.ln2_scale), ("ln2_bias", self.ln2_bias)):
            sp.dma_start(to[:], a["L0_attn_" + name].unsqueeze(0).broadcast_to([P, D])).then_inc(self.loaded, 16)
        sp.dma_start(self.b_out[:], a["L0_attn_b2"].unsqueeze(0)).then_inc(self.loaded, 16)
        sp.dma_start(self.gate_w[:], a["L0_ffn_gate_w"].rearrange("(k p) e -> p k e", p=P)).then_inc(self.loaded, 16)


class Norm:

    def __init__(self, c, ctx, name, eps):
        self.c, self.nc = c, c.nc
        self.stats = c.sb(name + "_stats", [P, NT, 6], ctx=ctx)
        self.moments = c.sb(name + "_moments", [P, NT, 2], ctx=ctx)
        self.eps = eps
        self.shifted = c.sb(name + "_shifted", [P, NT], ctx=ctx)
        self.inv_std = c.sb(name + "_inv_std", [P, NT], ctx=ctx)
        self.stats_done, self.moments_done = c.sem(name + "_stats_done"), c.sem(name + "_moments_done")
        self.shifted_done, self.inv_done = c.sem(name + "_shifted_done"), c.sem(name + "_inv_done")

    def gather(self, tile, tiles=range(NT)):
        for t in tiles:
            last = self.nc.vector.bn_stats(self.stats[:, t, :], tile(t))
        if t == NT - 1:
            last.then_inc(self.stats_done, 1)

    def aggregate(self, dve, b):
        dve.drain()
        for t in range(NT):
            last = self.nc.vector.bn_aggr(self.moments[:, t, :], self.stats[:, t, :])
        last.then_inc(self.moments_done, 1)

    def invert(self, pool, b):
        pool.wait_ge(self.moments_done, b + 1)
        self.nc.gpsimd.tensor_tensor(self.shifted[:], self.moments[:, :, 1], self.eps, ALU.add).then_inc(
            self.shifted_done, 1)
        pool.wait_ge(self.shifted_done, b + 1)
        self.nc.gpsimd.tensor_tensor(self.inv_std[:], self.shifted[:], self.c.neg_half[:, 0:NT], ALU.pow).then_inc(
            self.inv_done, 1)

    def apply(self, dve, b, to, tile, done):
        dve.wait_ge(self.inv_done, b + 1)
        for t in range(NT):
            last = self.nc.vector.tensor_scalar(to[:, t, :], tile(t), self.moments[:, t, 0:1], self.inv_std[:, t:t + 1],
                                                ALU.subtract, ALU.mult)
        last.then_inc(done, 1)


def transposes(pe, c, to, tiles):
    for k in range(KC):
        for t in range(NT):
            last = pe.transpose(to[:, k, t * P:(t + 1) * P], tiles[:, t, k * P:(k + 1) * P], c.ident[:])
    return last


def rows_of(ps, t):
    return ps[:, t // 2, (t % 2) * D:(t % 2 + 1) * D]


def retention_part(c, tables, w_ret, w_in, w_out):
    nc = c.nc
    with ExitStack() as ctx:
        def sb(name, shape, dt=F32):
            return c.sb(name, shape, dt, ctx)

        b_ret, ln1_scale, ln1_bias, b_in, gate_w = (tables.b_ret, tables.ln1_scale, tables.ln1_bias, tables.b_in,
                                                    tables.gate_w)
        ln2_scale, ln2_bias, b_out = tables.ln2_scale, tables.ln2_bias, tables.b_out
        half, eps = sb("half", [P, S]), sb("ln_eps", [P, NT])
        ident_wide = sb("ident_wide", [P, KC, D], F32R)
        ones, b_out_row = sb("ones", [P, P], F32R), sb("b_out_row", [P, D], F32R)
        norm_x, norm_1 = Norm(c, ctx, "norm_x", eps[:]), Norm(c, ctx, "norm_1", eps[:])
        norm_2, norm_next = Norm(c, ctx, "norm_2", eps[:]), Norm(c, ctx, "norm_next", eps[:])
        xn, xn_next = sb("xn", [P, NT, D]), sb("xn_next", [P, NT, D])
        h, h_next = sb("h", [P, KC, S]), sb("h_next", [P, KC, S])
        h0_parts, h1_parts = sb("h0_parts", [P, 2, KC, S], F32R), sb("h1_parts", [P, 2, KC, S], F32R)
        sig, average = sb("sig", [P, KC, S]), sb("average", [P, KC, S])
        G_BUFS = 4
        g = sb("g", [P, G_BUFS, S])
        hidden = sb("hidden", [P, 2, MC, S], F32R)
        gate_scale, gate_bias, y_scaled = sb("gate_scale", [P, D]), sb("gate_bias", [P, D]), sb("y_scaled", [P, NT, D])
        spare = sb("spare", [P, 1])
        tp_ps = c.psum("tp_ps", 2, ctx)
        ret_ps = c.psum("ret_ps", 2, ctx)
        in_ps = c.psum("in_ps", 2, ctx)
        out_ps = c.psum("out_ps", 2, ctx)

        tables_loaded, tables_set, b_out_head = tables.loaded, c.sem("tables_set"), c.sem("b_out_head")
        xn_done, xT_done, h0_done, h0_split = c.sem("xn_done"), c.sem("xT_done"), c.sem("h0_done"), c.sem("h0_split")
        ret_done, sig_done, average_done = c.sem("ret_done"), c.sem("sig_done"), c.sem("average_done")
        sum_done, sumT_done, n1_done, n1T_done = c.sem("sum_done"), c.sem("sumT_done"), c.sem("n1_done"), c.sem("n1T_done")
        h1_done, h1_split, in_done, g_done = c.sem("h1_done"), c.sem("h1_split"), c.sem("in_done"), c.sem("g_done")
        hidden_split, out_done = c.sem("hidden_split"), c.sem("out_done")
        gate_rows_done, x_biased, scaled_done, x_done = (c.sem("gate_rows_done"), c.sem("x_biased"),
                                                         c.sem("scaled_done"), c.sem("x_done"))
        next_done, nextT_done = c.sem("next_done"), c.sem("nextT_done")
        next_h_done, hT_kept = c.sem("next_h_done"), c.sem("hT_kept")
        logits_done, logits_kept, sums_read = c.sem("logits_done"), c.sem("logits_kept"), c.sem("sums_read")

        N_TABLES = 16 * tables.LOADS
        SET_BY_POOL = 2

        with nc.Block() as block:
            @block.gpsimd
            def _(pool):
                pool.memset(eps[:], LN_EPS)
                pool.memset(half[:], 0.5)
                pool.memset(ident_wide[:].bitcast(F32), 0.0)
                pool.memset(ones[:].bitcast(F32), 1.0)
                pool.memset(b_out_row[:].bitcast(F32), 0.0).then_inc(tables_set, 1)
                pool.wait_ge(tables_set, 1)
                for k in range(KC):
                    last = nc.gpsimd.tensor_copy(ident_wide[:, k, k * P:(k + 1) * P], c.ident[:])
                last.then_inc(tables_set, 1)
                pool.wait_ge(tables_loaded, N_TABLES)
                pool.wait_ge(c.constants, 16)

                def keep_hT(b):
                    pool.wait_ge(c.start, 1)
                    pool.wait_ge(next_h_done, b + 1)
                    nc.gpsimd.tensor_copy(c.hT[:, :, b, :], h_next[:]).then_inc(hT_kept, 1)

                def rest_h0(b):
                    pool.wait_ge(h0_done, b + 1)
                    nc.gpsimd.tensor_tensor(h0_parts[:, REST], h[:], h0_parts[:, HEAD].bitcast(F32),
                                            ALU.subtract).then_inc(h0_split, 1)

                def gate_tables(b):
                    pool.wait_ge(c.start, 1)
                    if not is_first(b):
                        pool.wait_ge(scaled_done, b)
                    nc.gpsimd.tensor_tensor(gate_scale[:], c.gate[:, b, :], ln2_scale[:], ALU.mult)
                    nc.gpsimd.tensor_tensor(gate_bias[:], c.gate[:, b, :], ln2_bias[:], ALU.mult).then_inc(
                        gate_rows_done, 1)
                    pool.wait_ge(c.start, 1)
                    pool.wait_ge(gate_rows_done, b + 1)
                    nc.gpsimd.tensor_tensor(c.x[:, b], c.x[:, b], gate_bias[:].unsqueeze(1).broadcast_to([P, NT, D]),
                                            ALU.add).then_inc(x_biased, 1)

                norm_x.invert(pool, 0)
                rest_h0(0)
                norm_1.invert(pool, 0)
                norm_x.invert(pool, 1)
                rest_h0(1)
                gate_tables(0)
                norm_1.invert(pool, 1)
                with pool.Fori(1, B - 1) as b:
                    norm_2.invert(pool, b - 1)
                    norm_x.invert(pool, b + 1)
                    norm_next.invert(pool, b - 1)
                    rest_h0(b + 1)
                    gate_tables(b)
                    keep_hT(b - 1)
                    norm_1.invert(pool, b + 1)
                norm_2.invert(pool, B - 2)
                norm_next.invert(pool, B - 2)
                gate_tables(B - 1)
                keep_hT(B - 2)
                norm_2.invert(pool, B - 1)
                norm_next.invert(pool, B - 1)
                keep_hT(B - 1)

            @block.tensor
            def _(pe):
                def x_by_feature(b):
                    pe.wait_ge(xn_done, b + 1)
                    transposes(nc.tensor, c, tp_ps, xn).then_inc(xT_done, 1)

                def retention(b):
                    pe.wait_ge(h0_split, b + 1)
                    for m in range(KC):
                        product(nc.tensor, ret_ps[:, m, :],
                                [(lambda i, k=k: w_ret[:, i, k, m * P:(m + 1) * P],
                                  lambda j, k=k: h0_parts[:, j, k, :]) for k in range(KC)]).then_inc(ret_done, 1)

                def sum_by_token(b):
                    pe.wait_ge(sum_done, b + 1)
                    for t in range(NT):
                        for k in range(KC):
                            last = nc.tensor.transpose(rows_of(ret_ps, t)[:, k * P:(k + 1) * P],
                                                       sig[:, k, t * P:(t + 1) * P], c.ident[:])
                    last.then_inc(sumT_done, 1)

                def h1_by_feature(b):
                    pe.wait_ge(n1_done, b + 1)
                    transposes(nc.tensor, c, tp_ps, xn).then_inc(n1T_done, 1)

                def widen(b, ms):
                    for m in ms:
                        if m == 0:
                            pe.wait_ge(h1_split, b + 1)
                        if m >= 2 or not is_first(b):
                            pe.wait_ge(g_done, MC * b + m - 1)
                        product(nc.tensor, in_ps[:, m % 2, :],
                                [(lambda i, k=k: w_in[:, i, k, m * P:(m + 1) * P],
                                  lambda j, k=k: h1_parts[:, j, k, :]) for k in range(KC)]).then_inc(in_done, 1)

                def bias_and_residual(t):
                    nc.tensor.matmul(rows_of(out_ps, t), ones[:], b_out_row[:], start=True, stop=False)
                    for k in range(KC):
                        for part in (HEAD, REST):
                            nc.tensor.matmul(rows_of(out_ps, t), h1_parts[:, part, k, t * P:(t + 1) * P],
                                             ident_wide[:, k, :], start=False, stop=False)

                def narrow(b, *ts):
                    for t in ts:
                        if t == 0:
                            pe.wait_ge(hidden_split, MC * (b + 1))
                        cols = slice(t * P, (t + 1) * P)
                        to = rows_of(out_ps, t)
                        if t != NT - 1:
                            bias_and_residual(t)
                        for m in range(MC):
                            for n, (i, j) in enumerate(PASSES):
                                last = nc.tensor.matmul(to, hidden[:, i, m, cols], w_out[:, j, m, :], start=False,
                                                        stop=m == MC - 1 and n == 2)
                        last.then_inc(out_done, 1)

                def next_by_feature(b):
                    pe.wait_ge(next_done, b + 1)
                    transposes(nc.tensor, c, ret_ps, xn_next).then_inc(nextT_done, 1)

                def route(b):
                    pe.wait_ge(next_h_done, b + 1)
                    for t in range(NT):
                        for k in range(KC):
                            last = nc.tensor.matmul(tp_ps[:, 0, t * E:(t + 1) * E], h_next[:, k, t * P:(t + 1) * P],
                                                    gate_w[:, k, :], start=k == 0, stop=k == KC - 1)
                    last.then_inc(logits_done, 1)

                def iteration(b, first=False, final=False):
                    widen(b, range(0, 4))
                    if not final:
                        x_by_feature(b + 1)
                    widen(b, range(4, 7))
                    if not first:
                        next_by_feature(b - 1)
                    widen(b, range(7, MC))
                    if not final:
                        if not first:
                            pe.wait_ge(next_h_done, b)
                        retention(b + 1)
                    if not first:
                        route(b - 1)
                    narrow(b, 0)
                    if not final:
                        sum_by_token(b + 1)
                    narrow(b, 1, 2)
                    bias_and_residual(NT - 1)
                    if not final:
                        if not first:
                            pe.wait_ge(logits_kept, b)
                        h1_by_feature(b + 1)
                    narrow(b, 3)

                pe.wait_ge(tables_loaded, N_TABLES)
                pe.wait_ge(tables_set, SET_BY_POOL)
                pe.wait_ge(b_out_head, 2)
                x_by_feature(0)
                retention(0)
                sum_by_token(0)
                h1_by_feature(0)
                iteration(0, first=True)
                with pe.Fori(1, B - 1) as b:
                    iteration(b)
                iteration(B - 1, final=True)
                next_by_feature(B - 1)
                route(B - 1)

            @block.scalar
            def _(act):
                def modulate_x(b):
                    act.wait_ge(c.start, 1)
                    act.wait_ge(xT_done, b + 1)
                    for to in (h, h0_parts[:, HEAD]):
                        for k in range(KC):
                            last = nc.scalar.activation(to[:, k, :], tp_ps[:, k, :], ACT.Identity,
                                                        bias=c.mod[:, 0, SA, k, bass.ds(b, 1)],
                                                        scale=c.mod[:, 0, CA, k, bass.ds(b, 1)])
                    last.then_inc(h0_done, 1)

                def sigmoids(b):
                    for m in range(KC):
                        act.wait_ge(ret_done, KC * b + m + 1)
                        nc.scalar.activation(sig[:, m, :], ret_ps[:, m, :], ACT.Sigmoid,
                                             bias=b_ret[:, m:m + 1]).then_inc(sig_done, 1)

                def scale_h1(b):
                    act.wait_ge(n1T_done, b + 1)
                    for to in (h, h1_parts[:, HEAD]):
                        for k in range(KC):
                            last = nc.scalar.activation(to[:, k, :], tp_ps[:, k, :], ACT.Identity,
                                                        bias=ln1_bias[:, k:k + 1], scale=ln1_scale[:, k:k + 1])
                    last.then_inc(h1_done, 1)

                def gelu(b, ms):
                    for m in ms:
                        act.wait_ge(in_done, MC * b + m + 1)
                        if not (is_first(b) and m < G_BUFS):
                            act.wait_ge(hidden_split, MC * b + m + 1 - G_BUFS)
                        nc.scalar.activation(g[:, m % G_BUFS, :], in_ps[:, m % 2, :], ACT.Gelu_apprx_tanh,
                                             bias=b_in[:, m:m + 1])
                        nc.scalar.activation(hidden[:, HEAD, m, :], in_ps[:, m % 2, :], ACT.Gelu_apprx_tanh,
                                             bias=b_in[:, m:m + 1]).then_inc(g_done, 1)

                def tail(b):
                    act.wait_ge(c.start, 1)
                    act.wait_ge(nextT_done, b + 1)
                    if not is_first(b):
                        act.wait_ge(hT_kept, b)
                    for k in range(KC):
                        last = nc.scalar.activation(h_next[:, k, :], ret_ps[:, k, :], ACT.Identity,
                                                    bias=c.mod[:, 0, SB, k, bass.ds(b, 1)], scale=c.mod[:, 0, CB, k, bass.ds(b, 1)])
                    last.then_inc(next_h_done, 1)

                def iteration(b, first=False, final=False):
                    gelu(b, range(0, 4))
                    if not final:
                        modulate_x(b + 1)
                    gelu(b, range(4, 7))
                    if not first:
                        tail(b - 1)
                    gelu(b, range(7, MC))
                    if not final:
                        sigmoids(b + 1)
                        scale_h1(b + 1)
                        nc.scalar.activation(spare[:], b_in[:, 0:1], ACT.Gelu_apprx_tanh)
                        act.drain()

                act.wait_ge(tables_loaded, N_TABLES)
                modulate_x(0)
                sigmoids(0)
                scale_h1(0)
                iteration(0, first=True)
                with act.Fori(1, B - 1) as b:
                    iteration(b)
                iteration(B - 1, final=True)
                tail(B - 1)

            @block.vector
            def _(dve):
                def x_tile(b):
                    return lambda t: c.x[:, b, t, :]

                def moments_x(b):
                    b = b if isinstance(b, int) else dve.snap(b)
                    norm_x.gather(x_tile(b))
                    norm_x.aggregate(dve, b)

                def normalise_x(b):
                    norm_x.apply(dve, b, xn, x_tile(b), xn_done)

                def average_and_sum(b):
                    for k in range(KC):
                        dve.wait_ge(sig_done, KC * b + k + 1)
                        nc.vector.tensor_tensor_scan(average[:, k, :], half[:], sig[:, k, :], 0.0, ALU.mult,
                                                     ALU.add).then_inc(average_done, 1)
                    dve.wait_ge(average_done, KC * (b + 1))
                    nc.vector.scalar_tensor_tensor(out=sig[:].rearrange("p k s -> p (k s)"),
                                                   in0=average[:].rearrange("p k s -> p (k s)"), scalar=0.5,
                                                   in1=h[:].rearrange("p k s -> p (k s)"),
                                                   op0=ALU.mult, op1=ALU.add).then_inc(sum_done, 1)

                def normalise_1(b):
                    dve.wait_ge(sumT_done, b + 1)
                    norm_1.gather(lambda t: rows_of(ret_ps, t))
                    norm_1.aggregate(dve, b)
                    norm_1.apply(dve, b, xn, lambda t: rows_of(ret_ps, t), n1_done)

                def rest_h1(b):
                    dve.wait_ge(h1_done, b + 1)
                    nc.vector.tensor_tensor(h1_parts[:, REST], h[:], h1_parts[:, HEAD].bitcast(F32),
                                            ALU.subtract).then_inc(h1_split, 1)

                def rest_hidden(b, ms):
                    for m in ms:
                        dve.wait_ge(g_done, MC * b + m + 1)
                        nc.vector.tensor_tensor(hidden[:, REST, m, :], g[:, m % G_BUFS, :],
                                                hidden[:, HEAD, m, :].bitcast(F32), ALU.subtract).then_inc(hidden_split, 1)

                def moments_2(b, ts):
                    dve.wait_ge(out_done, NT * b + ts[-1] + 1)
                    norm_2.gather(lambda t: rows_of(out_ps, t), ts)
                    if ts[-1] == NT - 1:
                        norm_2.aggregate(dve, b)

                def update_x(b):
                    dve.wait_ge(norm_2.moments_done, b + 1)
                    dve.wait_ge(gate_rows_done, b + 1)
                    for t in range(NT):
                        last = nc.vector.scalar_tensor_tensor(out=y_scaled[:, t, :], in0=rows_of(out_ps, t),
                                                              scalar=norm_2.moments[:, t, 0:1], in1=gate_scale[:],
                                                              op0=ALU.subtract, op1=ALU.mult)
                    last.then_inc(scaled_done, 1)
                    dve.wait_ge(c.start, 1)
                    dve.wait_ge(norm_2.inv_done, b + 1)
                    dve.wait_ge(x_biased, b + 1)
                    dve.wait_ge(scaled_done, b + 1)
                    for t in range(NT):
                        last = nc.vector.scalar_tensor_tensor(out=c.x[:, b, t, :], in0=y_scaled[:, t, :],
                                                              scalar=norm_2.inv_std[:, t:t + 1], in1=c.x[:, b, t, :],
                                                              op0=ALU.mult, op1=ALU.add)
                    last.then_inc(x_done, 1)

                def moments_next(b):
                    dve.wait_ge(c.start, 1)
                    dve.wait_ge(x_done, b + 1)
                    norm_next.gather(x_tile(b))
                    norm_next.aggregate(dve, b)

                def normalise_next(b):
                    norm_next.apply(dve, b, xn_next, x_tile(b), next_done)

                def keep_logits(b):
                    dve.wait_ge(c.start, 1)
                    dve.wait_ge(logits_done, b + 1)
                    nc.vector.tensor_copy(c.logits[:, b], tp_ps[:, 0, 0:NT * E].rearrange("p (t e) -> p t e", t=NT)
                                          ).then_inc(logits_kept, 1)

                def iteration(b, first=False, final=False):
                    if not first:
                        moments_2(b - 1, (2, 3))
                    if not final:
                        moments_x(b + 1)
                    rest_hidden(b, (0,))
                    if not final:
                        normalise_x(b + 1)
                    rest_hidden(b, (1,))
                    if not first:
                        update_x(b - 1)
                    rest_hidden(b, (2, 3))
                    if not first:
                        moments_next(b - 1)
                    rest_hidden(b, (4,))
                    if not first:
                        normalise_next(b - 1)
                    rest_hidden(b, range(5, MC))
                    if not final:
                        average_and_sum(b + 1)
                    if not first:
                        keep_logits(b - 1)
                    if not final:
                        normalise_1(b + 1)
                    moments_2(b, (0, 1))
                    if not final:
                        rest_h1(b + 1)

                dve.wait_ge(tables_loaded, N_TABLES)
                dve.wait_ge(tables_set, SET_BY_POOL)
                nc.vector.tensor_copy(b_out_row[0:1, :], b_out[:]).then_inc(b_out_head, 1)
                dve.wait_ge(b_out_head, 1)
                nc.vector.tensor_tensor(b_out_row[32:33, :], b_out[:], b_out_row[0:1, :].bitcast(F32),
                                        ALU.subtract).then_inc(b_out_head, 1)
                dve.wait_ge(c.x_first, 16)
                moments_x(0)
                normalise_x(0)
                average_and_sum(0)
                normalise_1(0)
                rest_h1(0)
                dve.wait_ge(c.x_rest, 16 * (B - 1))
                iteration(0, first=True)
                with dve.Fori(1, B - 1) as b:
                    iteration(b)
                iteration(B - 1, final=True)
                moments_2(B - 1, (2, 3))
                update_x(B - 1)
                moments_next(B - 1)
                normalise_next(B - 1)
                keep_logits(B - 1)


def weight_splitter(c, ctx, name, weights):
    nc = c.nc
    raw = [c.sb(f"{name}_raw_{n}", [P, split.shape[2], split.shape[3]], ctx=ctx) for n, (_, split, _) in enumerate(weights)]
    scales = [c.sb(f"{name}_scale_{n}", [P, split.shape[2]], ctx=ctx) for n, (_, split, _) in enumerate(weights)]
    loaded = [c.sem(f"{name}_loaded_{n}") for n in range(len(weights))]
    scaled, head_done, rest_done = c.sem(name + "_scaled"), c.sem(name + "_head_done"), c.sem(name + "_rest_done")

    def load(sp):
        for n, (view, split, scale) in enumerate(weights):
            if scale is not None:
                sp.dma_start(scales[n][:], scale).then_inc(loaded[n], 16)
            sp.dma_start(raw[n][:], view).then_inc(loaded[n], 16)

    def split(pool):
        n_scaled = 0
        for n, (view, to, scale) in enumerate(weights):
            pool.wait_ge(loaded[n], 16 if scale is None else 32)
            if scale is not None:
                for k in range(to.shape[2]):
                    nc.gpsimd.tensor_scalar(raw[n][:, k, :], raw[n][:, k, :], scales[n][:, k:k + 1], 1.0, ALU.mult,
                                            ALU.mult).then_inc(scaled, 1)
                    n_scaled += 1
                pool.wait_ge(scaled, n_scaled)
            nc.gpsimd.tensor_copy(to[:, HEAD], raw[n][:]).then_inc(head_done, 1)
            pool.wait_ge(head_done, n + 1)
            nc.gpsimd.tensor_tensor(to[:, REST], raw[n][:], to[:, HEAD].bitcast(F32), ALU.subtract).then_inc(rest_done, 1)

    return load, split


def choose(nc, dve, value, better, count, chosen, weight_sum, coef):
    for f in range(E):
        for lo, hi, op in ((0, f, ALU.is_gt), (f + 1, E, ALU.is_ge)):
            if lo < hi:
                nc.vector.tensor_tensor(better[:, :, lo:hi, f], value[:, :, f:f + 1].broadcast_to([P, B * NT, hi - lo]),
                                        value[:, :, lo:hi], op)
    dve.drain()
    nc.vector.tensor_reduce(count, better[:, :, :, :], AX, ALU.add)
    dve.drain()
    nc.vector.tensor_scalar(coef, count, 2.0, None, ALU.is_lt)
    dve.drain()
    nc.vector.tensor_tensor(chosen, coef, value, ALU.mult)
    dve.drain()
    nc.vector.tensor_reduce(weight_sum, chosen, AX, ALU.add)
    dve.drain()


def softmax_router(c, a, w_up, w_down):
    nc = c.nc
    N = B * NT
    with ExitStack() as ctx:
        peak, total, inv_total = (c.sb("gate_" + n, [P, N], ctx=ctx) for n in ("peak", "total", "inv_total"))
        shifted, power, gates, count, chosen = (c.sb("gate_" + n, [P, N, E], ctx=ctx)
                                                for n in ("shifted", "power", "values", "count", "chosen"))
        weight_sum, better = c.sb("gate_weight_sum", [P, N], ctx=ctx), c.sb("gate_better", [P, N, E, E], ctx=ctx)
        shifted_done, power_done = c.sem("gate_shifted_done"), c.sem("gate_power_done")
        better_zeroed = c.sem("gate_better_zeroed")
        modulation = Modulation(c, ctx, 1)
        raw_up, raw_down = c.sb("raw_up", [P, E * KC, P], ctx=ctx), c.sb("raw_down", [P, E, D], ctx=ctx)
        up_loaded, down_loaded = c.sem("raw_up_loaded"), c.sem("raw_down_loaded")
        heads_done, up_split, down_split = c.sem("e0_w_heads"), c.sem("e0_w_up_split"), c.sem("e0_w_down_split")
        logits, coef = c.logits[:].rearrange("p b t e -> p (b t) e"), c.coef[:].rearrange("p b t e -> p (b t) e")

        def spread(v):
            return v[:].unsqueeze(2).broadcast_to([P, N, E])

        with nc.Block() as block:
            @block.sync
            def _(sp):
                modulation.load(sp, a)
                sp.dma_start(raw_up[:], a["L0_ffn_w1"].rearrange("e (k p) n -> p (e k) n", p=P)).then_inc(up_loaded, 16)
                sp.dma_start(raw_down[:], a["L0_ffn_w2"].rearrange("e p n -> p e n")).then_inc(down_loaded, 16)
                sp.dma_start(c.gate[:], c.gates_dram[0, 1].unsqueeze(0).broadcast_to([P, B, D])).then_inc(c.constants, 16)
                modulation.store_rows(sp)

            @block.tensor
            def _(pe):
                modulation.products(pe)

            @block.scalar
            def _(act):
                modulation.silu(act)
                act.wait_ge(shifted_done, 1)
                nc.scalar.activation(power[:], shifted[:], ACT.Exp).then_inc(power_done, 1)
                act.wait_ge(up_loaded, 16)
                nc.scalar.activation(w_up[:, HEAD], raw_up[:], ACT.Identity).then_inc(heads_done, 1)
                act.wait_ge(down_loaded, 16)
                nc.scalar.activation(w_down[:, HEAD], raw_down[:], ACT.Identity).then_inc(heads_done, 1)

            @block.gpsimd
            def _(pool):
                pool.memset(better[:], 0.0).then_inc(better_zeroed, 1)
                pool.wait_ge(heads_done, 1)
                nc.gpsimd.tensor_tensor(w_up[:, REST], raw_up[:], w_up[:, HEAD].bitcast(F32), ALU.subtract).then_inc(up_split, 1)

            @block.vector
            def _(dve):
                nc.vector.tensor_reduce(peak[:], logits, AX, ALU.max)
                dve.drain()
                nc.vector.tensor_tensor(shifted[:], logits, spread(peak), ALU.subtract).then_inc(shifted_done, 1)
                dve.wait_ge(power_done, 1)
                nc.vector.tensor_reduce(total[:], power[:], AX, ALU.add)
                dve.drain()
                nc.vector.reciprocal(inv_total[:], total[:])
                dve.drain()
                nc.vector.tensor_tensor(gates[:], power[:], spread(inv_total), ALU.mult)
                dve.drain()
                dve.wait_ge(better_zeroed, 1)
                choose(nc, dve, gates[:], better, count[:], chosen[:], weight_sum[:], coef)
                nc.vector.tensor_tensor(coef, coef, spread(weight_sum), ALU.mult)
                dve.wait_ge(heads_done, 2)
                nc.vector.tensor_tensor(w_down[:, REST], raw_down[:], w_down[:, HEAD].bitcast(F32),
                                        ALU.subtract).then_inc(down_split, 1)
                modulation.keep(dve)


def gelu_experts_part(c, a, w_up, w_down, load_next_weights, next_weights):
    nc = c.nc
    with ExitStack() as ctx:
        def sb(name, shape, dt=F32):
            return c.sb("e0_" + name, shape, dt, ctx)

        b_up, b_down, ones, eps = sb("b_up", [P, E]), sb("b_down", [E, D]), sb("ones", [P, 1]), sb("eps", [P, NT])
        norm = Norm(c, ctx, "e0_norm", eps[:])
        h_parts, coef = sb("h_parts", [P, 2, KC, S], F32R), sb("coef", [P, NT, E])
        coefT, acc, y = sb("coefT", [E, S]), sb("acc", [P, NT, D]), sb("y", [P, NT, D])
        g, hidden = sb("g", [P, 2, S]), sb("hidden", [P, 2, 2, S], F32R)
        xn, squares = sb("xn", [P, NT, D]), sb("squares", [P, KC, S])
        tp_ps = c.psum("e0_tp_ps", 2, ctx)
        up_ps = c.psum("e0_up_ps", 2, ctx)
        down_ps = [c.psum(f"e0_down_ps_{n}", 2, ctx) for n in range(2)]
        (tables_loaded, tables_set, head_done, h_split, coef_done, coefT_done, coefT_kept, bias_done, acc_set, up_done,
         g_done, hidden_split, down_done, acc_done, y_done, x_done, xn_done, xT_done, next_done, squares_done, kept, rms_done) = (
            c.sem("e0_" + n) for n in
            ("tables_loaded tables_set head_done h_split coef_done coefT_done coefT_kept bias_done acc_set up_done "
             "g_done hidden_split down_done acc_done y_done x_done xn_done xT_done next_done squares_done kept rms_done").split())

        with nc.Block() as block:
            @block.sync
            def _(sp):
                sp.dma_start(b_up[:], a["e0_b_up"]).then_inc(tables_loaded, 16)
                sp.dma_start(b_down[:], a["L0_ffn_b2"]).then_inc(tables_loaded, 16)
                load_next_weights(sp)

            @block.gpsimd
            def _(pool):
                def take_coef(b):
                    if not is_first(b):
                        pool.wait_ge(c.start, 1)
                        pool.wait_ge(coefT_done, b)
                    nc.gpsimd.tensor_copy(coef[:], c.coef[:, b]).then_inc(coef_done, 1)

                def invert_rms(b):
                    pool.wait_ge(c.start, 1)
                    pool.wait_ge(kept, b + 1)
                    nc.gpsimd.tensor_tensor(c.inv_rms[:, b], c.mean_square[:, b], c.neg_half[:, 0:NT], ALU.pow
                                            ).then_inc(rms_done, 1)

                pool.memset(ones[:], 1.0)
                pool.memset(eps[:], LN_EPS).then_inc(tables_set, 1)
                pool.wait_ge(tables_set, 1)
                take_coef(0)
                next_weights(pool)
                take_coef(1)
                norm.invert(pool, 0)
                with pool.Fori(1, B - 1) as b:
                    take_coef(b + 1)
                    invert_rms(b - 1)
                    norm.invert(pool, b)
                invert_rms(B - 2)
                norm.invert(pool, B - 1)
                invert_rms(B - 1)

            @block.tensor
            def _(pe):
                def up(b, e):
                    if e == 0:
                        pe.wait_ge(h_split, b + 1)
                    if e >= 2 or not is_first(b):
                        pe.wait_ge(g_done, E * b + e - 1)
                    product(nc.tensor, up_ps[:, e % 2, :],
                            [(lambda i, k=k: w_up[:, i, e * KC + k, :],
                              lambda j, k=k: h_parts[:, j, k, :]) for k in range(KC)]).then_inc(up_done, 1)

                def down(b, e):
                    pe.wait_ge(hidden_split, E * b + e + 1)
                    if e >= 2 or not is_first(b):
                        pe.wait_ge(acc_done, E * b + e - 1)
                    for t in range(NT):
                        last = product(nc.tensor, rows_of(down_ps[e % 2], t),
                                       [(lambda i: hidden[:, i, e % 2, t * P:(t + 1) * P],
                                         lambda j: w_down[:, j, e, :])])
                    last.then_inc(down_done, 1)

                def coef_by_expert(b):
                    pe.wait_ge(coef_done, b + 1)
                    for t in range(NT):
                        last = nc.tensor.transpose(tp_ps[0:E, 0, t * P:(t + 1) * P], coef[:, t, :], c.ident[:])
                    last.then_inc(coefT_done, 1)

                def biases(b):
                    pe.wait_ge(coefT_kept, b + 1)
                    for t in range(NT):
                        last = nc.tensor.matmul(rows_of(tp_ps, t), coefT[:, t * P:(t + 1) * P], b_down[:], start=True,
                                                stop=True)
                    last.then_inc(bias_done, 1)

                def next_by_feature(b):
                    pe.wait_ge(xn_done, b + 1)
                    transposes(nc.tensor, c, tp_ps, xn).then_inc(xT_done, 1)

                def sum_squares(b):
                    pe.wait_ge(next_done, b + 1)
                    for t in range(NT):
                        for k in range(KC):
                            last = nc.tensor.matmul(tp_ps[:, 0, t:t + 1], squares[:, k, t * P:(t + 1) * P], ones[:],
                                                    start=k == 0, stop=k == KC - 1)
                    last.then_inc(squares_done, 1)

                def iteration(b, first=False, final=False):
                    for e in range(E):
                        if e + 1 < E:
                            up(b, e + 1)
                        if e == 4 and not first:
                            next_by_feature(b - 1)
                        down(b, e)
                        if e == 6 and not first:
                            sum_squares(b - 1)
                    if not final:
                        if not first:
                            pe.wait_ge(kept, b)
                        coef_by_expert(b + 1)
                        up(b + 1, 0)
                        biases(b + 1)

                pe.wait_ge(tables_loaded, 32)
                pe.wait_ge(tables_set, 1)
                coef_by_expert(0)
                up(0, 0)
                biases(0)
                iteration(0, first=True)
                with pe.Fori(1, B - 1) as b:
                    iteration(b)
                iteration(B - 1, final=True)
                next_by_feature(B - 1)
                sum_squares(B - 1)

            @block.scalar
            def _(act):
                def head_of_h(b):
                    if not is_first(b):
                        act.wait_ge(c.start, 1)
                        act.wait_ge(up_done, E * b)
                    nc.scalar.activation(h_parts[:, HEAD], c.hT[:, :, b, :], ACT.Identity).then_inc(head_done, 1)

                def keep_coefT(b):
                    act.wait_ge(coefT_done, b + 1)
                    if not is_first(b):
                        act.wait_ge(bias_done, b)
                    nc.scalar.activation(coefT[:], tp_ps[0:E, 0, :], ACT.Identity).then_inc(coefT_kept, 1)

                def gelu(b, e):
                    act.wait_ge(up_done, E * b + e + 1)
                    if e >= 2 or not is_first(b):
                        act.wait_ge(down_done, E * b + e - 1)
                    nc.scalar.activation(g[:, e % 2, :], up_ps[:, e % 2, :], ACT.Gelu, bias=b_up[:, e:e + 1])
                    nc.scalar.activation(hidden[:, HEAD, e % 2, :], up_ps[:, e % 2, :], ACT.Gelu,
                                         bias=b_up[:, e:e + 1]).then_inc(g_done, 1)

                def set_acc(b, first):
                    act.wait_ge(bias_done, b + 1)
                    if not first:
                        act.wait_ge(y_done, b)
                    nc.scalar.activation(acc[:].rearrange("p t d -> p (t d)"), tp_ps[:].rearrange("p n s -> p (n s)"),
                                         ACT.Identity).then_inc(acc_set, 1)

                def modulate(b, k):
                    act.wait_ge(c.start, 1)
                    act.wait_ge(xT_done, b + 1)
                    shift, scale = c.mod[:, 1, SA, k, bass.ds(b, 1)], c.mod[:, 1, CA, k, bass.ds(b, 1)]
                    nc.scalar.activation(c.hT[:, k, b, :], tp_ps[:, k, :], ACT.Identity, bias=shift, scale=scale)
                    last = nc.scalar.activation(squares[:, k, :], tp_ps[:, k, :], ACT.Square, bias=shift, scale=scale)
                    if k == KC - 1:
                        last.then_inc(next_done, 1)

                def iteration(b, first=False, final=False):
                    for e in range(E):
                        gelu(b, e)
                        if e == 0:
                            set_acc(b, first)
                        if e in (5, 6) and not first:
                            modulate(b - 1, e - 5)
                    if not final:
                        head_of_h(b + 1)
                        keep_coefT(b + 1)

                act.wait_ge(tables_loaded, 32)
                head_of_h(0)
                keep_coefT(0)
                iteration(0, first=True)
                with act.Fori(1, B - 1) as b:
                    iteration(b)
                iteration(B - 1, final=True)
                for k in range(KC):
                    modulate(B - 1, k)

            @block.vector
            def _(dve):
                def rest_of_h(b):
                    dve.wait_ge(head_done, b + 1)
                    nc.vector.tensor_tensor(h_parts[:, REST], c.hT[:, :, b, :], h_parts[:, HEAD].bitcast(F32),
                                            ALU.subtract).then_inc(h_split, 1)

                def rest_hidden(b, e):
                    dve.wait_ge(g_done, E * b + e + 1)
                    nc.vector.tensor_tensor(hidden[:, REST, e % 2, :], g[:, e % 2, :],
                                            hidden[:, HEAD, e % 2, :].bitcast(F32), ALU.subtract).then_inc(hidden_split, 1)

                def accumulate(b, e):
                    if e == 0:
                        dve.wait_ge(acc_set, b + 1)
                    else:
                        dve.wait_ge(acc_done, E * b + e)
                    dve.wait_ge(down_done, E * b + e + 1)
                    for t in range(NT):
                        last = nc.vector.scalar_tensor_tensor(out=acc[:, t, :], in0=rows_of(down_ps[e % 2], t),
                                                              scalar=c.coef[:, b, t, e:e + 1],
                                                              in1=acc[:, t, :],
                                                              op0=ALU.mult, op1=ALU.add)
                    last.then_inc(acc_done, 1)

                def gate_rows(b):
                    dve.wait_ge(acc_done, E * (b + 1))
                    nc.vector.tensor_tensor(y[:], acc[:], c.gate[:, b, :].unsqueeze(1).broadcast_to([P, NT, D]),
                                            ALU.mult).then_inc(y_done, 1)

                def update_x(b):
                    dve.wait_ge(c.start, 1)
                    dve.wait_ge(y_done, b + 1)
                    nc.vector.tensor_tensor(c.x[:, b], c.x[:, b], y[:], ALU.add).then_inc(x_done, 1)

                def moments(b):
                    dve.wait_ge(c.start, 1)
                    dve.wait_ge(x_done, b + 1)
                    norm.gather(lambda t: c.x[:, b, t, :])
                    norm.aggregate(dve, b)

                def normalise(b):
                    norm.apply(dve, b, xn, lambda t: c.x[:, b, t, :], xn_done)

                def keep_sums(b):
                    dve.wait_ge(c.start, 1)
                    dve.wait_ge(squares_done, b + 1)
                    nc.vector.tensor_scalar(c.mean_square[:, b], tp_ps[:, 0, 0:NT], 1.0 / D, RMS_EPS, ALU.mult,
                                            ALU.add).then_inc(kept, 1)

                TAIL = {0: update_x, 1: moments, 2: normalise, 6: keep_sums}

                def iteration(b, first=False, final=False):
                    rest_hidden(b, 0)
                    for e in range(E):
                        if e + 1 < E:
                            rest_hidden(b, e + 1)
                        if e == E - 2 and not final:
                            rest_of_h(b + 1)
                        accumulate(b, e)
                        if e in TAIL and not first:
                            TAIL[e](b - 1)
                    gate_rows(b)

                dve.wait_ge(c.constants, 32)
                rest_of_h(0)
                iteration(0, first=True)
                with dve.Fori(1, B - 1) as b:
                    iteration(b)
                iteration(B - 1, final=True)
                update_x(B - 1)
                moments(B - 1)
                normalise(B - 1)
                keep_sums(B - 1)


def attention_part(c, a, w_qk, w_v, w_o):
    nc = c.nc
    PAIRS = H // 2
    VW = 3 * HD + 1
    with ExitStack() as ctx:
        def sb(name, shape, dt=F32):
            return c.sb("at_" + name, shape, dt, ctx)

        qk_bias, v_bias, o_bias = sb("qk_bias", [P, 2 * D]), sb("v_bias", [P, D]), sb("o_bias", [P, D])
        cos, sin, router_w = sb("cos", [P, NT, HD]), sb("sin", [P, NT, HD]), sb("router_w", [P, KC, E])
        eps = sb("eps", [P, NT])
        norm = Norm(c, ctx, "at_norm", eps[:])
        h_parts = sb("h_parts", [P, 2, KC, S], F32R)
        qk, turned, rotated = sb("qk", [P, 2, 2 * D]), sb("turned", [P, 2, 2 * D]), sb("rotated", [P, 2, 2 * D])
        wide = sb("wide", [P, 2, 4 * S])
        qkT = sb("qkT", [P, 2, PAIRS, S], F32R)
        v = sb("v", [P, NT, D])
        v_parts = sb("v_parts", [P, NT, H, VW], BF16)
        sig_head_mem, sig_rest_mem = sb("sig_head", [P, 2 * NT * D]), sb("sig_rest", [P, 2 * NT * D])
        sig_head = sig_head_mem[:].bitcast(F16).rearrange("p (u t s) -> p u t s", u=2, t=NT)
        sig_rest = sig_rest_mem[:].bitcast(F16).rearrange("p (u t s) -> p u t s", u=2, t=NT)
        v_left = sig_head_mem[:, 0:NT * D].rearrange("p (t d) -> p t d", t=NT)
        gated_rows = sig_rest_mem[:, 0:NT * D].rearrange("p (t d) -> p t d", t=NT)
        h = sig_rest_mem[:, NT * D:].rearrange("p (k s) -> p k s", k=KC)
        o_sum, denom, inv_denom = sb("o_sum", [P, 2, 2, NT, HD]), sb("denom", [P, 2, 2 * NT]), sb("inv_denom", [P, 2, 2 * NT])
        o_parts = sb("o_parts", [P, 2, KC, S], F32R)
        rows, gate_bias = sb("rows", [P, NT, D]), sb("gate_bias", [P, D])
        a_ps = c.psum("at_a_ps", 2, ctx)
        sc_ps = c.psum("at_sc_ps", 4, ctx)
        o_ps = c.psum("at_o_ps", 2, ctx)
        (tables_loaded, tables_set, head_done, h_split, qk_done, v_done, qk_scaled, v_kept,
         cos_done, rot_done, sin_done, qk_head_done, qk_split, keysT_done, keys_kept, qkT_done, qkT_kept, v1_done, v_split, score_done, sig_done, sig_head_done,
         sig_split, av_done, sum_done, inv_done, heads_done, oT_done, o_head_done, o_split, proj_done, gated,
         x_biased, x_done, xn_done, xT_done, next_done, hT_kept, logits_done, logits_kept, gb_done) = (
            c.sem("at_" + n) for n in
            ("tables_loaded tables_set head_done h_split qk_done v_done qk_scaled v_kept "
             "cos_done rot_done sin_done qk_head_done qk_split keysT_done keys_kept qkT_done qkT_kept v1_done v_split score_done sig_done sig_head_done "
             "sig_split av_done sum_done inv_done heads_done oT_done o_head_done o_split proj_done gated "
             "x_biased x_done xn_done xT_done next_done hT_kept logits_done logits_kept gb_done").split())
        N_TABLES = 16 * 6

        def by_head(t):
            return wide[:, t % 2, :].rearrange("p (i h c d) -> p i h c d", i=2, h=H, c=4)

        def heads_of(v):
            return v.rearrange("p (h d) -> p h d", d=HD)

        with nc.Block() as block:
            @block.sync
            def _(sp):
                for name, to, n in (("qk_bias", qk_bias, 2 * D), ("L1_attn_v_b", v_bias, D), ("L1_attn_o_b", o_bias, D)):
                    sp.dma_start(to[:], a[name].unsqueeze(0).broadcast_to([P, n])).then_inc(tables_loaded, 16)
                sp.dma_start(cos[:], a["cos"]).then_inc(tables_loaded, 16)
                sp.dma_start(sin[:], a["sin"]).then_inc(tables_loaded, 16)
                sp.dma_start(router_w[:], a["router_w"].rearrange("(k p) e -> p k e", p=P)).then_inc(tables_loaded, 16)
                sp.dma_start(c.gate[:], c.gates_dram[1, 0].unsqueeze(0).broadcast_to([P, B, D])).then_inc(c.constants, 16)

            @block.gpsimd
            def _(pool):
                vh = v[:].rearrange("p t (h d) -> p (t h) d", d=HD)
                left = v_left.rearrange("p t (h d) -> p (t h) d", d=HD)
                v_sources = (vh, left, left)

                def v_part(part):
                    return v_parts[:, :, :, part * HD:(part + 1) * HD].rearrange("p t h d -> p (t h) d")

                def bias_x(b):
                    nc.gpsimd.tensor_tensor(gate_bias[:], c.gate[:, b, :], o_bias[:], ALU.mult).then_inc(gb_done, 1)
                    pool.wait_ge(c.start, 1)
                    pool.wait_ge(gb_done, b + 1)
                    nc.gpsimd.tensor_tensor(c.x[:, b], c.x[:, b], gate_bias[:].unsqueeze(1).broadcast_to([P, NT, D]),
                                            ALU.add).then_inc(x_biased, 1)

                def times_cos(b, t):
                    pool.wait_ge(qk_scaled, NT * b + t + 1)
                    nc.gpsimd.tensor_tensor(heads_of(rotated[:, t % 2, :]), heads_of(qk[:, t % 2, :]),
                                            cos[:, t, :].unsqueeze(1).broadcast_to([P, 2 * H, HD]),
                                            ALU.mult).then_inc(cos_done, 1)

                def keep_v_part(b, part):
                    if part == 0:
                        pool.wait_ge(v_kept, 2 * (b + 1))
                        if not is_first(b):
                            pool.wait_ge(av_done, H * b)
                    else:
                        pool.wait_ge(v1_done, 2 * b + part)
                    pool.sem_inc(c.passed, 1)
                    nc.gpsimd.tensor_scalar(v_part(part), v_sources[part], 1.0, 1.0, ALU.mult, ALU.mult).then_inc(v_split, 1)

                def left_of_v(b, part):
                    pool.wait_ge(v_split, 3 * b + part + 1)
                    nc.gpsimd.tensor_tensor(left, v_sources[part], v_part(part), ALU.subtract).then_inc(v1_done, 1)

                def sigmoid_heads(b, n):
                    for j in range(2):
                        if j == 0 and n == 0:
                            pool.wait_ge(v_split, 3 * (b + 1))
                        if j == 0 and n >= 2:
                            pool.wait_ge(av_done, H * b + n - 1)
                        pool.wait_ge(sig_done, 2 * (H * b + n) + j + 1)
                        pool.sem_inc(c.passed, 1)
                        nc.gpsimd.tensor_scalar(sig_head[:, n % 2, 2 * j:2 * j + 2].rearrange("p t s -> p (t s)"),
                                                wide[:, n % 2, 2 * j * S:(2 * j + 2) * S],
                                                SIG_SCALE, 1.0, ALU.mult, ALU.mult).then_inc(sig_head_done, 1)

                def iteration(b, after):
                    for n in range(H):
                        sigmoid_heads(b, n)
                        if n == 6:
                            bias_x(b)
                        if after is not None and n in (10, 11):
                            times_cos(after, n - 10)
                    if after is not None:
                        keep_v_part(after, 0)
                        left_of_v(after, 0)
                        times_cos(after, 2)
                        keep_v_part(after, 1)
                        times_cos(after, 3)
                        left_of_v(after, 1)
                    norm.invert(pool, b)
                    if after is not None:
                        keep_v_part(after, 2)

                pool.memset(eps[:], LN_EPS)
                pool.memset(v_parts[:, :, :, VW - 1], 1.0).then_inc(tables_set, 1)
                pool.wait_ge(tables_loaded, N_TABLES)
                pool.wait_ge(c.constants, 48)
                pool.wait_ge(tables_set, 1)
                for t in range(NT):
                    times_cos(0, t)
                for part in range(3):
                    keep_v_part(0, part)
                    if part < 2:
                        left_of_v(0, part)
                with pool.Fori(0, B - 1) as b:
                    iteration(b, b + 1)
                iteration(B - 1, None)

            @block.tensor
            def _(pe):
                def values(b, t):
                    if t == 0:
                        pe.wait_ge(h_split, b + 1)
                    last = product(nc.tensor, rows_of(a_ps, t),
                                   [(lambda i, k=k: h_parts[:, i, k, t * P:(t + 1) * P], lambda j, k=k: w_v[:, j, k, :])
                                    for k in range(KC)])
                    if t % 2:
                        last.then_inc(v_done, 1)

                def queries_keys(b, t):
                    if t < 2:
                        pe.wait_ge(v_kept, 2 * b + t + 1)
                    product(nc.tensor, a_ps[:, t % 2, :],
                            [(lambda i, k=k: h_parts[:, i, k, t * P:(t + 1) * P], lambda j, k=k: w_qk[:, j, k, :])
                             for k in range(KC)]).then_inc(qk_done, 1)

                def by_feature(b, t, i):
                    if i == 1:
                        pe.wait_ge(qk_split, NT * b + t + 1)
                    if t:
                        pe.wait_ge(keys_kept if i else qkT_kept, NT * b + t)
                    for pair in range(PAIRS):
                        n = i * PAIRS + pair
                        last = nc.tensor.transpose(sc_ps[:, n // 4, (n % 4) * P:(n % 4 + 1) * P],
                                                   wide[:, t % 2, n * P:(n + 1) * P], c.ident[:])
                    last.then_inc(keysT_done if i else qkT_done, 1)

                def scores(b, n):
                    base, pair = 64 * (n % 2), n // 2
                    if n == 0:
                        pe.wait_ge(qkT_kept, NT * (b + 1))
                    for j in range(2):
                        if n >= 1:
                            pe.wait_ge(sig_done, 2 * (H * b + n) + j - 1)
                        for k in (2 * j, 2 * j + 1):
                            last = nc.tensor.matmul(sc_ps[:, k, :], qkT[base:base + 64, 1, pair, k * P:(k + 1) * P],
                                                    qkT[base:base + 64, 0, pair, :], start=True, stop=True)
                        last.then_inc(score_done, 1)

                def attend(b, n):
                    if n == 0:
                        pe.wait_ge(v_split, 3 * (b + 1))
                    pe.wait_ge(sig_split, 2 * (H * b + n + 1))
                    if n % 2 == 0 and n >= 4:
                        pe.wait_ge(heads_done, PAIRS * b + n // 2 - 1)
                    for t in range(NT):
                        at = (n % 2) * 256 + t * 64
                        for k in range(NT):
                            for part in (sig_head, sig_rest):
                                last = nc.tensor.matmul(o_ps[:, (n // 2) % 2, at:at + VW],
                                                        part[:, n % 2, k, t * P:(t + 1) * P], v_parts[:, k, n, :],
                                                        start=k == 0 and part is sig_head,
                                                        stop=k == NT - 1 and part is sig_rest)
                    last.then_inc(av_done, 1)

                def output_by_feature(b):
                    pe.wait_ge(heads_done, PAIRS * (b + 1))
                    transposes(nc.tensor, c, sc_ps, rows).then_inc(oT_done, 1)

                def project(b):
                    for t in range(NT):
                        last = product(nc.tensor, rows_of(o_ps, t),
                                       [(lambda i, k=k: o_parts[:, i, k, t * P:(t + 1) * P],
                                         lambda j, k=k: w_o[:, j, k, :]) for k in range(KC)])
                    last.then_inc(proj_done, 1)

                def next_by_feature(b):
                    pe.wait_ge(xn_done, b + 1)
                    transposes(nc.tensor, c, o_ps, rows).then_inc(xT_done, 1)

                def route(b):
                    pe.wait_ge(next_done, b + 1)
                    for t in range(NT):
                        for k in range(KC):
                            last = nc.tensor.matmul(o_ps[:, 0, t * E:(t + 1) * E], h[:, k, t * P:(t + 1) * P],
                                                    router_w[:, k, :], start=k == 0, stop=k == KC - 1)
                    last.then_inc(logits_done, 1)

                def early(b, n):
                    if 2 <= n < 6:
                        values(b, n - 2)
                    elif n in (7, 8):
                        queries_keys(b, n - 7)

                def iteration(b, after):
                    for n in range(H):
                        if n + 2 < H:
                            scores(b, n + 2)
                        attend(b, n)
                        if after is not None:
                            early(after, n)
                    if after is None:
                        output_by_feature(b)
                        pe.wait_ge(o_split, b + 1)
                        project(b)
                        next_by_feature(b)
                        route(b)
                        return
                    by_feature(after, 0, 1)
                    output_by_feature(b)
                    queries_keys(after, 2)
                    pe.wait_ge(o_split, b + 1)
                    by_feature(after, 0, 0)
                    project(b)
                    by_feature(after, 1, 1)
                    by_feature(after, 1, 0)
                    queries_keys(after, 3)
                    for t in (2, 3):
                        by_feature(after, t, 1)
                        by_feature(after, t, 0)
                    next_by_feature(b)
                    scores(after, 0)
                    route(b)
                    scores(after, 1)
                    pe.wait_ge(logits_kept, b + 1)

                for t in range(NT):
                    values(0, t)
                pe.wait_ge(tables_loaded, N_TABLES)
                pe.wait_ge(tables_set, 1)
                for t in range(NT):
                    if t >= 2:
                        by_feature(0, t - 2, 1)
                        by_feature(0, t - 2, 0)
                    queries_keys(0, t)
                for t in (2, 3):
                    by_feature(0, t, 1)
                    by_feature(0, t, 0)
                scores(0, 0)
                scores(0, 1)
                with pe.Fori(0, B - 1) as b:
                    iteration(b, b + 1)
                iteration(B - 1, None)

            @block.scalar
            def _(act):
                def head_of_h(b):
                    if not is_first(b):
                        act.wait_ge(c.start, 1)
                        act.wait_ge(qk_done, NT * b)
                    nc.scalar.activation(h_parts[:, HEAD], c.hT[:, :, b, :], ACT.Copy).then_inc(head_done, 1)

                def queries_keys_heads(b, t):
                    act.wait_ge(rot_done, NT * b + t + 1)
                    if t >= 2:
                        act.wait_ge(qkT_done, NT * b + t - 1)
                    elif not is_first(b):
                        act.wait_ge(sig_split, 2 * (H * b - 1 + t))
                    src = rotated[:, t % 2, :].rearrange("p (i h d) -> p i h d", i=2, d=HD)
                    to = by_head(t).bitcast(F32R)
                    nc.scalar.activation(to[:, 0, :, 0:3:2, :], src[:, 0].unsqueeze(2).broadcast_to([P, H, 2, HD]),
                                         ACT.Copy)
                    nc.scalar.activation(to[:, 1, :, 0:2, :], src[:, 1].unsqueeze(2).broadcast_to([P, H, 2, HD]),
                                         ACT.Copy).then_inc(qk_head_done, 1)

                def keep_by_feature(b, t):
                    for i, made, kept in ((1, keysT_done, keys_kept), (0, qkT_done, qkT_kept)):
                        act.wait_ge(made, NT * b + t + 1)
                        for half in range(2):
                            last = nc.scalar.activation(
                                qkT[:, i, half * 4:half * 4 + 4, t * P:(t + 1) * P],
                                sc_ps[:, 2 * i + half, :].rearrange("p (g s) -> p g s", g=4), ACT.Copy)
                        last.then_inc(kept, 1)

                def sigmoids(b, n):
                    for j in range(2):
                        if n >= 2:
                            act.wait_ge(sig_split, 2 * (H * b + n - 2) + j + 1)
                        act.wait_ge(score_done, 2 * (H * b + n) + j + 1)
                        nc.scalar.activation(wide[:, n % 2, j * 2 * S:(j + 1) * 2 * S],
                                             sc_ps[:, 2 * j:2 * j + 2, :].rearrange("p n s -> p (n s)"),
                                             ACT.Sigmoid, scale=float(HD) ** -0.5).then_inc(sig_done, 1)

                def output_head(b):
                    act.wait_ge(oT_done, b + 1)
                    nc.scalar.activation(o_parts[:, HEAD], sc_ps[:, 0:KC, :], ACT.Copy).then_inc(o_head_done, 1)

                def modulate(b):
                    act.wait_ge(c.start, 1)
                    act.wait_ge(xT_done, b + 1)
                    for k in range(KC):
                        last = nc.scalar.activation(h[:, k, :], o_ps[:, k, :], ACT.Identity,
                                                    bias=c.mod[:, 1, SB, k, bass.ds(b, 1)],
                                                    scale=c.mod[:, 1, CB, k, bass.ds(b, 1)])
                    last.then_inc(next_done, 1)

                def iteration(b, after):
                    for n in range(H):
                        sigmoids(b, n)
                        if after is not None and n == 1:
                            head_of_h(after)
                    if after is not None:
                        queries_keys_heads(after, 0)
                    output_head(b)
                    if after is not None:
                        queries_keys_heads(after, 1)
                        keep_by_feature(after, 0)
                        queries_keys_heads(after, 2)
                        keep_by_feature(after, 1)
                        queries_keys_heads(after, 3)
                        keep_by_feature(after, 2)
                        keep_by_feature(after, 3)
                    modulate(b)

                head_of_h(0)
                for t in range(NT):
                    queries_keys_heads(0, t)
                    keep_by_feature(0, t)
                with act.Fori(0, B - 1) as b:
                    iteration(b, b + 1)
                iteration(B - 1, None)

            @block.vector
            def _(dve):
                def rest_of_h(b):
                    dve.wait_ge(head_done, b + 1)
                    nc.vector.tensor_tensor(h_parts[:, REST], c.hT[:, :, b, :], h_parts[:, HEAD].bitcast(F32),
                                            ALU.subtract).then_inc(h_split, 1)

                def rotate(b, t):
                    dve.wait_ge(c.start, 1)
                    dve.wait_ge(qk_done, NT * b + t + 1)
                    buf = t % 2
                    nc.vector.scalar_tensor_tensor(out=qk[:, buf, :], in0=a_ps[:, buf, :],
                                                   scalar=c.inv_rms[:, b, t:t + 1], in1=qk_bias[:], op0=ALU.mult,
                                                   op1=ALU.add).then_inc(qk_scaled, 1)
                    dve.wait_ge(qk_scaled, NT * b + t + 1)
                    src = qk[:, buf, :].rearrange("p (h d two) -> p h d two", two=2, d=HD // 2)
                    to = turned[:, buf, :].rearrange("p (h d two) -> p h d two", two=2, d=HD // 2)
                    sines = sin[:, t, :].rearrange("p (d two) -> p d two", two=2)
                    for i in range(2):
                        last = nc.vector.tensor_tensor(to[:, :, :, i], src[:, :, :, 1 - i],
                                                       sines[:, :, i].unsqueeze(1).broadcast_to([P, 2 * H, HD // 2]),
                                                       ALU.mult)
                    last.then_inc(sin_done, 1)

                def add_turned(b, t):
                    buf = t % 2
                    dve.wait_ge(sin_done, NT * b + t + 1)
                    dve.wait_ge(cos_done, NT * b + t + 1)
                    nc.vector.tensor_tensor(rotated[:, buf, :], rotated[:, buf, :], turned[:, buf, :],
                                            ALU.add).then_inc(rot_done, 1)

                def keep_values(b, half):
                    dve.wait_ge(v_done, 2 * b + half + 1)
                    nc.vector.tensor_tensor(v[:, 2 * half:2 * half + 2, :], a_ps[:, half, :].rearrange("p (t d) -> p t d", t=2),
                                            v_bias[:].unsqueeze(1).broadcast_to([P, 2, D]), ALU.add).then_inc(v_kept, 1)

                def rests(b, t):
                    dve.wait_ge(qk_head_done, NT * b + t + 1)
                    src = rotated[:, t % 2, :].rearrange("p (i h d) -> p i h d", i=2, d=HD)
                    to, of = by_head(t).bitcast(F32R), by_head(t)
                    nc.vector.tensor_tensor(to[:, 0, :, 1:4:2, :], src[:, 0].unsqueeze(2).broadcast_to([P, H, 2, HD]),
                                            of[:, 0, :, 0:3:2, :], ALU.subtract)
                    nc.vector.tensor_tensor(to[:, 1, :, 2:4, :], src[:, 1].unsqueeze(2).broadcast_to([P, H, 2, HD]),
                                            of[:, 1, :, 0:2, :], ALU.subtract).then_inc(qk_split, 1)

                def sigmoid_rests(b, n):
                    for j in range(2):
                        dve.wait_ge(sig_head_done, 2 * (H * b + n) + j + 1)
                        nc.vector.scalar_tensor_tensor(out=sig_rest[:, n % 2, 2 * j:2 * j + 2].rearrange("p t s -> p (t s)"),
                                                       in0=wide[:, n % 2, 2 * j * S:(2 * j + 2) * S], scalar=SIG_SCALE,
                                                       in1=sig_head[:, n % 2, 2 * j:2 * j + 2].rearrange("p t s -> p (t s)"),
                                                       op0=ALU.mult, op1=ALU.subtract).then_inc(sig_split, 1)

                def sum_parts(b, pair):
                    dve.wait_ge(av_done, H * b + 2 * pair + 2)
                    got = o_ps[:, pair % 2, :].rearrange("p (n w) -> p n w", w=64)
                    buf = pair % 2
                    nc.vector.tensor_reduce(o_sum[:, buf].rearrange("p n t d -> p (n t) d"),
                                            got[:, :, 0:3 * HD].rearrange("p n (c d) -> p n d c", c=3), AX, ALU.add)
                    nc.vector.tensor_scalar(denom[:, buf, :], got[:, :, 3 * HD], SUM_EPS * SIG_SCALE, None,
                                            ALU.add).then_inc(sum_done, 1)
                    dve.wait_ge(sum_done, PAIRS * b + pair + 1)
                    nc.vector.reciprocal(inv_denom[:, buf, :], denom[:, buf, :]).then_inc(inv_done, 1)
                    dve.wait_ge(inv_done, PAIRS * b + pair + 1)
                    to = rows[:, :, 2 * pair * HD:(2 * pair + 2) * HD].rearrange("p t (n d) -> p n t d", n=2)
                    for n in range(2):
                        last = nc.vector.tensor_tensor(to[:, n], o_sum[:, buf, n],
                                                       inv_denom[:, buf, n * NT:(n + 1) * NT].unsqueeze(2).broadcast_to(
                                                           [P, NT, HD]), ALU.mult)
                    last.then_inc(heads_done, 1)

                def output_rest(b):
                    dve.wait_ge(o_head_done, b + 1)
                    nc.vector.tensor_tensor(o_parts[:, REST], sc_ps[:, 0:KC, :], o_parts[:, HEAD].bitcast(F32),
                                            ALU.subtract).then_inc(o_split, 1)

                def gate_rows(b):
                    dve.wait_ge(proj_done, b + 1)
                    nc.vector.tensor_tensor(gated_rows, o_ps[:].rearrange("p n (t d) -> p (n t) d", d=D),
                                            c.gate[:, b, :].unsqueeze(1).broadcast_to([P, NT, D]),
                                            ALU.mult).then_inc(gated, 1)

                def update_x(b):
                    dve.wait_ge(c.start, 1)
                    dve.wait_ge(gated, b + 1)
                    dve.wait_ge(x_biased, b + 1)
                    nc.vector.tensor_tensor(c.x[:, b], c.x[:, b], gated_rows, ALU.add).then_inc(x_done, 1)

                def moments(b):
                    dve.wait_ge(c.start, 1)
                    dve.wait_ge(x_done, b + 1)
                    norm.gather(lambda t: c.x[:, b, t, :])
                    norm.aggregate(dve, b)

                def normalise(b):
                    norm.apply(dve, b, rows, lambda t: c.x[:, b, t, :], xn_done)

                def keep_hT(b):
                    dve.wait_ge(c.start, 1)
                    dve.wait_ge(next_done, b + 1)
                    nc.vector.tensor_copy(c.hT[:, :, b, :], h).then_inc(hT_kept, 1)

                def keep_logits(b):
                    dve.wait_ge(c.start, 1)
                    dve.wait_ge(logits_done, b + 1)
                    nc.vector.tensor_copy(c.logits[:, b], o_ps[:, 0, 0:NT * E].rearrange("p (t e) -> p t e", t=NT)
                                          ).then_inc(logits_kept, 1)

                def early(b, n):
                    if n == 1:
                        rest_of_h(b)
                    elif n in (4, 6):
                        keep_values(b, (n - 4) // 2)
                    elif n in (9, 10):
                        rotate(b, n - 9)
                    elif n in (12, 13):
                        add_turned(b, n - 12)

                def iteration(b, after):
                    for n in range(H):
                        sigmoid_rests(b, n)
                        if n % 2 == 1 and n >= 3:
                            sum_parts(b, n // 2 - 1)
                        if after is not None:
                            early(after, n)
                    if after is not None:
                        rests(after, 0)
                    sum_parts(b, PAIRS - 1)
                    if after is None:
                        output_rest(b)
                        gate_rows(b)
                        update_x(b)
                        moments(b)
                        normalise(b)
                        keep_hT(b)
                        keep_logits(b)
                        return
                    output_rest(b)
                    rests(after, 1)
                    rotate(after, 2)
                    add_turned(after, 2)
                    gate_rows(b)
                    rests(after, 2)
                    rotate(after, 3)
                    add_turned(after, 3)
                    update_x(b)
                    rests(after, 3)
                    moments(b)
                    normalise(b)
                    keep_hT(b)
                    keep_logits(b)
                    dve.wait_ge(hT_kept, b + 1)

                rest_of_h(0)
                dve.wait_ge(tables_loaded, N_TABLES)
                dve.wait_ge(c.constants, 48)
                keep_values(0, 0)
                keep_values(0, 1)
                for t in range(NT):
                    rotate(0, t)
                    add_turned(0, t)
                    rests(0, t)
                with dve.Fori(0, B - 1) as b:
                    iteration(b, b + 1)
                iteration(B - 1, None)


def silu_experts_part(c, a, out):
    nc = c.nc
    NX = E + 1
    CHUNK = (2 * KC * F1 + IC * D) // B
    with ExitStack() as ctx:
        def sb(name, shape, dt=F32):
            return c.sb("e1_" + name, shape, dt, ctx)

        raw, w = sb("raw", [P, B, CHUNK]), sb("w", [P, 2, 2, B, CHUNK], F32R)
        h_parts, hidden = sb("h_parts", [P, 2, KC, S], F32R), sb("hidden", [P, 2, IC, S], F32R)
        gu_silu = sb("gu_silu", [P, 4 * S])
        silu = gu_silu[:, 0:2 * S].rearrange("p (u s) -> p u s", u=2)
        gu = gu_silu[:, 2 * S:].rearrange("p (u s) -> p u s", u=2)
        acc, coef = sb("acc", [P, B, NT, D]), sb("coef", [P, NX * B, NT])
        gate_ps = c.psum("e1_gate_ps", 2, ctx)
        up_ps = c.psum("e1_up_ps", 2, ctx)
        down_ps = c.psum("e1_down_ps", NT, ctx)
        (raw_loaded, w_head_done, w_split, h_head_done, h_split, gate_done, up_done, silu_done, gu_done, hidden_head_done,
         hidden_split, down_done, acc_done, y_done, x_done, stored) = (
            c.sem("e1_" + n) for n in
            ("raw_loaded w_head_done w_split h_head_done h_split gate_done up_done silu_done gu_done hidden_head_done "
             "hidden_split down_done acc_done y_done x_done stored").split())

        N = B * NT
        weight_sum, inv_sum = sb("weight_sum", [P, N]), sb("inv_sum", [P, N])
        probs, count, chosen = (sb(n, [P, N, E]) for n in ("probs", "count", "chosen"))
        bias = sb("bias", [P, E])
        better = gu_silu[:].rearrange("p (n e f) -> p n e f", e=E, f=E)
        bias_loaded, zeroed, biased_done, probs_done = (c.sem("e1_" + n) for n in
                                                        ("bias_loaded", "zeroed", "biased_done", "probs_done"))

        def weights(buf, part):
            return w[:, buf, part].rearrange("p b c -> p (b c)")

        def gate_up(buf, part, k, which, i):
            at = (2 * k + which) * F1 + i * P
            return weights(buf, part)[:, at:at + P]

        def down_rows(buf, part, i):
            at = 2 * KC * F1 + i * D
            return weights(buf, part)[:, at:at + D]

        with nc.Block() as block:
            @block.sync
            def _(sp):
                sp.dma_start(bias[:], a["L1_ffn_routing_bias"].unsqueeze(0).broadcast_to([P, E])).then_inc(bias_loaded, 16)
                sp.dma_start(raw[:], a["experts"][0]).then_inc(raw_loaded, 16)
                sp.dma_start(c.gate[:], c.gates_dram[1, 1].unsqueeze(0).broadcast_to([P, B, D])).then_inc(c.constants, 16)
                with sp.Fori(1, NX) as x:
                    sp.wait_ge(w_split, B * x)
                    sp.dma_start(raw[:], a["experts"][x]).then_inc(raw_loaded, 16)
                view = out.rearrange("b (t p) d -> b p t d", p=P)
                with sp.Fori(0, B) as b:
                    sp.wait_ge(x_done, b + 1)
                    sp.dma_start(view[b], c.x[:, b]).then_inc(stored, 16)
                sp.wait_ge(stored, 16 * B)

            @block.gpsimd
            def _(pool):
                pool.memset(gu_silu[:], 0.0).then_inc(zeroed, 1)
                pool.memset(acc[:], 0.0).then_inc(zeroed, 1)

            @block.tensor
            def _(pe):
                def step(n, buf, chunks):
                    pe.wait_ge(w_split, chunks)
                    pe.wait_ge(h_split, n + 1)
                    for i in range(IC):
                        if i >= 2:
                            pe.wait_ge(gu_done, IC * n + i - 1)
                        for which, ps, done in ((0, gate_ps, gate_done), (1, up_ps, up_done)):
                            product(nc.tensor, ps[:, i % 2, :],
                                    [(lambda p, k=k: gate_up(buf, p, k, which, i),
                                      lambda p, k=k: h_parts[:, p, k, :]) for k in range(KC)]).then_inc(done, 1)
                    pe.wait_ge(acc_done, n + 1)
                    for i in range(IC):
                        pe.wait_ge(hidden_split, IC * n + i + 1)
                        for t in range(NT):
                            for m, (p, r) in enumerate(PASSES):
                                last = nc.tensor.matmul(down_ps[:, t, 0:D], hidden[:, p, i, t * P:(t + 1) * P],
                                                        down_rows(buf, r, i), start=i == 0 and m == 0,
                                                        stop=i == IC - 1 and m == 2)
                    last.then_inc(down_done, 1)

                with pe.Fori(0, E // 2) as q:
                    for buf in range(2):
                        with pe.Fori(0, B) as b:
                            step(q * (2 * B) + buf * B + b, buf, q * (2 * B) + (buf + 1) * B)
                with pe.Fori(0, B) as b:
                    step(b + E * B, E % 2, NX * B)

            @block.scalar
            def _(act):
                def split_weight_heads(b, buf):
                    nc.scalar.activation(w[:, buf, HEAD, b], raw[:, b], ACT.Copy).then_inc(w_head_done, 1)

                def head_of_h(b):
                    nc.scalar.activation(h_parts[:, HEAD], c.hT[:, :, b, :], ACT.Copy).then_inc(h_head_done, 1)

                def step(n, b, buf, after, more_weights):
                    def silu_of(i):
                        act.wait_ge(gate_done, IC * n + i + 1)
                        nc.scalar.activation(silu[:, i % 2, :], gate_ps[:, i % 2, :], ACT.Silu).then_inc(silu_done, 1)

                    silu_of(0)
                    act.wait_ge(acc_done, n + 1)
                    for i in range(IC):
                        if i + 1 < IC:
                            silu_of(i + 1)
                        act.wait_ge(gu_done, IC * n + i + 1)
                        nc.scalar.activation(hidden[:, HEAD, i, :], gu[:, i % 2, :], ACT.Copy).then_inc(hidden_head_done, 1)
                    if after is not None:
                        act.wait_ge(up_done, IC * (n + 1))
                        head_of_h(after)
                    if more_weights:
                        split_weight_heads(b, 1 - buf)

                act.wait_ge(biased_done, 1)
                nc.scalar.activation(probs[:], c.logits[:].rearrange("p b t e -> p (b t) e"), ACT.Sigmoid
                                     ).then_inc(probs_done, 1)
                act.wait_ge(raw_loaded, 16)
                for b in range(B):
                    split_weight_heads(b, 0)
                head_of_h(0)
                with act.Fori(0, E // 2) as q:
                    for buf in range(2):
                        act.wait_ge(raw_loaded, q * 32 + 16 * (buf + 2))
                        with act.Fori(0, B - 1) as b:
                            step(q * (2 * B) + buf * B + b, b, buf, b + 1, True)
                        step(q * (2 * B) + (buf + 1) * B - 1, B - 1, buf, 0, True)
                with act.Fori(0, B - 1) as b:
                    step(b + E * B, b, 0, b + 1, False)
                step(NX * B - 1, B - 1, 0, None, False)

            @block.vector
            def _(dve):
                def split_weight_rests(m, b, buf):
                    dve.wait_ge(w_head_done, m + 1)
                    nc.vector.tensor_tensor(w[:, buf, REST, b], raw[:, b], w[:, buf, HEAD, b].bitcast(F32),
                                            ALU.subtract).then_inc(w_split, 1)

                def rest_of_h(n, b):
                    dve.wait_ge(h_head_done, n + 1)
                    nc.vector.tensor_tensor(h_parts[:, REST], c.hT[:, :, b, :], h_parts[:, HEAD].bitcast(F32),
                                            ALU.subtract).then_inc(h_split, 1)

                def step(n, b, buf, after, more_weights):
                    def times_up(i):
                        if i < 2:
                            dve.wait_ge(acc_done, n + 1)
                        else:
                            dve.wait_ge(hidden_split, IC * n + i - 1)
                        dve.wait_ge(silu_done, IC * n + i + 1)
                        dve.wait_ge(up_done, IC * n + i + 1)
                        nc.vector.tensor_tensor(gu[:, i % 2, :], silu[:, i % 2, :], up_ps[:, i % 2, :],
                                                ALU.mult).then_inc(gu_done, 1)

                    times_up(0)
                    for i in range(IC):
                        if i + 1 < IC:
                            times_up(i + 1)
                        dve.wait_ge(hidden_head_done, IC * n + i + 1)
                        nc.vector.tensor_tensor(hidden[:, REST, i, :], gu[:, i % 2, :],
                                                hidden[:, HEAD, i, :].bitcast(F32), ALU.subtract).then_inc(hidden_split, 1)
                    if after is not None:
                        rest_of_h(n + 1, after)
                    if more_weights:
                        split_weight_rests(n + B, b, 1 - buf)
                    dve.wait_ge(down_done, n + 1)
                    for t in range(NT):
                        last = nc.vector.scalar_tensor_tensor(out=acc[:, b, t, :], in0=down_ps[:, t, 0:D],
                                                              scalar=coef[:, n, t:t + 1], in1=acc[:, b, t, :],
                                                              op0=ALU.mult, op1=ALU.add)
                    last.then_inc(acc_done, 1)

                def finish(b):
                    dve.wait_ge(acc_done, b + E * B + 2)
                    nc.vector.tensor_tensor(acc[:, b], acc[:, b], c.gate[:, b, :].unsqueeze(1).broadcast_to([P, NT, D]),
                                            ALU.mult).then_inc(y_done, 1)
                    dve.wait_ge(y_done, b + 1)
                    nc.vector.tensor_tensor(c.x[:, b], c.x[:, b], acc[:, b], ALU.add).then_inc(x_done, 1)

                logits = c.logits[:].rearrange("p b t e -> p (b t) e")
                chosen_coef = c.coef[:].rearrange("p b t e -> p (b t) e")
                dve.wait_ge(bias_loaded, 16)
                nc.vector.tensor_tensor(logits, logits, bias[:].unsqueeze(1).broadcast_to([P, N, E]),
                                        ALU.add).then_inc(biased_done, 1)
                dve.wait_ge(zeroed, 1)
                dve.wait_ge(probs_done, 1)
                choose(nc, dve, probs[:], better, count[:], chosen[:], weight_sum[:], chosen_coef)
                nc.vector.reciprocal(inv_sum[:], weight_sum[:])
                dve.drain()
                nc.vector.memset(coef[:, 0:B, :], 1.0)
                nc.vector.tensor_tensor(coef[:, B:, :].rearrange("p (e b) t -> p (b t) e", e=E), chosen[:],
                                        inv_sum[:].unsqueeze(2).broadcast_to([P, N, E]), ALU.mult)
                dve.drain()
                dve.wait_ge(zeroed, 2)
                dve.sem_inc(acc_done, 1)
                for b in range(B):
                    split_weight_rests(b, b, 0)
                rest_of_h(0, 0)
                dve.wait_ge(c.constants, 64)
                with dve.Fori(0, E // 2) as q:
                    for buf in range(2):
                        with dve.Fori(0, B - 1) as b:
                            step(q * (2 * B) + buf * B + b, b, buf, b + 1, True)
                        step(q * (2 * B) + (buf + 1) * B - 1, B - 1, buf, 0, True)
                with dve.Fori(0, B - 1) as b:
                    step(b + E * B, b, 0, b + 1, False)
                    finish(b)
                step(NX * B - 1, B - 1, 0, None, False)
                finish(B - 1)


def program(nc, a, out):
    with ExitStack() as ctx:
        c = Core(nc, ctx)
        with ExitStack() as weights:
            w_ret = c.sb("w_ret", [P, 2, KC, D], F32R, weights)
            w_in = c.sb("w_in", [P, 2, KC, F0], F32R, weights)
            w_out = c.sb("w_out", [P, 2, MC, D], F32R, weights)
            tables = RetentionTables(c, weights)
            modulation_and_weights(c, a, tables, w_ret, w_in, w_out)
            c.begin_part()
            retention_part(c, tables, w_ret, w_in, w_out)
            c.end_part()
        with ExitStack() as weights:
            w_qk = c.sb("w_qk", [P, 2, KC, 2 * D], F32R, weights)
            w_v = c.sb("w_v", [P, 2, KC, D], F32R, weights)
            w_o = c.sb("w_o", [P, 2, KC, D], F32R, weights)
            with ExitStack() as experts:
                w_up = c.sb("e0_w_up", [P, 2, E * KC, P], F32R, experts)
                w_down = c.sb("e0_w_down", [P, 2, E, D], F32R, experts)
                softmax_router(c, a, w_up, w_down)
                chunks = "(k p) n -> p k n"
                load_weights, split_weights = weight_splitter(
                    c, experts, "at_w", ((a["wqT"].rearrange(chunks, p=P), w_qk[:, :, :, 0:D], a["qn_scale"]),
                                         (a["wkT"].rearrange(chunks, p=P), w_qk[:, :, :, D:2 * D], a["kn_scale"]),
                                         (a["wvT"].rearrange(chunks, p=P), w_v, None),
                                         (a["woT"].rearrange(chunks, p=P), w_o, None)))
                gelu_experts_part(c, a, w_up, w_down, load_weights, split_weights)
            attention_part(c, a, w_qk, w_v, w_o)
        silu_experts_part(c, a, out)


def _columns(v):
    import numpy as np
    return np.ascontiguousarray(v.reshape(-1, P).T)


def layout(i):
    import numpy as np
    o = {"cT": np.ascontiguousarray(np.stack([i[f"L{l}_c"].T.reshape(KC, P, B).transpose(1, 0, 2) for l in range(2)], 1))}
    for name, of in (("b_ret", "L0_attn_b_ret"), ("ln1_scale", "L0_attn_ln1_scale"), ("ln1_bias", "L0_attn_ln1_bias"),
                     ("b_in", "L0_attn_b1"), ("e0_b_up", "L0_ffn_b1"), ("qn_scale", "L1_attn_qn_scale"),
                     ("kn_scale", "L1_attn_kn_scale")):
        o[name] = _columns(i[of])
    for name in ("L0_wmod", "L1_wmod", "L0_attn_x", "L0_attn_W_ret", "L0_attn_W1", "L0_attn_W2", "L0_attn_ln2_scale",
                 "L0_attn_ln2_bias", "L0_attn_b2", "L0_ffn_gate_w",
                 "L0_ffn_w1", "L0_ffn_w2", "L0_ffn_b2", "L1_attn_v_b", "L1_attn_o_b"):
        o[name] = np.ascontiguousarray(i[name])
    for name, of in (("wqT", "L1_attn_q_w"), ("wkT", "L1_attn_k_w"), ("wvT", "L1_attn_v_w"), ("woT", "L1_attn_o_w"),
                     ("router_w", "L1_ffn_router_w")):
        o[name] = np.ascontiguousarray(i[of].T)
    o["qk_bias"] = np.concatenate([i["L1_attn_q_b"], i["L1_attn_k_b"]])
    o["L1_ffn_routing_bias"] = np.ascontiguousarray(i["L1_ffn_routing_bias"])
    experts = []
    for gate, up, down in [tuple(i["L1_ffn_" + n] for n in ("sg_w", "su_w", "sd_w"))] + [
            tuple(i["L1_ffn_" + n][e] for n in ("wg", "wu", "wd")) for e in range(E)]:
        both = np.concatenate([gate.T, up.T], axis=1).reshape(KC, P, 2 * F1).transpose(1, 0, 2).reshape(P, -1)
        experts.append(np.concatenate([both, down.T.reshape(IC, P, D).transpose(1, 0, 2).reshape(P, -1)], axis=1))
    o["experts"] = np.ascontiguousarray(np.stack(experts).reshape(E + 1, P, B, -1))
    o["cos"], o["sin"] = rope_tables()
    return o


def rope_tables():
    import numpy as np
    inv_freq = np.float32(1.0) / np.float32(10000.0) ** (np.arange(0, HD, 2, dtype=np.float32) / np.float32(HD))
    freqs = np.arange(S, dtype=np.float32)[:, None] * inv_freq[None, :].astype(np.float32)
    emb = np.concatenate([freqs, freqs], axis=-1).astype(np.float64)
    sign = np.where(np.arange(HD) % 2 == 0, -1.0, 1.0)
    return tuple(np.ascontiguousarray(v.astype(np.float32).reshape(NT, P, HD).transpose(1, 0, 2))
                 for v in (np.cos(emb), np.sin(emb) * sign))


def kernel(**inputs):
    import numpy as np
    import concourse.bacc as bacc
    from concourse.bass_utils import run_bass_kernel_spmd

    nc = bacc.Bacc("TRN2", target_bir_lowering=False, num_devices=1)
    arrays = layout({k: np.asarray(v) for k, v in inputs.items()})
    a = {k: nc.dram_tensor("in_" + k, v.shape, mybir.dt.from_np(v.dtype), kind="ExternalInput").ap() for k, v in arrays.items()}
    out = nc.dram_tensor("out", (B, S, D), F32, kind="ExternalOutput").ap()
    program(nc, a, out)
    return run_bass_kernel_spmd(nc, [{"in_" + k: v for k, v in arrays.items()}], core_ids=[0]).results[0]["out"]
```
